# Optimizing a Trainium2 kernel written in Bass

```python
import numpy as np
import jax
import jax.numpy as jnp

def _softmax(x, axis=-1):
    return jax.nn.softmax(x, axis=axis)

def _gelu(x):
    return jax.nn.gelu(x, approximate=True)

def _silu(x):
    return jax.nn.silu(x)

def _sigmoid(x):
    return jax.nn.sigmoid(x)

def _layernorm(x, axis=-1, eps=1e-05):
    m = jnp.mean(x, axis=axis, keepdims=True)
    v = jnp.var(x, axis=axis, keepdims=True)
    return (x - m) / jnp.sqrt(v + eps)

def _scatter_add(tgt, idx, src, axis=0):
    return tgt.at[idx].add(src)

def _segment_sum(src, seg, n):
    return jax.ops.segment_sum(src, seg, n)
kernel_name = 'mk_flamingo_gated_d1_seqx_r2_1afa08'

def setup_inputs(seed: int=0):
    np.random.seed(seed)
    _w = jnp.asarray

    def _rec_inputs():
        import jax
        import jax.numpy as jnp
        _rk = jax.random.key(seed)
        x = -0.0002928 + 1 * jax.random.normal(jax.random.fold_in(_rk, 1), (4, 2048, 512), jnp.float32)
        _lenS = 2048 - jax.random.randint(jax.random.fold_in(_rk, 7), (4,), 0, max(1, 2048 // 4) + 1, jnp.int32)
        _lenS2 = 77 - jax.random.randint(jax.random.fold_in(_rk, 8), (4,), 0, max(1, 77 // 4) + 1, jnp.int32)
        _ctx_1024P = jax.random.normal(jax.random.fold_in(_rk, 11), (4, 16, 512), jnp.float32)
        _ctx_1024c = jax.random.dirichlet(jax.random.fold_in(_rk, 511), 0.3 * jnp.ones((16,), jnp.float32), (4, 77))
        _ctx_1024t = jnp.einsum('bsk,bkd->bsd', _ctx_1024c, _ctx_1024P)
        _ctx_1024t = _ctx_1024t * jax.lax.rsqrt(jnp.mean(jnp.square(_ctx_1024t)) + 1e-12) * 0.953939
        ctx_1024 = 4.13588e-05 + 0.999923 * (_ctx_1024t + 0.3 * jax.random.normal(jax.random.fold_in(_rk, 611), (4, 77, 512), jnp.float32))
        _g = jax.random.normal(jax.random.fold_in(_rk, 9001), (2, 1), jnp.float32)
        _g = jnp.sign(_g) * jnp.maximum(jnp.abs(_g), 1.0) + (_g == 0) * 1.0
        g_xattn = _g[0]
        g_ffn = _g[1]
        return (x, ctx_1024, g_xattn, g_ffn)
    x, ctx_1024, g_xattn, g_ffn = _rec_inputs()

    def _L0_xattn_setup():
        import jax, jax.numpy as jnp
        import numpy as np
        DIM = 512
        NUM_HEADS = 16
        DIM_HEAD = 64
        INNER = NUM_HEADS * DIM_HEAD
        SCALE = DIM_HEAD ** (-0.5)

        def _layernorm(x, gamma, beta, eps=1e-05):
            mu = jnp.mean(x, axis=-1, keepdims=True)
            var = jnp.mean(jnp.square(x - mu), axis=-1, keepdims=True)
            return (x - mu) * jax.lax.rsqrt(var + eps) * gamma + beta
        key = jax.random.key(seed)
        ks = jax.random.split(key, 8)
        B, SQ, SK = (2, 1024, 2048)
        x = jax.random.normal(ks[0], (B, SQ, DIM), dtype=jnp.float32)
        context = jax.random.normal(ks[1], (B, SK, DIM), dtype=jnp.float32)
        ln_gamma = jnp.ones((DIM,), jnp.float32)
        ln_beta = jnp.zeros((DIM,), jnp.float32)
        w_q = jax.random.normal(ks[2], (DIM, INNER), dtype=jnp.float32) / np.sqrt(DIM)
        w_kv = jax.random.normal(ks[3], (DIM, 2 * INNER), dtype=jnp.float32) / np.sqrt(DIM)
        w_out = jax.random.normal(ks[4], (INNER, DIM), dtype=jnp.float32) / np.sqrt(INNER)
        b_out = jnp.zeros((DIM,), jnp.float32)
        gate = jnp.array([0.5], jnp.float32)
        return {'x': x, 'context': context, 'ln_gamma': ln_gamma, 'ln_beta': ln_beta, 'w_q': w_q, 'w_kv': w_kv, 'w_out': w_out, 'b_out': b_out, 'gate': gate}
    _L0_xattn_all = _L0_xattn_setup()
    _L0_xattn_in = {k: v for k, v in _L0_xattn_all.items() if k in ('ln_gamma', 'ln_beta', 'w_q', 'w_kv', 'w_out', 'b_out', 'gate')}
    del _L0_xattn_all

    def _L0_ffn_setup():
        import jax, jax.numpy as jnp
        import numpy as np
        NUM_TRUE = 8
        NUM_NULL = 2
        NUM_EXPERTS = NUM_TRUE + NUM_NULL
        TOP_K = 2
        key = jax.random.key(seed)
        k0, k1, k2 = jax.random.split(key, 3)
        B, S, D = (4, 1024, 512)
        inputs = jax.random.normal(k0, (B, S, D), dtype=jnp.float32)
        gate_w = jax.random.normal(k1, (NUM_EXPERTS, D), dtype=jnp.float32) * 0.02
        gate_b = jnp.zeros((NUM_EXPERTS,), dtype=jnp.float32)
        expert_w = jax.random.normal(k2, (NUM_TRUE, D, D), dtype=jnp.float32) * 0.02
        expert_b = jnp.zeros((NUM_TRUE, D), dtype=jnp.float32)
        return {'inputs': inputs, 'gate_w': gate_w, 'gate_b': gate_b, 'expert_w': expert_w, 'expert_b': expert_b}
    _L0_ffn_all = _L0_ffn_setup()
    _L0_ffn_in = {k: v for k, v in _L0_ffn_all.items() if k in ('gate_w', 'gate_b', 'expert_w', 'expert_b')}
    del _L0_ffn_all
    return {'x': x, 'ctx_1024': ctx_1024, 'g_xattn': g_xattn, 'g_ffn': g_ffn, 'L0_xattn_ln_gamma': _L0_xattn_in['ln_gamma'], 'L0_xattn_ln_beta': _L0_xattn_in['ln_beta'], 'L0_xattn_w_q': _L0_xattn_in['w_q'], 'L0_xattn_w_kv': _L0_xattn_in['w_kv'], 'L0_xattn_w_out': _L0_xattn_in['w_out'], 'L0_xattn_b_out': _L0_xattn_in['b_out'], 'L0_xattn_gate': _L0_xattn_in['gate'], 'L0_ffn_gate_w': _L0_ffn_in['gate_w'], 'L0_ffn_gate_b': _L0_ffn_in['gate_b'], 'L0_ffn_expert_w': _L0_ffn_in['expert_w'], 'L0_ffn_expert_b': _L0_ffn_in['expert_b']}

def reference(x, ctx_1024, g_xattn, g_ffn, L0_xattn_ln_gamma, L0_xattn_ln_beta, L0_xattn_w_q, L0_xattn_w_kv, L0_xattn_w_out, L0_xattn_b_out, L0_xattn_gate, L0_ffn_gate_w, L0_ffn_gate_b, L0_ffn_expert_w, L0_ffn_expert_b):
    import jax
    import jax.numpy as jnp

    def _L0_xattn_ref(x, context, ln_gamma, ln_beta, w_q, w_kv, w_out, b_out, gate):
        import jax, jax.numpy as jnp
        import numpy as np
        DIM = 512
        NUM_HEADS = 16
        DIM_HEAD = 64
        INNER = NUM_HEADS * DIM_HEAD
        SCALE = DIM_HEAD ** (-0.5)

        def _layernorm(x, gamma, beta, eps=1e-05):
            mu = jnp.mean(x, axis=-1, keepdims=True)
            var = jnp.mean(jnp.square(x - mu), axis=-1, keepdims=True)
            return (x - mu) * jax.lax.rsqrt(var + eps) * gamma + beta
        B, SQ, _ = x.shape
        SK = context.shape[1]
        xn = _layernorm(x, ln_gamma, ln_beta)
        q = (xn @ w_q).reshape(B, SQ, NUM_HEADS, DIM_HEAD)
        kv = context @ w_kv
        k, v = jnp.split(kv, 2, axis=-1)
        k = k.reshape(B, SK, NUM_HEADS, DIM_HEAD)
        v = v.reshape(B, SK, NUM_HEADS, DIM_HEAD)
        scores = jnp.einsum('bqhd,bkhd->bhqk', q * SCALE, k)
        attn = jax.nn.softmax(scores, axis=-1)
        out = jnp.einsum('bhqk,bkhd->bqhd', attn, v).reshape(B, SQ, INNER)
        out = out @ w_out + b_out
        return out * jnp.tanh(gate[0])

    def _L0_ffn_ref(inputs, gate_w, gate_b, expert_w, expert_b):
        import jax, jax.numpy as jnp
        import numpy as np
        NUM_TRUE = 8
        NUM_NULL = 2
        NUM_EXPERTS = NUM_TRUE + NUM_NULL
        TOP_K = 2
        D = inputs.shape[-1]
        x = inputs.reshape(-1, D)
        gate_logits = x @ gate_w.T + gate_b
        gate_probs = jax.nn.softmax(gate_logits, axis=-1)
        weights, selected = jax.lax.top_k(gate_probs, TOP_K)
        true_mask = selected < NUM_TRUE
        true_weights = weights * true_mask
        denom = true_weights.sum(axis=-1, keepdims=True)
        denom = jnp.where(denom > 0, denom, jnp.ones_like(denom))
        norm_w = (true_weights / denom).astype(x.dtype)
        one_hot = jax.nn.one_hot(selected, NUM_EXPERTS, dtype=norm_w.dtype)
        combine_w = jnp.einsum('tk,tke->te', norm_w, one_hot)[:, :NUM_TRUE]
        expert_out = jnp.einsum('td,edh->teh', x, expert_w) + expert_b[None, :, :]
        out = jnp.einsum('te,teh->th', combine_w, expert_out)
        return out.reshape(inputs.shape[:-1] + (out.shape[-1],))
    x = x + jnp.tanh(g_xattn[0]) * _L0_xattn_ref(_layernorm(x, axis=-1), ctx_1024, L0_xattn_ln_gamma, L0_xattn_ln_beta, L0_xattn_w_q, L0_xattn_w_kv, L0_xattn_w_out, L0_xattn_b_out, L0_xattn_gate)
    x = x + jnp.tanh(g_ffn[0]) * _L0_ffn_ref(_layernorm(x, axis=-1), L0_ffn_gate_w, L0_ffn_gate_b, L0_ffn_expert_w, L0_ffn_expert_b)
    return x

_drawn_inputs = setup_inputs


def setup_inputs(seed=0):
    import zlib

    import numpy as np

    out = dict(_drawn_inputs(seed))
    spreads = {'L0_xattn_ln_gamma': (1.0, 0.2),
     'L0_xattn_ln_beta': (0.0, 0.1),
     'L0_xattn_b_out': (0.0, 0.1),
     'L0_ffn_gate_b': (0.0, 0.1),
     'L0_ffn_expert_b': (0.0, 0.1)}
    factors = {}
    for name, (base, spread) in spreads.items():
        noise = np.random.default_rng([zlib.crc32(name.encode()), seed]).standard_normal(out[name].shape)
        drawn = base * np.exp(spread * noise) if base else spread * noise
        out[name] = jnp.asarray(drawn.astype(out[name].dtype))
    for name, factor in factors.items():
        out[name] = (out[name] * factor).astype(out[name].dtype)
    return out
```

```python
from contextlib import ExitStack

import concourse.bass as bass
from concourse import mybir
from concourse.alu_op_type import AluOpType as ALU

F32 = mybir.dt.float32
F16 = mybir.dt.float16
I32 = mybir.dt.int32
U32 = mybir.dt.uint32
ACT = mybir.ActivationFunctionType
AX_X = mybir.AxisListType.X

P = 128
D = 512
DT = D // P
HEADS = 16
DH = 64
INNER = HEADS * DH
PAIRS = INNER // P
BATCH = 4
SEQ = 2048
KEYS = 77
TOKENS = BATCH * SEQ
TILES = TOKENS // P
TPB = SEQ // P
COLS = HEADS * KEYS
KT = -(-COLS // P)
LAST = COLS - (KT - 1) * P
BANK_HEADS = (6, 5, 5)
HEAD0 = (0, 6, 11)
PT_GROUPS = ((0, 4), (4, 8), (8, 10))
EPS = 1e-5
EXPERTS = 8
GATES = EXPERTS + 2
TOP_K = 2
REGIONS = EXPERTS + 1
SLOT_TILES = TILES + EXPERTS
REGION_ROWS = SLOT_TILES * P
TABLE_ROWS = TOP_K * REGIONS * REGION_ROWS
NO_ROW = float(1 << 20)
NO_TOKEN = float(TOKENS)

M_SCALE = 64.0
U_SCALE = 64.0
P_SCALE = 4096.0
G_SCALE = 64.0
W_SCALE = 64.0
PRODUCTS = ((0, 0), (0, 1), (1, 0))


def fold_context(nc, ident, x_in, wq, wkv, wout, b_out, gate, g_xattn, ctx, m_dram, u_dram, expert_w,
                 w_parts, table):
    JOBS_T, JOBS_Q, JOBS_KV = DT, PAIRS, 2 * PAIRS
    NB = 8
    UR = 3
    FILL = 54
    PASSES = TABLE_ROWS // P // FILL
    with ExitStack() as stack:
        def sb(name, shape, dt=F32):
            return stack.enter_context(nc.sbuf_tensor(name, shape, dt))

        def sem(name):
            return stack.enter_context(nc.semaphore(name))

        ctx_sb = sb("ctx_sb", [KEYS, BATCH, D])
        ctxT = sb("ctxT", [P, DT, BATCH * KEYS])
        wq_sb = sb("wq_sb", [P, DT, INNER])
        wqT = sb("wqT", [P, PAIRS, D])
        wkv_sb = sb("wkv_sb", [P, DT, 2 * INNER])
        kvT = sb("kvT", [P, 2 * PAIRS, BATCH * KEYS])
        wout_sb = sb("wout_sb", [P, PAIRS, D])
        m_stage = sb("m_stage", [P, 2, BATCH, 2, 4 * KEYS], F16)
        u_val = sb("u_val", [KEYS, UR, D])
        u_stage = sb("u_stage", [KEYS, UR, 2, D], F16)
        fill = sb("fill", [P, FILL, 4])
        w_raw = wkv_sb[:].rearrange("p t n -> p (t n)").rearrange("p (e t n) -> p e t n", e=4, t=DT)
        bias = sb("bias", [KEYS, D])
        gates = sb("gates", [P, 2])
        tanhs = sb("tanhs", [P, 2])
        u_gain = sb("u_gain", [P, 1])
        banks = [stack.enter_context(nc.psum_tensor(f"fold{i}", [P, 512], F32)) for i in range(NB)]

        ctx_in = sem("ctx_in")
        wq_in = sem("wq_in")
        wkv_in = sem("wkv_in")
        wout_in = sem("wout_in")
        small_in = sem("small_in")
        tanh_ready = sem("tanh_ready")
        gain_ready = sem("gain_ready")
        bias_ready = sem("bias_ready")
        product_ready = sem("product_ready")
        act_read = sem("act_read")
        dve_read = sem("dve_read")
        u_summed = sem("u_summed")
        u_hi_ready = sem("u_hi_ready")
        u_lo_ready = sem("u_lo_ready")
        m_stored = [sem(f"m_stored{i}") for i in range(2)]
        u_stored = [sem(f"u_stored{i}") for i in range(UR)]
        w_in = [sem(f"w_in{i}") for i in range(4)]
        w_scaled = sem("w_scaled")
        w_hi_ready = sem("w_hi_ready")
        w_lo_ready = sem("w_lo_ready")
        fill_zero = sem("fill_zero")
        fill_ready = sem("fill_ready")
        table_clear = sem("table_clear")

        M0 = JOBS_T + JOBS_Q + JOBS_KV
        NM = DT * HEADS
        U0 = M0 + NM
        NU = BATCH * HEADS

        def m_job(n):
            dt, h = divmod(n, HEADS)
            return dt, h

        def u_job(n):
            return divmod(n, HEADS)

        block = stack.enter_context(nc.Block())

        @block.sync
        def _(sp):
            def load_expert(e):
                sp.dma_start(w_raw[:, e % 4], expert_w[e].rearrange("(t p) n -> p t n", p=P)).then_inc(w_in[e % 4], 16)

            sp.dma_start(ctx_sb[:], ctx.rearrange("b j d -> j b d")).then_inc(ctx_in, 16)
            sp.dma_start(wq_sb[:], wq.rearrange("(t p) n -> p t n", p=P)).then_inc(wq_in, 16)
            sp.dma_start(gates[:, 0:1], gate.rearrange("(a b) -> a b", a=1).broadcast_to([P, 1])).then_inc(small_in, 16)
            sp.dma_start(gates[:, 1:2], g_xattn.rearrange("(a b) -> a b", a=1).broadcast_to([P, 1])).then_inc(small_in, 16)
            sp.dma_start(bias[:], b_out.rearrange("(a d) -> a d", a=1).broadcast_to([KEYS, D])).then_inc(small_in, 16)
            sp.dma_start(wkv_sb[:], wkv.rearrange("(t p) n -> p t n", p=P)).then_inc(wkv_in, 16)
            sp.dma_start(wout_sb[:], wout.rearrange("(t p) n -> p t n", p=P)).then_inc(wout_in, 16)
            sp.wait_ge(fill_ready, 1)
            sp.dma_start(table.rearrange("(p c r) w -> p c (r w)", p=P, c=PASSES),
                         fill[:].rearrange("p r w -> p (r w)").unsqueeze(1).broadcast_to([P, PASSES, FILL * 4]),
                         ).then_inc(table_clear, 16)
            sp.wait_ge(product_ready, M0)
            for e in range(4):
                load_expert(e)
            for g in range(DT * 4):
                dt, quad = divmod(g, 4)
                sp.wait_ge(act_read, M0 + 4 * g + 4)
                sp.wait_ge(dve_read, 4 * g + 4)
                for b in range(BATCH):
                    sp.dma_start(m_dram[b, :, dt, :, quad * 4 * KEYS:(quad + 1) * 4 * KEYS],
                                 m_stage[:, g % 2, b]).then_inc(m_stored[g % 2], 16)
                if g % 4 == 3:
                    sp.wait_ge(w_lo_ready, g // 4 + 1)
                    load_expert(g // 4 + 4)
            for n in range(NU):
                b, h = u_job(n)
                sp.wait_ge(u_lo_ready, n + 1)
                sp.wait_ge(u_hi_ready, n + 1)
                sp.dma_start(u_dram[b, h * KEYS:(h + 1) * KEYS], u_stage[:, n % UR]).then_inc(u_stored[n % UR], 16)
            for s in range(2):
                sp.wait_ge(m_stored[s], 16 * BATCH * DT * 4 // 2)
            for s in range(UR):
                sp.wait_ge(u_stored[s], 16 * len(range(s, NU, UR)))
            sp.wait_ge(table_clear, 16)

        @block.tensor
        def _(pe):
            def bank(n):
                if n >= NB:
                    pe.wait_ge(act_read, n - NB + 1)
                if M0 <= n - NB < U0:
                    pe.wait_ge(dve_read, n - NB - M0 + 1)
                return banks[n % NB]

            pe.wait_ge(ctx_in, 16)
            for t in range(DT):
                out = bank(t)
                for b in range(BATCH):
                    last = pe.transpose(out[:, b * KEYS:(b + 1) * KEYS], ctx_sb[:, b, t * P:(t + 1) * P],
                                        ident[0:KEYS, 0:KEYS])
                last.then_inc(product_ready, 1)
            pe.wait_ge(wq_in, 16)
            for m in range(PAIRS):
                out = bank(DT + m)
                for t in range(DT):
                    last = pe.transpose(out[:, t * P:(t + 1) * P], wq_sb[:, t, m * P:(m + 1) * P], ident[:])
                last.then_inc(product_ready, 1)
            pe.wait_ge(wkv_in, 16)
            pe.wait_ge(act_read, DT)
            for m in range(2 * PAIRS):
                out = bank(DT + PAIRS + m)
                for t in range(DT):
                    last = pe.matmul(out[:, 0:BATCH * KEYS], wkv_sb[:, t, m * P:(m + 1) * P], ctxT[:, t, :],
                                     start=(t == 0), stop=(t == DT - 1))
                last.then_inc(product_ready, 1)
            for n in range(NM):
                dt, h = m_job(n)
                half = slice(DH * (h % 2), DH * (h % 2) + DH)
                out = bank(M0 + n)
                if n == 0:
                    pe.wait_ge(act_read, M0)
                pe.matmul(out[:, 0:BATCH * KEYS], wqT[half, h // 2, dt * P:(dt + 1) * P], kvT[half, h // 2, :],
                          start=True, stop=True).then_inc(product_ready, 1)
            pe.wait_ge(wout_in, 16)
            for n in range(NU):
                b, h = u_job(n)
                half = slice(DH * (h % 2), DH * (h % 2) + DH)
                out = bank(U0 + n)
                pe.matmul(out[0:KEYS, :], kvT[half, PAIRS + h // 2, b * KEYS:(b + 1) * KEYS], wout_sb[half, h // 2, :],
                          start=True, stop=True).then_inc(product_ready, 1)

        @block.scalar
        def _(act):
            act.wait_ge(small_in, 48)
            act.activation(tanhs[:], gates[:], ACT.Tanh).then_inc(tanh_ready, 1)
            for n in range(M0):
                act.wait_ge(product_ready, n + 1)
                if n < DT:
                    act.copy(ctxT[:, n, :], banks[n % NB][:, 0:BATCH * KEYS]).then_inc(act_read, 1)
                elif n < DT + PAIRS:
                    act.copy(wqT[:, n - DT, :], banks[n % NB][:]).then_inc(act_read, 1)
                else:
                    act.copy(kvT[:, n - DT - PAIRS, :], banks[n % NB][:, 0:BATCH * KEYS]).then_inc(act_read, 1)
            for n in range(NM):
                g, hh = divmod(n, 4)
                if hh == 0 and g >= 2:
                    act.wait_ge(m_stored[g % 2], 16 * BATCH * (g // 2))
                act.wait_ge(product_ready, M0 + n + 1)
                act.mul(m_stage[:, g % 2, :, 0, hh * KEYS:(hh + 1) * KEYS],
                        banks[(M0 + n) % NB][:, 0:BATCH * KEYS].rearrange("p (b j) -> p b j", b=BATCH),
                        M_SCALE * DH ** -0.5).then_inc(act_read, 1)
            act.wait_ge(gain_ready, 1)
            for n in range(NU):
                if n >= UR:
                    act.wait_ge(u_lo_ready, n - UR + 1)
                act.wait_ge(product_ready, U0 + n + 1)
                act.activation(u_val[:, n % UR, :], banks[(U0 + n) % NB][0:KEYS, :], ACT.Copy,
                               scale=u_gain[0:KEYS, :]).then_inc(act_read, 1)

        @block.vector
        def _(dve):
            dve.wait_ge(tanh_ready, 1)
            dve.scalar_tensor_tensor(u_gain[:], tanhs[:, 0:1], U_SCALE, tanhs[:, 1:2], ALU.mult,
                                     ALU.mult).then_inc(gain_ready, 1)
            dve.wait_ge(gain_ready, 1)
            dve.tensor_scalar(bias[:], bias[:], u_gain[0:KEYS, :], None, ALU.mult).then_inc(bias_ready, 1)
            for n in range(NM):
                g, hh = divmod(n, 4)
                dve.wait_ge(act_read, M0 + n + 1)
                if hh == 0 and g >= 2:
                    dve.wait_ge(m_stored[g % 2], 16 * BATCH * (g // 2))
                cols = slice(hh * KEYS, (hh + 1) * KEYS)
                dve.scalar_tensor_tensor(m_stage[:, g % 2, :, 1, cols],
                                         banks[(M0 + n) % NB][:, 0:BATCH * KEYS].rearrange("p (b j) -> p b j", b=BATCH),
                                         M_SCALE * DH ** -0.5, m_stage[:, g % 2, :, 0, cols], ALU.mult,
                                         ALU.subtract).then_inc(dve_read, 1)
            for n in range(NU):
                b, h = u_job(n)
                dve.wait_ge(act_read, U0 + n + 1)
                if n >= UR:
                    dve.wait_ge(u_stored[n % UR], 16 * (n // UR))
                if h == 0:
                    dve.wait_ge(bias_ready, 1)
                    dve.tensor_tensor(u_val[:, n % UR, :], u_val[:, n % UR, :], bias[:], ALU.add).then_inc(u_summed, 1)
                    dve.wait_ge(u_summed, b + 1)
                dve.tensor_copy(u_stage[:, n % UR, 0, :], u_val[:, n % UR, :]).then_inc(u_hi_ready, 1)
                dve.wait_ge(u_hi_ready, n + 1)
                dve.tensor_tensor(u_stage[:, n % UR, 1, :], u_val[:, n % UR, :], u_stage[:, n % UR, 0, :],
                                  ALU.subtract).then_inc(u_lo_ready, 1)

        @block.gpsimd
        def _(pool):
            pool.memset(fill[:], 0.0).then_inc(fill_zero, 1)
            pool.wait_ge(fill_zero, 1)
            pool.memset(fill[:, :, 0:1], NO_TOKEN).then_inc(fill_ready, 1)
            for e in range(EXPERTS):
                pool.wait_ge(w_in[e % 4], 16 * (e // 4 + 1))
                pool.tensor_scalar(w_raw[:, e % 4], w_raw[:, e % 4], W_SCALE, None, ALU.mult).then_inc(w_scaled, 1)
                pool.wait_ge(w_scaled, e + 1)
                pool.tensor_copy(w_parts[:, e, :, 0, :], w_raw[:, e % 4]).then_inc(w_hi_ready, 1)
                pool.wait_ge(w_hi_ready, e + 1)
                pool.tensor_tensor(w_parts[:, e, :, 1, :], w_raw[:, e % 4], w_parts[:, e, :, 0, :],
                                   ALU.subtract).then_inc(w_lo_ready, 1)


def attend(nc, ident16, x_in, ln_gamma, ln_beta, m_dram, u_dram, x_mid, x_final, gate_w, gate_b, g_ffn,
           table, placed, ones16):
    with ExitStack() as stack:
        def sb(name, shape, dt=F32):
            return stack.enter_context(nc.sbuf_tensor(name, shape, dt))

        def psum(name, shape, dt=F32):
            return stack.enter_context(nc.psum_tensor(name, shape, dt))

        def sem(name):
            return stack.enter_context(nc.semaphore(name))

        m_sb = sb("m_sb", [P, DT, 2, COLS], F16)
        u_sb = sb("u_sb", [P, KT, 2, D], F16)
        gamma = sb("gamma", [P, D])
        beta = sb("beta", [P, D])
        x_ln = sb("x_ln", [P, 2, D])
        x_res = sb("x_res", [P, 2, D])
        stats = sb("stats", [P, 2, 6])
        moments = sb("moments", [P, 2, 2])
        spread = sb("spread", [P, 2, 1])
        rstd = sb("rstd", [P, 2, 1])
        minus_half = sb("minus_half", [P, 1])
        z = sb("z", [P, 2, D])
        z_parts = sb("z_parts", [P, 2, 2, D], F16)
        zT = sb("zT", [P, 2, 2, DT, P], F16)
        top = sb("top", [P, 2, HEADS])
        expd = sb("expd", [P, 2, COLS])
        total = sb("total", [P, 2, HEADS])
        inverse = sb("inverse", [P, 2, HEADS])
        p_parts = sb("p_parts", [P, 2, COLS], F16)
        pT = sb("pT", [P, KT, 2, P], F16)
        x_out = sb("x_out", [P, 2, D])
        x_stats = sb("x_stats", [P, 2, 6])
        x_moments = sb("x_moments", [P, 2, 2])
        x_spread = sb("x_spread", [P, 2, 1])
        x_rstd = sb("x_rstd", [P, 2, 1])
        y = sb("y", [P, 2, D])
        y_parts = sb("y_parts", [P, 2, 2, D], F16)
        yT = sb("yT", [P, 2, DT, P], F16)
        gate_raw = sb("gate_raw", [P, DT, GATES])
        gate_scaled = sb("gate_scaled", [P, DT, GATES])
        gate_parts = sb("gate_parts", [P, DT, 2, GATES], F16)
        gate_bias = sb("gate_bias", [P, GATES])
        logits = sb("logits", [P, 2, GATES])
        largest = sb("largest", [P, 2, 8])
        found = sb("found", [P, 2, 8], U32)
        expert = sb("expert", [P, 2, TOP_K])
        gap = sb("gap", [P, 2, TOP_K])
        ratio = sb("ratio", [P, 2, TOP_K])
        norms = sb("norms", [P, 2, 2])
        onehot = sb("onehot", [P, 2, TOP_K, EXPERTS], F16)
        iota_e = sb("iota_e", [P, TOP_K, EXPERTS])
        region = sb("region", [P, TOP_K, EXPERTS])
        iota_t = sb("iota_t", [P, TILES])
        below = sb("below", [P, P], F16)
        g_raw = sb("g_raw", [P, 1])
        g_tanh = sb("g_tanh", [P, 1])
        place = sb("place", [P, TOP_K, EXPERTS])
        mine = sb("mine", [P, TOP_K, EXPERTS])
        row = sb("row", [P, TOP_K])
        no_row = sb("no_row", [P, TOP_K])
        row_f = sb("row_f", [P, TOP_K])
        row_i = sb("row_i", [P, 2, TOP_K], I32)
        kept = sb("kept", [P, TOP_K])
        kept_sum = sb("kept_sum", [P, 1])
        kept_div = sb("kept_div", [P, 1])
        kept_inv = sb("kept_inv", [P, 1])
        payload = sb("payload", [P, 2, TOP_K, 4])

        scores = [psum(f"scores{k}", [P, 512]) for k in range(3)]
        pT_bank = [psum(f"pT_bank{k}", [P, 4, 2, P], F16) for k in range(3)]
        gate_bank = pT_bank[2][:, 2:4].rearrange("p a b c -> p (a b c)").bitcast(F32)[:, 0:GATES]
        rank_bank = pT_bank[2][:, 2:4].rearrange("p a b c -> p (a b c)").bitcast(F32)[:, 16:16 + TOP_K * EXPERTS]
        zT_bank = psum("zT_bank", [P, 2, DT, P], F16)
        mix = psum("mix", [P, D])

        affine_in = sem("affine_in")
        m_in = sem("m_in")
        u_in = sem("u_in")
        x_ln_in = [sem(f"x_ln_in{s}") for s in range(2)]
        x_res_in = [sem(f"x_res_in{s}") for s in range(2)]
        stored = [sem(f"stored{s}") for s in range(2)]
        const_ready = sem("const_ready")
        stats_ready = sem("stats_ready")
        moments_ready = sem("moments_ready")
        spread_ready = sem("spread_ready")
        rstd_ready = sem("rstd_ready")
        z_ready = sem("z_ready")
        scaled_ready = sem("scaled_ready")
        shifted_ready = sem("shifted_ready")
        z_hi_ready = sem("z_hi_ready")
        z_lo_ready = sem("z_lo_ready")
        zT_summed = sem("zT_summed")
        zT_ready = sem("zT_ready")
        scores_ready = sem("scores_ready")
        top_ready = sem("top_ready")
        less_ready = sem("less_ready")
        exp_ready = sem("exp_ready")
        pT_summed = sem("pT_summed")
        pT_ready = sem("pT_ready")
        total_ready = sem("total_ready")
        inverse_ready = sem("inverse_ready")
        p_ready = sem("p_ready")
        p_hi_ready = sem("p_hi_ready")
        p_lo_ready = sem("p_lo_ready")
        mix_ready = sem("mix_ready")
        x_out_ready = sem("x_out_ready")

        gate_in = sem("gate_in")
        gate_scaled_ready = sem("gate_scaled_ready")
        gate_hi_ready = sem("gate_hi_ready")
        gate_lo_ready = sem("gate_lo_ready")
        x_stats_ready = sem("x_stats_ready")
        x_moments_ready = sem("x_moments_ready")
        x_spread_ready = sem("x_spread_ready")
        x_rstd_ready = sem("x_rstd_ready")
        y_ready = sem("y_ready")
        y_hi_ready = sem("y_hi_ready")
        y_lo_ready = sem("y_lo_ready")
        yT_summed = sem("yT_summed")
        yT_ready = sem("yT_ready")
        gate_summed = sem("gate_summed")
        logits_ready = sem("logits_ready")
        largest_ready = sem("largest_ready")
        choice_ready = sem("choice_ready")
        expert_ready = sem("expert_ready")
        gap_ready = sem("gap_ready")
        ratio_ready = sem("ratio_ready")
        norms_ready = sem("norms_ready")
        onehot_ready = sem("onehot_ready")
        g_in = sem("g_in")
        g_ready = sem("g_ready")
        iota_ready = sem("iota_ready")
        rank_summed = sem("rank_summed")
        place_ready = sem("place_ready")
        mine_ready = sem("mine_ready")
        row_ready = sem("row_ready")
        no_row_ready = sem("no_row_ready")
        row_f_ready = sem("row_f_ready")
        row_i_ready = sem("row_i_ready")
        kept_ready = sem("kept_ready")
        kept_sum_ready = sem("kept_sum_ready")
        kept_div_ready = sem("kept_div_ready")
        kept_inv_ready = sem("kept_inv_ready")
        weight_ready = sem("weight_ready")
        payload_ready = sem("payload_ready")
        placed_ready = sem("placed_ready")
        scattered = [sem(f"scattered{s}") for s in range(2)]

        def live(i):
            return not isinstance(i, int) or 0 <= i < TILES

        def later(i, n):
            return not isinstance(i, int) or i >= n

        def run(engine, step):
            first, last = 6, TILES - 2
            for i in range(first):
                step(i, i % 2)
            with engine.Fori(0, (last - first) // 2) as r:
                for k in range(2):
                    step(2 * r + first + k, k)
            for i in range(last, TILES + 7):
                step(i, i % 2)

        def rows(tensor, i):
            return tensor[bass.ds(i * P, P), :]

        block = stack.enter_context(nc.Block())

        @block.sync
        def _(sp):
            def load_x_ln(i, s):
                sp.dma_start(x_ln[:, s, :], rows(x_in, i)).then_inc(x_ln_in[s], 16)

            def load_x_res(i, s):
                sp.dma_start(x_res[:, s, :], rows(x_in, i)).then_inc(x_res_in[s], 16)

            def load_m(b):
                sp.dma_start(m_sb[:], m_dram[bass.ds(b, 1)].rearrange("a p t l c -> (a p) t l c")).then_inc(m_in, 16)

            def load_u(b):
                u = u_dram[bass.ds(b, 1)].rearrange("a r l n -> (a r) l n")
                sp.dma_start(u_sb[:, 0:KT - 1], u[0:(KT - 1) * P].rearrange("(k p) l n -> p k l n", p=P)).then_inc(u_in, 16)
                sp.dma_start(u_sb[0:LAST, KT - 1], u[(KT - 1) * P:COLS]).then_inc(u_in, 16)

            def store(i, s):
                sp.dma_start(rows(x_mid, i), x_out[:, s, :]).then_inc(stored[s], 16)
                sp.dma_start(rows(x_final, i), x_out[:, s, :]).then_inc(stored[s], 16)

            def step(i, s, more=True, before=True):
                if more:
                    sp.wait_ge(z_ready, i + 1)
                    load_x_ln(i + 2, s)
                if before:
                    sp.wait_ge(x_out_ready, i - 1)
                    store(i - 2, s)
                load_x_res(i, s)

            sp.dma_start(gamma[:], ln_gamma.rearrange("(a d) -> a d", a=1).broadcast_to([P, D])).then_inc(affine_in, 16)
            sp.dma_start(beta[:], ln_beta.rearrange("(a d) -> a d", a=1).broadcast_to([P, D])).then_inc(affine_in, 16)
            load_x_ln(0, 0)
            load_x_ln(1, 1)
            sp.dma_start(gate_bias[:], gate_b.rearrange("(a e) -> a e", a=1).broadcast_to([P, GATES])).then_inc(gate_in, 16)
            sp.dma_start(g_raw[:], g_ffn.rearrange("(a b) -> a b", a=1).broadcast_to([P, 1])).then_inc(g_in, 16)
            for t in range(DT):
                sp.dma_start(gate_raw[:, t, :], gate_w[:, t * P:(t + 1) * P].rearrange("e p -> p e"),
                             allow_slow_non_contiguous=True).then_inc(gate_in, 16)
            load_m(0)
            load_u(0)

            def batch(b, first=False, last=False):
                i0 = b * TPB
                step(i0, 0, before=not first)
                if not first:
                    sp.wait_ge(mix_ready, i0)
                    load_u(b)
                step(i0 + 1, 1, before=not first)
                with sp.Fori(0, TPB // 2 - 2) as q:
                    for k in range(2):
                        step(i0 + 2 * q + 2 + k, k)
                for k in range(2):
                    step(i0 + TPB - 2 + k, k, more=not last)
                if not last:
                    sp.wait_ge(scores_ready, 3 * (i0 + TPB))
                    load_m(b + 1)

            batch(0, first=True)
            with sp.Fori(1, BATCH - 1) as b:
                batch(b)
            batch(BATCH - 1, last=True)
            for i in range(TILES - 2, TILES):
                sp.wait_ge(x_out_ready, i + 1)
                store(i, i % 2)
            for s in range(2):
                sp.wait_ge(stored[s], 32 * TILES // 2)

        @block.tensor
        def _(pe):
            def transpose_z(i, s):
                pe.wait_ge(z_hi_ready, i + 1)
                pe.wait_ge(z_lo_ready, i + 1)
                pe.wait_ge(zT_ready, i)
                if later(i, 4):
                    pe.wait_ge(yT_ready, i - 3)
                for part in range(2):
                    for t in range(DT):
                        last = pe.transpose(zT_bank[:, part, t, :], z_parts[:, s, part, t * P:(t + 1) * P], ident16[:])
                last.then_inc(zT_summed, 1)

            def score(i, s):
                pe.wait_ge(zT_ready, i + 1)
                pe.wait_ge(m_in, 16 * (i // TPB) + 16)
                for k in range(3):
                    if later(i, 1):
                        pe.wait_ge(less_ready, 3 * (i - 1) + k + 1)
                    n, c0 = BANK_HEADS[k] * KEYS, HEAD0[k] * KEYS
                    for t in range(DT):
                        for zp, mp in PRODUCTS:
                            last = pe.matmul(scores[k][:, 0:n], zT[:, s, zp, t, :], m_sb[:, t, mp, c0:c0 + n],
                                             start=(t == 0 and (zp, mp) == PRODUCTS[0]),
                                             stop=(t == DT - 1 and (zp, mp) == PRODUCTS[-1]))
                    last.then_inc(scores_ready, 1)

            def transpose_p(i):
                pe.wait_ge(p_hi_ready, i + 1)
                pe.wait_ge(p_lo_ready, i + 1)
                for g, (k0, k1) in enumerate(PT_GROUPS):
                    if later(i, 1):
                        pe.wait_ge(pT_ready, 3 * i + g - 2)
                    if g == 2 and later(i, 3):
                        pe.wait_ge(logits_ready, i - 2)
                    if g == 2 and later(i, 5):
                        pe.wait_ge(place_ready, i - 4)
                    for k in range(k0, k1):
                        n = P if k < KT - 1 else LAST
                        for part in range(2):
                            last = pe.transpose(pT_bank[g][0:n, k - k0, part, :], p_parts[:, part, k * P:k * P + n],
                                                ident16[:])
                    last.then_inc(pT_summed, 1)

            def mix_values(i):
                pe.wait_ge(u_in, 32 * (i // TPB) + 32)
                pe.wait_ge(x_out_ready, i)
                for g, (k0, k1) in enumerate(PT_GROUPS):
                    pe.wait_ge(pT_ready, 3 * i + g + 1)
                    for k in range(k0, k1):
                        n = P if k < KT - 1 else LAST
                        for pp, up in PRODUCTS:
                            last = pe.matmul(mix[:], pT[0:n, k, pp, :], u_sb[0:n, k, up, :],
                                             start=(k == 0 and (pp, up) == PRODUCTS[0]),
                                             stop=(k == KT - 1 and (pp, up) == PRODUCTS[-1]))
                last.then_inc(mix_ready, 1)

            def transpose_y(i, s):
                pe.wait_ge(y_hi_ready, i + 1)
                pe.wait_ge(y_lo_ready, i + 1)
                pe.wait_ge(zT_ready, i + 4 if not isinstance(i, int) or i + 4 <= TILES else TILES)
                for part in range(2):
                    for t in range(DT):
                        last = pe.transpose(zT_bank[:, part, t, :], y_parts[:, s, part, t * P:(t + 1) * P], ident16[:])
                last.then_inc(yT_summed, 1)

            def gate(i):
                pe.wait_ge(yT_ready, i + 1)
                if isinstance(i, int) and i == 0:
                    pe.wait_ge(gate_lo_ready, 1)
                pe.wait_ge(logits_ready, i)
                if later(i, 3):
                    pe.wait_ge(place_ready, i - 2)
                pe.wait_ge(pT_ready, 3 * (i + 3) if not isinstance(i, int) or i + 3 <= TILES else 3 * TILES)
                for t in range(DT):
                    for yp, gp in PRODUCTS:
                        last = pe.matmul(gate_bank, yT[:, yp, t, :], gate_parts[:, t, gp, :],
                                         start=(t == 0 and (yp, gp) == PRODUCTS[0]),
                                         stop=(t == DT - 1 and (yp, gp) == PRODUCTS[-1]))
                last.then_inc(gate_summed, 1)

            def rank(i, s):
                pe.wait_ge(onehot_ready, i + 1)
                pe.wait_ge(placed_ready, i + 1)
                pe.wait_ge(place_ready, i)
                pe.wait_ge(logits_ready, i + 2 if not isinstance(i, int) or i + 2 <= TILES else TILES)
                pe.wait_ge(pT_ready, 3 * (i + 5) if not isinstance(i, int) or i + 5 <= TILES else 3 * TILES)
                hot = onehot[:, s].rearrange("p k e -> p (k e)")
                pe.matmul(rank_bank, below[:], hot, start=True, stop=False)
                pe.matmul(rank_bank, ones16[:], placed[:, 1 - s], start=False, stop=True).then_inc(rank_summed, 1)

            def step(i, s):
                if live(i):
                    score(i, s)
                if live(i - 1):
                    transpose_p(i - 1)
                if live(i + 1):
                    transpose_z(i + 1, 1 - s)
                if live(i - 1):
                    mix_values(i - 1)
                if live(i - 5):
                    rank(i - 5, 1 - s)
                if live(i - 3):
                    gate(i - 3)
                if live(i - 2):
                    transpose_y(i - 2, s)

            transpose_z(0, 0)
            run(pe, step)

        @block.scalar
        def _(act):
            def split_z(i, s):
                act.wait_ge(shifted_ready, i + 1)
                if not isinstance(i, int) or i >= 2:
                    act.wait_ge(zT_summed, i - 1)
                act.copy(z_parts[:, s, 0, :], z[:, s, :]).then_inc(z_hi_ready, 1)

            def copy_zT(i, s):
                act.wait_ge(zT_summed, i + 1)
                if not isinstance(i, int) or i >= 2:
                    act.wait_ge(scores_ready, 3 * (i - 1))
                act.copy(zT[:, s], zT_bank[:]).then_inc(zT_ready, 1)

            def exponent(i, s, k):
                n, c0 = BANK_HEADS[k] * KEYS, HEAD0[k] * KEYS
                act.wait_ge(less_ready, 3 * i + k + 1)
                act.activation(expd[:, s, c0:c0 + n], expd[:, s, c0:c0 + n], ACT.Exp,
                               scale=1.0 / M_SCALE).then_inc(exp_ready, 1)

            def split_p(i, s):
                act.wait_ge(p_ready, i + 1)
                act.wait_ge(pT_summed, 3 * i)
                act.copy(p_parts[:, 0, :], expd[:, s, :]).then_inc(p_hi_ready, 1)

            def copy_pT(i, g):
                k0, k1 = PT_GROUPS[g]
                act.wait_ge(pT_summed, 3 * i + g + 1)
                act.wait_ge(mix_ready, i)
                if k1 < KT:
                    act.copy(pT[:, k0:k1], pT_bank[g][:, 0:k1 - k0]).then_inc(pT_ready, 1)
                else:
                    act.copy(pT[:, k0:k1 - 1], pT_bank[g][:, 0:k1 - k0 - 1])
                    act.copy(pT[0:LAST, k1 - 1], pT_bank[g][0:LAST, k1 - k0 - 1]).then_inc(pT_ready, 1)

            def split_y(i, s):
                act.wait_ge(y_ready, i + 1)
                if later(i, 2):
                    act.wait_ge(yT_summed, i - 1)
                act.copy(y_parts[:, s, 0, :], y[:, s, :]).then_inc(y_hi_ready, 1)

            def copy_yT(i):
                act.wait_ge(yT_summed, i + 1)
                act.wait_ge(gate_summed, i)
                act.copy(yT[:], zT_bank[:]).then_inc(yT_ready, 1)

            def exponent_gap(i, s):
                act.wait_ge(gap_ready, i + 1)
                act.activation(ratio[:, s], gap[:, s], ACT.Exp).then_inc(ratio_ready, 1)

            def step(i, s):
                if live(i - 3):
                    copy_yT(i - 3)
                if live(i):
                    exponent(i, s, 0)
                if live(i - 2):
                    split_y(i - 2, s)
                if live(i):
                    exponent(i, s, 1)
                if live(i + 2):
                    split_z(i + 2, s)
                if live(i - 1):
                    copy_pT(i - 1, 0)
                if live(i):
                    exponent(i, s, 2)
                if live(i - 1):
                    copy_pT(i - 1, 1)
                    copy_pT(i - 1, 2)
                if live(i + 1):
                    copy_zT(i + 1, 1 - s)
                if live(i):
                    split_p(i, s)
                if live(i - 4):
                    exponent_gap(i - 4, s)

            act.wait_ge(g_in, 16)
            act.activation(g_tanh[:], g_raw[:], ACT.Tanh).then_inc(g_ready, 1)
            split_z(0, 0)
            copy_zT(0, 0)
            split_z(1, 1)
            run(act, step)

        @block.vector
        def _(dve):
            def moments_of(i, s):
                dve.wait_ge(x_ln_in[s], 8 * (i - s) + 16)
                dve.bn_stats(stats[:, s], x_ln[:, s, :]).then_inc(stats_ready, 1)

            def spread_of(i, s):
                dve.bn_aggr(moments[:, s], stats[:, s]).then_inc(moments_ready, 1)
                dve.wait_ge(moments_ready, i + 1)
                dve.tensor_scalar(spread[:, s], moments[:, s, 1:2], 1.0 + EPS, EPS * EPS, ALU.mult,
                                  ALU.add).then_inc(spread_ready, 1)

            def normalize(i, s):
                dve.wait_ge(rstd_ready, i + 1)
                if not isinstance(i, int) or i >= 2:
                    dve.wait_ge(z_lo_ready, i - 1)
                dve.tensor_scalar(z[:, s, :], x_ln[:, s, :], moments[:, s, 0:1], rstd[:, s], ALU.subtract,
                                  ALU.mult).then_inc(z_ready, 1)

            def less_top(i, s, k):
                h0, nh = HEAD0[k], BANK_HEADS[k]
                c0, n = h0 * KEYS, nh * KEYS
                bank = scores[k][:, 0:n].rearrange("p (h j) -> p h j", h=nh)
                dve.wait_ge(scores_ready, 3 * i + k + 1)
                dve.tensor_reduce(top[:, s, h0:h0 + nh], bank, AX_X, ALU.max).then_inc(top_ready, 1)
                dve.wait_ge(top_ready, 3 * i + k + 1)
                dve.tensor_tensor(expd[:, s, c0:c0 + n].rearrange("p (h j) -> p h j", h=nh), bank,
                                  top[:, s, h0:h0 + nh].unsqueeze(2).broadcast_to([P, nh, KEYS]),
                                  ALU.subtract).then_inc(less_ready, 1)

            def probabilities(i, s):
                e = expd[:, s, :].rearrange("p (h j) -> p h j", h=HEADS)
                dve.wait_ge(exp_ready, 3 * i + 3)
                dve.tensor_reduce(total[:, s], e, AX_X, ALU.add).then_inc(total_ready, 1)
                dve.wait_ge(total_ready, i + 1)
                dve.reciprocal(inverse[:, s], total[:, s]).then_inc(inverse_ready, 1)
                dve.wait_ge(inverse_ready, i + 1)
                dve.scalar_tensor_tensor(e, e, P_SCALE, inverse[:, s].unsqueeze(2).broadcast_to([P, HEADS, KEYS]),
                                         ALU.mult, ALU.mult).then_inc(p_ready, 1)

            def low_p(i, s):
                dve.wait_ge(p_hi_ready, i + 1)
                dve.tensor_tensor(p_parts[:, 1, :], expd[:, s, :], p_parts[:, 0, :], ALU.subtract).then_inc(p_lo_ready, 1)

            def residual(i, s):
                dve.wait_ge(mix_ready, i + 1)
                dve.wait_ge(x_res_in[s], 8 * (i - s) + 16)
                if not isinstance(i, int) or i >= 2:
                    dve.wait_ge(stored[s], 16 * (i - s))
                dve.scalar_tensor_tensor(x_out[:, s, :], mix[:], 1.0 / (P_SCALE * U_SCALE), x_res[:, s, :], ALU.mult,
                                         ALU.add).then_inc(x_out_ready, 1)

            def y_moments_of(i, s):
                dve.wait_ge(x_out_ready, i + 1)
                dve.bn_stats(x_stats[:, s], x_out[:, s, :]).then_inc(x_stats_ready, 1)

            def y_spread_of(i, s):
                dve.bn_aggr(x_moments[:, s], x_stats[:, s]).then_inc(x_moments_ready, 1)
                dve.wait_ge(x_moments_ready, i + 1)
                dve.tensor_scalar(x_spread[:, s], x_moments[:, s, 1:2], EPS, None, ALU.add).then_inc(x_spread_ready, 1)

            def y_normalize(i, s):
                dve.wait_ge(x_rstd_ready, i + 1)
                if later(i, 2):
                    dve.wait_ge(y_lo_ready, i - 1)
                dve.tensor_scalar(y[:, s, :], x_out[:, s, :], x_moments[:, s, 0:1], x_rstd[:, s], ALU.subtract,
                                  ALU.mult).then_inc(y_ready, 1)

            def choose(i, s):
                dve.wait_ge(gate_summed, i + 1)
                dve.scalar_tensor_tensor(logits[:, s, :], gate_bank, 1.0 / G_SCALE, gate_bias[:], ALU.mult,
                                         ALU.add).then_inc(logits_ready, 1)
                dve.wait_ge(logits_ready, i + 1)
                dve.nop(nofuse=True)
                dve.max(largest[:, s, :], logits[:, s, :]).then_inc(largest_ready, 1)
                dve.wait_ge(largest_ready, i + 1)
                dve.nop(nofuse=True)
                dve.max_index(found[:, s, :], largest[:, s, :], logits[:, s, :]).then_inc(choice_ready, 1)
                dve.tensor_scalar(gap[:, s], largest[:, s, 0:TOP_K], largest[:, s, 0:1], None,
                                  ALU.subtract).then_inc(gap_ready, 1)
                dve.tensor_copy(norms[:, s, 0:1], x_moments[:, s, 0:1])
                dve.tensor_copy(norms[:, s, 1:2], x_rstd[:, s]).then_inc(norms_ready, 1)
                dve.wait_ge(choice_ready, i + 1)
                dve.tensor_copy(expert[:, s], found[:, s, 0:TOP_K]).then_inc(expert_ready, 1)
                dve.wait_ge(expert_ready, i + 1)
                dve.tensor_tensor(onehot[:, s], iota_e[:], expert[:, s].unsqueeze(2).broadcast_to([P, TOP_K, EXPERTS]),
                                  ALU.is_equal).then_inc(onehot_ready, 1)

            def place_rows(i, s):
                dve.wait_ge(rank_summed, i + 1)
                dve.wait_ge(gate_summed, i + 3 if not isinstance(i, int) or i + 3 <= TILES else TILES)
                dve.tensor_tensor(place[:].rearrange("p k e -> p (k e)"), rank_bank, region[:].rearrange("p k e -> p (k e)"),
                                  ALU.add).then_inc(place_ready, 1)
                dve.wait_ge(ratio_ready, i + 1)
                dve.scalar_tensor_tensor(kept[:], expert[:, s], float(EXPERTS), ratio[:, s], ALU.is_lt,
                                         ALU.mult).then_inc(kept_ready, 1)
                dve.wait_ge(place_ready, i + 1)
                dve.tensor_tensor(mine[:], place[:], onehot[:, s], ALU.mult).then_inc(mine_ready, 1)
                dve.wait_ge(kept_ready, i + 1)
                dve.tensor_reduce(kept_sum[:], kept[:], AX_X, ALU.add).then_inc(kept_sum_ready, 1)
                dve.wait_ge(mine_ready, i + 1)
                dve.tensor_reduce(row[:], mine[:], AX_X, ALU.add).then_inc(row_ready, 1)
                dve.wait_ge(kept_sum_ready, i + 1)
                dve.scalar_tensor_tensor(kept_div[:], kept_sum[:], 0.0, kept_sum[:], ALU.is_equal,
                                         ALU.add).then_inc(kept_div_ready, 1)
                dve.tensor_scalar(no_row[:], expert[:, s], float(EXPERTS), NO_ROW, ALU.is_ge,
                                  ALU.mult).then_inc(no_row_ready, 1)
                dve.wait_ge(kept_div_ready, i + 1)
                dve.reciprocal(kept_inv[:], kept_div[:]).then_inc(kept_inv_ready, 1)
                dve.wait_ge(row_ready, i + 1)
                dve.wait_ge(no_row_ready, i + 1)
                dve.tensor_tensor(row_f[:], row[:], no_row[:], ALU.add).then_inc(row_f_ready, 1)
                if later(i, 2):
                    dve.wait_ge(scattered[s], 16 * (i - s))
                dve.wait_ge(row_f_ready, i + 1)
                dve.tensor_copy(row_i[:, s], row_f[:]).then_inc(row_i_ready, 1)
                dve.wait_ge(kept_inv_ready, i + 1)
                dve.tensor_scalar(payload[:, s, :, 1], kept[:], kept_inv[:], g_tanh[:], ALU.mult,
                                  ALU.mult).then_inc(weight_ready, 1)
                dve.tensor_copy(payload[:, s, :, 0], iota_t[:, bass.ds(i, 1)].broadcast_to([P, TOP_K]))
                dve.wait_ge(norms_ready, i + 1)
                dve.tensor_copy(payload[:, s, :, 2:4], norms[:, s].unsqueeze(1).broadcast_to([P, TOP_K, 2])).then_inc(
                    payload_ready, 1)
                dve.tensor_tensor(placed[:, s], placed[:, 1 - s], onehot[:, s].rearrange("p k e -> p (k e)"),
                                  ALU.add).then_inc(placed_ready, 1)

            def step(i, s):
                if live(i - 2):
                    residual(i - 2, s)
                    y_moments_of(i - 2, s)
                if live(i + 2):
                    moments_of(i + 2, s)
                if live(i - 6):
                    place_rows(i - 6, s)
                if live(i - 4):
                    choose(i - 4, s)
                if live(i - 2):
                    dve.wait_ge(x_stats_ready, i - 1)
                if live(i + 2):
                    dve.wait_ge(stats_ready, i + 3)
                dve.nop(nofuse=True)
                if live(i - 2):
                    y_spread_of(i - 2, s)
                if live(i + 2):
                    spread_of(i + 2, s)
                if live(i):
                    less_top(i, s, 0)
                if live(i - 2):
                    y_normalize(i - 2, s)
                if live(i + 2):
                    normalize(i + 2, s)
                if live(i):
                    less_top(i, s, 1)
                    less_top(i, s, 2)
                    probabilities(i, s)
                    low_p(i, s)

            dve.memset(minus_half[:], -0.5).then_inc(const_ready, 1)
            dve.wait_ge(gate_in, 16 * (DT + 1))
            dve.tensor_scalar(gate_scaled[:], gate_raw[:], G_SCALE, None, ALU.mult).then_inc(gate_scaled_ready, 1)
            dve.wait_ge(gate_scaled_ready, 1)
            dve.tensor_copy(gate_parts[:, :, 0, :], gate_scaled[:]).then_inc(gate_hi_ready, 1)
            dve.wait_ge(gate_hi_ready, 1)
            dve.tensor_tensor(gate_parts[:, :, 1, :], gate_scaled[:], gate_parts[:, :, 0, :],
                              ALU.subtract).then_inc(gate_lo_ready, 1)
            dve.wait_ge(iota_ready, 4)
            dve.wait_ge(g_ready, 1)
            dve.memset(placed[:], 0.0).then_inc(placed_ready, 1)
            dve.wait_ge(placed_ready, 1)
            for i in range(2):
                moments_of(i, i)
                dve.wait_ge(stats_ready, i + 1)
                spread_of(i, i)
                normalize(i, i)
            run(dve, step)

        @block.gpsimd
        def _(pool):
            def layernorm(i, s):
                pool.wait_ge(spread_ready, i + 1)
                pool.tensor_tensor(rstd[:, s], spread[:, s], minus_half[:], ALU.pow).then_inc(rstd_ready, 1)
                pool.wait_ge(z_ready, i + 1)
                pool.tensor_tensor(z[:, s, :], z[:, s, :], gamma[:], ALU.mult).then_inc(scaled_ready, 1)
                pool.wait_ge(scaled_ready, i + 1)
                pool.tensor_tensor(z[:, s, :], z[:, s, :], beta[:], ALU.add).then_inc(shifted_ready, 1)
                pool.wait_ge(z_hi_ready, i + 1)
                pool.tensor_tensor(z_parts[:, s, 1, :], z[:, s, :], z_parts[:, s, 0, :], ALU.subtract).then_inc(z_lo_ready, 1)

            def y_rstd(i, s):
                pool.wait_ge(x_spread_ready, i + 1)
                pool.tensor_tensor(x_rstd[:, s], x_spread[:, s], minus_half[:], ALU.pow).then_inc(x_rstd_ready, 1)

            def y_low(i, s):
                pool.wait_ge(y_hi_ready, i + 1)
                pool.tensor_tensor(y_parts[:, s, 1, :], y[:, s, :], y_parts[:, s, 0, :], ALU.subtract).then_inc(y_lo_ready, 1)

            def scatter(i, s):
                pool.wait_ge(row_i_ready, i + 1)
                pool.wait_ge(weight_ready, i + 1)
                pool.wait_ge(payload_ready, i + 1)
                pool.nop(nofuse=True)
                for k in range(TOP_K):
                    pool.indirect_dma_start(table, bass.IndirectOffsetOnAxis(ap=row_i[:, s, k:k + 1], axis=0),
                                            payload[:, s, k, :], None, bounds_check=TABLE_ROWS - 1,
                                            oob_is_err=False).then_inc(scattered[s], 16)

            def step(i, s):
                if live(i - 2):
                    y_rstd(i - 2, s)
                if live(i + 2):
                    layernorm(i + 2, s)
                if live(i - 2):
                    y_low(i - 2, s)
                if live(i - 6):
                    scatter(i - 6, s)

            for k in range(TOP_K):
                pool.iota(iota_e[:, k], pattern=[[1, EXPERTS]], base=0, channel_multiplier=0,
                          allow_small_or_imprecise_dtypes=True)
                last = pool.iota(region[:, k], pattern=[[REGION_ROWS, EXPERTS]], base=k * REGIONS * REGION_ROWS,
                                 channel_multiplier=0, allow_small_or_imprecise_dtypes=True)
            last.then_inc(iota_ready, 1)
            pool.iota(iota_t[:], pattern=[[P, TILES]], base=0, channel_multiplier=1,
                      allow_small_or_imprecise_dtypes=True).then_inc(iota_ready, 1)
            pool.memset(below[:], 1.0).then_inc(iota_ready, 1)
            pool.wait_ge(iota_ready, 3)
            pool.affine_select(out=below[:], in_=below[:], compare_op=ALU.is_gt, fill=0.0, base=0,
                               pattern=[[1, P]], channel_multiplier=-1).then_inc(iota_ready, 1)
            pool.wait_ge(const_ready, 1)
            pool.wait_ge(affine_in, 32)
            layernorm(0, 0)
            layernorm(1, 1)
            run(pool, step)
            for s in range(2):
                pool.wait_ge(scattered[s], 16 * TOP_K * TILES // 2)


def list_tiles(nc, ones16, placed, tile_expert, tile_row):
    with ExitStack() as stack:
        def sb(name, shape, dt=F32):
            return stack.enter_context(nc.sbuf_tensor(name, shape, dt))

        def sem(name):
            return stack.enter_context(nc.semaphore(name))

        tokens = sb("tokens", [P, TOP_K, EXPERTS], I32)
        padded = sb("padded", [P, TOP_K, EXPERTS], I32)
        tiles_i = sb("tiles_i", [P, TOP_K, EXPERTS], I32)
        tiles_f = sb("tiles_f", [P, TOP_K, EXPERTS])
        ends = [sb(f"ends{n}", [P, TOP_K, EXPERTS]) for n in range(4)]
        iota_j = sb("iota_j", [P, SLOT_TILES, EXPERTS])
        iota_r = sb("iota_r", [P, SLOT_TILES])
        past = sb("past", [P, TOP_K, SLOT_TILES, EXPERTS])
        before = sb("before", [P, TOP_K, SLOT_TILES, EXPERTS])
        owner = sb("owner", [P, TOP_K, SLOT_TILES])
        clamped = sb("clamped", [P, TOP_K, SLOT_TILES])
        gone = sb("gone", [P, TOP_K, SLOT_TILES])
        nth = sb("nth", [P, TOP_K, SLOT_TILES])
        first = sb("first", [P, TOP_K, SLOT_TILES])
        sums = stack.enter_context(nc.psum_tensor("sums", [P, TOP_K * EXPERTS], F32))
        summed = sem("summed")
        iotas = sem("iotas")
        done = sem("done")
        block = stack.enter_context(nc.Block())

        @block.tensor
        def _(pe):
            pe.matmul(sums[:], ones16[:], placed[:, (TILES - 1) % 2], start=True, stop=True).then_inc(summed, 1)

        @block.gpsimd
        def _(pool):
            pool.iota(iota_j[:], pattern=[[1, SLOT_TILES], [0, EXPERTS]], base=0, channel_multiplier=0,
                      allow_small_or_imprecise_dtypes=True).then_inc(iotas, 1)
            pool.iota(iota_r[:], pattern=[[P, SLOT_TILES]], base=0, channel_multiplier=0,
                      allow_small_or_imprecise_dtypes=True).then_inc(iotas, 1)

        @block.vector
        def _(dve):
            count = [0]

            def after(instruction):
                instruction.then_inc(done, 1)
                count[0] += 1
                dve.wait_ge(done, count[0])

            dve.wait_ge(summed, 1)
            dve.wait_ge(iotas, 2)
            after(dve.tensor_scalar(tokens[:].rearrange("p k e -> p (k e)"), sums[:], float(P - 1), None, ALU.add))
            after(dve.tensor_scalar(tiles_i[:], tokens[:], 7, None, ALU.arith_shift_right))
            after(dve.tensor_copy(tiles_f[:], tiles_i[:]))
            last, n = tiles_f, 1
            for to in ends[0:3]:
                after(dve.tensor_copy(to[:, :, 0:n], last[:, :, 0:n]))
                after(dve.tensor_tensor(to[:, :, n:], last[:, :, n:], last[:, :, 0:EXPERTS - n], ALU.add))
                last, n = to, 2 * n
            for k in range(TOP_K):
                end = last[:, k].unsqueeze(1).broadcast_to([P, SLOT_TILES, EXPERTS])
                size = tiles_f[:, k].unsqueeze(1).broadcast_to([P, SLOT_TILES, EXPERTS])
                after(dve.tensor_tensor(past[:, k], iota_j[:], end, ALU.is_ge))
                after(dve.tensor_tensor(before[:, k], past[:, k], size, ALU.mult))
                after(dve.tensor_reduce(owner[:, k], past[:, k], AX_X, ALU.add))
                after(dve.tensor_reduce(gone[:, k], before[:, k], AX_X, ALU.add))
                after(dve.tensor_scalar(clamped[:, k], owner[:, k], float(EXPERTS - 1), None, ALU.min))
                after(dve.tensor_copy(tile_expert[:, k], clamped[:, k]))
                after(dve.scalar_tensor_tensor(nth[:, k], gone[:, k], -float(P), iota_r[:], ALU.mult, ALU.add))
                after(dve.scalar_tensor_tensor(first[:, k], owner[:, k], float(REGION_ROWS), nth[:, k], ALU.mult,
                                               ALU.add))
                after(dve.tensor_scalar(tile_row[:, k], first[:, k], float(k * REGIONS * REGION_ROWS), None, ALU.add))


def run_experts(nc, k, ident16, w_parts, tile_expert, tile_row, expert_bias, table, x_mid, x_sum, x_final):
    R = 4
    same = x_sum is x_mid
    with ExitStack() as stack:
        def sb(name, shape, dt=F32):
            return stack.enter_context(nc.sbuf_tensor(f"{name}_{k}", shape, dt))

        def sem(name):
            return stack.enter_context(nc.semaphore(f"{name}_{k}"))

        slots = sb("slots", [P, SLOT_TILES, 4])
        token = sb("token", [P, R, 1], I32)
        token_out = sb("token_out", [P, R, 1], I32)
        x_got = sb("x_got", [P, R, D])
        sum_got = x_got if same else sb("sum_got", [P, R, D])
        y = sb("y", [P, 2, D])
        y_parts = sb("y_parts", [P, 2, 2, D], F16)
        yT = sb("yT", [P, 2, 2, DT, P], F16)
        biased = sb("biased", [P, 2, D])
        result = sb("result", [P, R, D])
        yT_bank = [stack.enter_context(nc.psum_tensor(f"yT_bank{s}_{k}", [P, 2, DT, P], F16)) for s in range(2)]
        out_bank = [stack.enter_context(nc.psum_tensor(f"out_bank{s}_{k}", [P, D], F32)) for s in range(2)]

        slots_in = sem("slots_in")
        cleared = sem("cleared")
        token_ready = sem("token_ready")
        got = [sem(f"got{s}") for s in range(R)]
        y_ready = sem("y_ready")
        y_hi_ready = sem("y_hi_ready")
        y_lo_ready = sem("y_lo_ready")
        yT_summed = sem("yT_summed")
        yT_ready = sem("yT_ready")
        expert_summed = sem("expert_summed")
        biased_ready = sem("biased_ready")
        token_out_ready = sem("token_out_ready")
        result_ready = sem("result_ready")
        put = [sem(f"put{s}") for s in range(R)]
        GATHERS = 16 if same else 32

        def live(j):
            return not isinstance(j, int) or 0 <= j < SLOT_TILES

        def later(j, n):
            return not isinstance(j, int) or j >= n

        def run(engine, step):
            first, last = R, SLOT_TILES - R
            for j in range(-4, first):
                step(j, j % R)
            with engine.Fori(0, (last - first) // R) as r:
                for s in range(R):
                    step(R * r + first + s, s)
            for j in range(last, SLOT_TILES + 1):
                step(j, j % R)

        block = stack.enter_context(nc.Block())

        @block.sync
        def _(sp):
            with sp.Fori(0, SLOT_TILES) as j:
                row = sp.value_load(tile_row[0:1, k, bass.ds(j, 1)], min_val=0, max_val=TABLE_ROWS - P)
                sp.dma_start(slots[:, bass.ds(j, 1), :].rearrange("p a w -> p (a w)"),
                             table[bass.ds(row, P), :]).then_inc(slots_in, 16)

        @block.gpsimd
        def _(pool):
            def gather(j, s):
                pool.wait_ge(token_ready, j + 1)
                pool.nop(nofuse=True)
                at = bass.IndirectOffsetOnAxis(ap=token[:, s, :], axis=0)
                pool.indirect_dma_start(x_got[:, s, :], None, x_mid, at, bounds_check=TOKENS - 1,
                                        oob_is_err=False).then_inc(got[s], 16)
                if not same:
                    pool.indirect_dma_start(sum_got[:, s, :], None, x_sum, at, bounds_check=TOKENS - 1,
                                            oob_is_err=False).then_inc(got[s], 16)

            def scatter(j, s):
                pool.wait_ge(token_out_ready, j + 1)
                pool.wait_ge(result_ready, j + 1)
                pool.nop(nofuse=True)
                pool.indirect_dma_start(x_final, bass.IndirectOffsetOnAxis(ap=token_out[:, s, :], axis=0),
                                        result[:, s, :], None, bounds_check=TOKENS - 1,
                                        oob_is_err=False).then_inc(put[s], 16)

            def step(j, s):
                if live(j - 1):
                    scatter(j - 1, (s - 1) % R)
                if live(j + 3):
                    gather(j + 3, (s + 3) % R)

            pool.wait_ge(cleared, 2)
            run(pool, step)
            for s in range(R):
                pool.wait_ge(put[s], 16 * SLOT_TILES // R)

        @block.tensor
        def _(pe):
            def transpose_y(j, s):
                pe.wait_ge(y_hi_ready, j + 1)
                pe.wait_ge(y_lo_ready, j + 1)
                if later(j, 2):
                    pe.wait_ge(yT_ready, j - 1)
                for part in range(2):
                    for t in range(DT):
                        last = pe.transpose(yT_bank[s][:, part, t, :], y_parts[:, s, part, t * P:(t + 1) * P], ident16[:])
                last.then_inc(yT_summed, 1)

            def multiply(j, s):
                e = pe.value_load(tile_expert[0:1, k, bass.ds(j, 1)], min_val=0, max_val=EXPERTS - 1)
                pe.wait_ge(yT_ready, j + 1)
                if later(j, 2):
                    pe.wait_ge(biased_ready, j - 1)
                for t in range(DT):
                    for yp, wp in PRODUCTS:
                        last = pe.matmul(out_bank[s][:], yT[:, s, yp, t, :],
                                         w_parts[:, bass.ds(e, 1), t, wp, :].rearrange("p a n -> p (a n)"),
                                         start=(t == 0 and (yp, wp) == PRODUCTS[0]),
                                         stop=(t == DT - 1 and (yp, wp) == PRODUCTS[-1]))
                last.then_inc(expert_summed, 1)

            def step(j, s):
                if live(j + 1):
                    transpose_y(j + 1, (s + 1) % 2)
                if live(j):
                    multiply(j, s % 2)

            run(pe, step)

        @block.scalar
        def _(act):
            def step(j, s):
                if live(j + 1):
                    act.wait_ge(yT_summed, j + 2)
                    if later(j, 1):
                        act.wait_ge(expert_summed, j)
                    act.copy(yT[:, (s + 1) % 2], yT_bank[(s + 1) % 2][:]).then_inc(yT_ready, 1)
                if live(j + 2):
                    act.wait_ge(y_ready, j + 3)
                    if later(j, 0):
                        act.wait_ge(yT_summed, j + 1)
                    act.copy(y_parts[:, s % 2, 0, :], y[:, s % 2, :]).then_inc(y_hi_ready, 1)

            run(act, step)

        @block.vector
        def _(dve):
            def name_token(j, s):
                if later(j, R):
                    dve.wait_ge(got[s], GATHERS * ((j - s) // R) if isinstance(j, int) else GATHERS // R * (j - s))
                dve.tensor_copy(token[:, s, :], slots[:, bass.ds(j, 1), 0:1].rearrange("p a b -> p (a b)")).then_inc(
                    token_ready, 1)

            def normalize(j, s):
                dve.wait_ge(got[s], GATHERS * ((j - s) // R + 1) if isinstance(j, int) else GATHERS // R * (j - s) + GATHERS)
                if later(j, 2):
                    dve.wait_ge(y_lo_ready, j - 1)
                at = slots[:, bass.ds(j, 1), 2:4].rearrange("p a b -> p (a b)")
                dve.tensor_scalar(y[:, s % 2, :], x_got[:, s, :], at[:, 0:1], at[:, 1:2], ALU.subtract,
                                  ALU.mult).then_inc(y_ready, 1)

            def low_y(j, s):
                dve.wait_ge(y_hi_ready, j + 1)
                dve.tensor_tensor(y_parts[:, s % 2, 1, :], y[:, s % 2, :], y_parts[:, s % 2, 0, :],
                                  ALU.subtract).then_inc(y_lo_ready, 1)

            def finish(j, s):
                e = dve.value_load(tile_expert[0:1, k, bass.ds(j, 1)], min_val=0, max_val=EXPERTS - 1)
                dve.wait_ge(expert_summed, j + 1)
                dve.scalar_tensor_tensor(biased[:, s % 2, :], out_bank[s % 2][:], 1.0 / W_SCALE,
                                         expert_bias[:, bass.ds(e, 1), :].rearrange("p a n -> p (a n)"), ALU.mult,
                                         ALU.add).then_inc(biased_ready, 1)
                if later(j, R):
                    dve.wait_ge(put[s], 16 * ((j - s) // R) if isinstance(j, int) else 4 * (j - s))
                at = slots[:, bass.ds(j, 1), 0:2].rearrange("p a b -> p (a b)")
                dve.tensor_copy(token_out[:, s, :], at[:, 0:1]).then_inc(token_out_ready, 1)
                dve.wait_ge(biased_ready, j + 1)
                dve.scalar_tensor_tensor(result[:, s, :], biased[:, s % 2, :], at[:, 1:2], sum_got[:, s, :], ALU.mult,
                                         ALU.add).then_inc(result_ready, 1)

            def step(j, s):
                if live(j - 1):
                    finish(j - 1, (s - 1) % R)
                if live(j + 4):
                    name_token(j + 4, s)
                if live(j + 2):
                    normalize(j + 2, (s + 2) % R)
                    low_y(j + 2, (s + 2) % R)

            dve.memset(x_got[:], 0.0).then_inc(cleared, 1)
            dve.memset(sum_got[:] if not same else biased[:], 0.0).then_inc(cleared, 1)
            dve.wait_ge(cleared, 2)
            dve.wait_ge(slots_in, 16 * SLOT_TILES)
            run(dve, step)


def flamingo_block(nc, x, ctx_1024, g_xattn, g_ffn, L0_xattn_ln_gamma, L0_xattn_ln_beta, L0_xattn_w_q,
                   L0_xattn_w_kv, L0_xattn_w_out, L0_xattn_b_out, L0_xattn_gate, L0_ffn_gate_w, L0_ffn_gate_b,
                   L0_ffn_expert_w, L0_ffn_expert_b, identity, out):
    x_in = x.rearrange("b s d -> (b s) d")
    x_final = out.rearrange("b s d -> (b s) d")
    m_dram = nc.dram_tensor("m_dram", [BATCH, P, DT, 2, COLS], F16, kind="Internal").ap()
    u_dram = nc.dram_tensor("u_dram", [BATCH, COLS, 2, D], F16, kind="Internal").ap()
    x_mid = nc.dram_tensor("x_mid", [TOKENS, D], F32, kind="Internal").ap()
    table = nc.dram_tensor("table", [TABLE_ROWS, 4], F32, kind="Internal").ap()
    with ExitStack() as stack:
        ident = stack.enter_context(nc.sbuf_tensor("ident", [P, P], F32))
        ident16 = stack.enter_context(nc.sbuf_tensor("ident16", [P, P], F16))
        ones16 = stack.enter_context(nc.sbuf_tensor("ones16", [P, P], F16))
        placed = stack.enter_context(nc.sbuf_tensor("placed", [P, 2, TOP_K * EXPERTS], F16))
        w_parts = stack.enter_context(nc.sbuf_tensor("w_parts", [P, EXPERTS, DT, 2, D], F16))
        ident_in = stack.enter_context(nc.semaphore("ident_in"))
        ident16_ready = stack.enter_context(nc.semaphore("ident16_ready"))
        bias_in = stack.enter_context(nc.semaphore("bias_in"))
        with nc.Block() as block:
            @block.sync
            def _(sp):
                sp.dma_start(ident[:], identity).then_inc(ident_in, 16)

            @block.vector
            def _(dve):
                dve.wait_ge(ident_in, 16)
                dve.tensor_copy(ident16[:], ident[:]).then_inc(ident16_ready, 1)
                dve.memset(ones16[:], 1.0).then_inc(ident16_ready, 1)
                dve.wait_ge(ident16_ready, 2)

        fold_context(nc, ident, x_in, L0_xattn_w_q, L0_xattn_w_kv, L0_xattn_w_out, L0_xattn_b_out, L0_xattn_gate,
                     g_xattn, ctx_1024, m_dram, u_dram, L0_ffn_expert_w, w_parts, table)
        attend(nc, ident16, x_in, L0_xattn_ln_gamma, L0_xattn_ln_beta, m_dram, u_dram, x_mid, x_final,
               L0_ffn_gate_w, L0_ffn_gate_b, g_ffn, table, placed, ones16)
        tile_expert = stack.enter_context(nc.sbuf_tensor("tile_expert", [P, TOP_K, SLOT_TILES], I32))
        tile_row = stack.enter_context(nc.sbuf_tensor("tile_row", [P, TOP_K, SLOT_TILES], I32))
        expert_bias = stack.enter_context(nc.sbuf_tensor("expert_bias", [P, EXPERTS, D], F32))
        with nc.Block() as block:
            @block.sync
            def _(sp):
                sp.dma_start(expert_bias[:], L0_ffn_expert_b.rearrange("(a e) d -> a e d", a=1).broadcast_to(
                    [P, EXPERTS, D])).then_inc(bias_in, 16)
                sp.wait_ge(bias_in, 16)

        list_tiles(nc, ones16, placed, tile_expert, tile_row)
        run_experts(nc, 0, ident16, w_parts, tile_expert, tile_row, expert_bias, table, x_mid, x_mid, x_final)
        run_experts(nc, 1, ident16, w_parts, tile_expert, tile_row, expert_bias, table, x_mid, x_final, x_final)


_INS = ['x', 'ctx_1024', 'g_xattn', 'g_ffn', 'L0_xattn_ln_gamma', 'L0_xattn_ln_beta', 'L0_xattn_w_q',
        'L0_xattn_w_kv', 'L0_xattn_w_out', 'L0_xattn_b_out', 'L0_xattn_gate', 'L0_ffn_gate_w', 'L0_ffn_gate_b',
        'L0_ffn_expert_w', 'L0_ffn_expert_b']


def kernel(**inputs):
    import numpy as _np
    import concourse.bacc as _bacc
    from concourse import mybir as _mybir
    from concourse.bass_utils import run_bass_kernel_spmd as _run

    nc = _bacc.Bacc("TRN2", target_bir_lowering=False, num_devices=1)
    arrays, args = {}, []
    given = [(name, _np.ascontiguousarray(inputs[name])) for name in _INS]
    given.append(("identity", _np.eye(128, dtype=_np.float32)))
    for name, a in given:
        arrays[f"in_{name}_dram"] = a
        args.append(nc.dram_tensor(f"in_{name}_dram", a.shape, _mybir.dt.from_np(a.dtype), kind="ExternalInput").ap())
    args.append(nc.dram_tensor("out_0_dram", (4, 2048, 512), _mybir.dt.float32, kind="ExternalOutput").ap())
    flamingo_block(nc, *args)
    r = _run(nc, [arrays], core_ids=[0])
    return r.results[0]["out_0_dram"]
```

```python
from contextlib import ExitStack

import concourse.bass as bass
from concourse import mybir
from concourse.alu_op_type import AluOpType as ALU

F32 = mybir.dt.float32
F16 = mybir.dt.float16
I32 = mybir.dt.int32
U32 = mybir.dt.uint32
ACT = mybir.ActivationFunctionType
AX_X = mybir.AxisListType.X

P = 128
D = 512
DT = D // P
HEADS = 16
DH = 64
INNER = HEADS * DH
PAIRS = INNER // P
BATCH = 4
SEQ = 2048
KEYS = 77
TOKENS = BATCH * SEQ
TILES = TOKENS // P
TPB = SEQ // P
COLS = HEADS * KEYS
KT = -(-COLS // P)
LAST = COLS - (KT - 1) * P
BANK_HEADS = (6, 5, 5)
HEAD0 = (0, 6, 11)
PT_GROUPS = ((0, 4), (4, 8), (8, 10))
EPS = 1e-5
EXPERTS = 8
GATES = EXPERTS + 2
TOP_K = 2
REGIONS = EXPERTS + 1
SLOT_TILES = TILES + EXPERTS
REGION_ROWS = SLOT_TILES * P
TABLE_ROWS = TOP_K * REGIONS * REGION_ROWS
TABLE_TILES = TABLE_ROWS // P
NO_ROW = float(1 << 25)
RING = 6
PASSES = SLOT_TILES // RING
LISTED = 8
NO_TOKEN = float(TOKENS)

M_SCALE = 64.0
U_SCALE = 64.0
P_SCALE = 4096.0
G_SCALE = 64.0
W_SCALE = 64.0
PRODUCTS = ((0, 0), (0, 1), (1, 0))


def fold_context(nc, ident, wq, wkv, wout, b_out, gate, g_xattn, ctx, m_dram, u_dram, expert_w, w_parts, table):
    NB = 8
    US = 4
    RAW = 4
    FILL = 54
    FILLS = TABLE_TILES // FILL
    C_SCALE, W16, K_SCALE = 16.0, 64.0, 16.0
    WQ_CHUNK, WOUT_CHUNK, EXPERT_CHUNK = 4, 6, 8
    KV0 = DT
    WQ0 = KV0 + 2 * PAIRS
    M0 = WQ0 + PAIRS
    NM = DT * HEADS
    U0 = M0 + NM
    NU = BATCH * HEADS
    CK = BATCH * KEYS
    with ExitStack() as stack:
        def sb(name, shape, dt=F32):
            return stack.enter_context(nc.sbuf_tensor(name, shape, dt))

        def sem(name):
            return stack.enter_context(nc.semaphore(name))

        raw = sb("raw", [P, RAW, DT, D])
        ctx_sb = sb("ctx_sb", [KEYS, BATCH, D])
        ctxT = sb("ctxT", [P, 2, DT, CK], F16)
        kvw_parts = sb("kvw_parts", [P, 4, 2, DT, D], F16)
        wqT = sb("wqT", [P, 2, PAIRS, D], F16)
        kvT = sb("kvT", [P, 2, 2 * PAIRS, CK], F16)
        stage = sb("stage", [P, 2 * BATCH * 2 * 4 * KEYS], F16)
        m_stage = stage[:].rearrange("p (g b l c) -> p g b l c", g=2, b=BATCH, l=2)
        u_stage = stage[0:KEYS, 0:US * 2 * D].rearrange("p (u l n) -> p u l n", u=US, l=2)
        fill = sb("fill", [P, FILL, 4])
        bias = sb("bias", [1, D])
        bias_parts = sb("bias_parts", [1, 2, D], F16)
        ones_row = sb("ones_row", [1, KEYS], F16)
        gates = sb("gates", [P, 2])
        tanhs = sb("tanhs", [P, 2])
        u_gain = sb("u_gain", [P, 1])
        banks = [stack.enter_context(nc.psum_tensor(f"fold{i}", [P, 512], F32)) for i in range(NB)]

        ctx_in = sem("ctx_in")
        raw_in = [sem(f"raw_in{i}") for i in range(RAW)]
        small_in = sem("small_in")
        tanh_ready = sem("tanh_ready")
        gain_ready = sem("gain_ready")
        ones_ready = sem("ones_ready")
        bias_hi_ready = sem("bias_hi_ready")
        bias_lo_ready = sem("bias_lo_ready")
        chunk_hi_ready = sem("chunk_hi_ready")
        chunk_lo_ready = sem("chunk_lo_ready")
        product_ready = sem("product_ready")
        hi_ready = sem("hi_ready")
        lo_ready = sem("lo_ready")
        m_stored = [sem(f"m_stored{i}") for i in range(2)]
        u_stored = [sem(f"u_stored{i}") for i in range(US)]
        w_scaled = sem("w_scaled")
        w_hi_ready = sem("w_hi_ready")
        w_lo_ready = sem("w_lo_ready")
        fill_zero = sem("fill_zero")
        fill_ready = sem("fill_ready")
        table_clear = sem("table_clear")

        def raw_wait(engine, c):
            engine.wait_ge(raw_in[c % RAW], 16 * (c // RAW + 1))

        def job(n):
            bank = banks[n % NB]
            if n < KV0:
                return ctxT[:, 0, n], ctxT[:, 1, n], bank[:, 0:CK], C_SCALE
            if n < WQ0:
                m = n - KV0
                return kvT[:, 0, m], kvT[:, 1, m], bank[:, 0:CK], K_SCALE / (C_SCALE * W16)
            if n < M0:
                m = n - WQ0
                return wqT[:, 0, m], wqT[:, 1, m], bank[:], W16
            if n < U0:
                g, hh = divmod(n - M0, 4)
                cols = slice(hh * KEYS, (hh + 1) * KEYS)
                return (m_stage[:, g % 2, :, 0, cols], m_stage[:, g % 2, :, 1, cols],
                        bank[:, 0:CK].rearrange("p (b j) -> p b j", b=BATCH),
                        M_SCALE * DH ** -0.5 / (K_SCALE * W16))
            u = (n - U0) % US
            return u_stage[:, u, 0], u_stage[:, u, 1], bank[0:KEYS, :], u_gain[0:KEYS, :]

        def stage_free(engine, n):
            if M0 <= n < U0:
                g, hh = divmod(n - M0, 4)
                if hh == 0 and g >= 2:
                    engine.wait_ge(m_stored[g % 2], 16 * BATCH * (g // 2))
            elif n >= U0 + US:
                engine.wait_ge(u_stored[n % US], 16 * ((n - U0) // US))
            elif n == U0:
                for g in range(2):
                    engine.wait_ge(m_stored[g], 16 * BATCH * NM // 8)

        block = stack.enter_context(nc.Block())

        @block.sync
        def _(sp):
            def load_chunk(c):
                if c < WQ_CHUNK:
                    src = wkv[:, c * D:(c + 1) * D]
                elif c < WOUT_CHUNK:
                    src = wq[:, (c - WQ_CHUNK) * D:(c - WQ_CHUNK + 1) * D]
                elif c < EXPERT_CHUNK:
                    src = wout[(c - WOUT_CHUNK) * DT * P:(c - WOUT_CHUNK + 1) * DT * P, :]
                else:
                    src = expert_w[c - EXPERT_CHUNK]
                sp.dma_start(raw[:, c % RAW], src.rearrange("(t p) n -> p t n", p=P)).then_inc(raw_in[c % RAW], 16)

            sp.dma_start(ctx_sb[:], ctx.rearrange("b j d -> j b d")).then_inc(ctx_in, 16)
            for c in range(RAW):
                load_chunk(c)
            sp.dma_start(gates[:, 0:1], gate.rearrange("(a b) -> a b", a=1).broadcast_to([P, 1])).then_inc(small_in, 16)
            sp.dma_start(gates[:, 1:2], g_xattn.rearrange("(a b) -> a b", a=1).broadcast_to([P, 1])).then_inc(small_in, 16)
            sp.dma_start(bias[:], b_out.rearrange("(a d) -> a d", a=1)).then_inc(small_in, 16)
            for c in range(WQ_CHUNK, EXPERT_CHUNK):
                sp.wait_ge(chunk_lo_ready, c - RAW + 1)
                load_chunk(c)
            sp.wait_ge(fill_ready, 1)
            sp.dma_start(table.rearrange("(p c r) w -> p c (r w)", p=P, c=FILLS),
                         fill[:].rearrange("p r w -> p (r w)").unsqueeze(1).broadcast_to([P, FILLS, FILL * 4]),
                         ).then_inc(table_clear, 16)
            sp.wait_ge(product_ready, M0)
            for c in (8, 9):
                load_chunk(c)
            sp.wait_ge(chunk_lo_ready, 6)
            for c in (10, 11):
                load_chunk(c)
            for g in range(NM // 4):
                dt, quad = divmod(g, 4)
                sp.wait_ge(hi_ready, M0 + 4 * g + 4)
                sp.wait_ge(lo_ready, M0 + 4 * g + 4)
                for b in range(BATCH):
                    sp.dma_start(m_dram[b, :, dt, :, quad * 4 * KEYS:(quad + 1) * 4 * KEYS],
                                 m_stage[:, g % 2, b]).then_inc(m_stored[g % 2], 16)
            for n in range(NU):
                b, h = divmod(n, HEADS)
                sp.wait_ge(hi_ready, U0 + n + 1)
                sp.wait_ge(lo_ready, U0 + n + 1)
                sp.dma_start(u_dram[b, h * KEYS:(h + 1) * KEYS], u_stage[:, n % US]).then_inc(u_stored[n % US], 16)
                if n % 12 == 0 and n // 12 < 4:
                    sp.wait_ge(w_lo_ready, n // 12 + 1)
                    load_chunk(12 + n // 12)
            for s in range(US):
                sp.wait_ge(u_stored[s], 16 * NU // US)
            sp.wait_ge(table_clear, 16)

        @block.tensor
        def _(pe):
            def bank(n):
                if n >= NB:
                    pe.wait_ge(hi_ready, n - NB + 1)
                    pe.wait_ge(lo_ready, n - NB + 1)
                return banks[n % NB]

            pe.wait_ge(ctx_in, 16)
            for t in range(DT):
                out = bank(t)
                for b in range(BATCH):
                    last = pe.transpose(out[:, b * KEYS:(b + 1) * KEYS], ctx_sb[:, b, t * P:(t + 1) * P],
                                        ident[0:KEYS, 0:KEYS])
                last.then_inc(product_ready, 1)
            pe.wait_ge(hi_ready, DT)
            pe.wait_ge(lo_ready, DT)
            for m in range(2 * PAIRS):
                out = bank(KV0 + m)
                c, at = divmod(m * P, D)
                pe.wait_ge(chunk_hi_ready, c + 1)
                pe.wait_ge(chunk_lo_ready, c + 1)
                for t in range(DT):
                    for wp, cp in PRODUCTS:
                        last = pe.matmul(out[:, 0:CK], kvw_parts[:, c, wp, t, at:at + P], ctxT[:, cp, t, :],
                                         start=(t == 0 and (wp, cp) == PRODUCTS[0]),
                                         stop=(t == DT - 1 and (wp, cp) == PRODUCTS[-1]))
                last.then_inc(product_ready, 1)
            for m in range(PAIRS):
                out = bank(WQ0 + m)
                c, at = divmod(m * P, D)
                raw_wait(pe, WQ_CHUNK + c)
                for t in range(DT):
                    last = pe.transpose(out[:, t * P:(t + 1) * P], raw[:, (WQ_CHUNK + c) % RAW, t, at:at + P], ident[:])
                last.then_inc(product_ready, 1)
            pe.wait_ge(hi_ready, M0)
            pe.wait_ge(lo_ready, M0)
            for n in range(NM):
                dt, h = divmod(n, HEADS)
                half = slice(DH * (h % 2), DH * (h % 2) + DH)
                out = bank(M0 + n)
                for qp, kp in PRODUCTS:
                    last = pe.matmul(out[:, 0:CK], wqT[half, qp, h // 2, dt * P:(dt + 1) * P], kvT[half, kp, h // 2, :],
                                     start=((qp, kp) == PRODUCTS[0]), stop=((qp, kp) == PRODUCTS[-1]))
                last.then_inc(product_ready, 1)
            pe.wait_ge(chunk_hi_ready, 6)
            pe.wait_ge(chunk_lo_ready, 6)
            pe.wait_ge(ones_ready, 1)
            pe.wait_ge(bias_lo_ready, 1)
            for n in range(NU):
                b, h = divmod(n, HEADS)
                half = slice(DH * (h % 2), DH * (h % 2) + DH)
                out = bank(U0 + n)
                c, at = divmod(h // 2, DT)
                if h == 0:
                    for part in range(2):
                        pe.matmul(out[0:KEYS, :], ones_row[:], bias_parts[:, part], start=(part == 0), stop=False)
                for vp, wp in PRODUCTS:
                    last = pe.matmul(out[0:KEYS, :], kvT[half, vp, PAIRS + h // 2, b * KEYS:(b + 1) * KEYS],
                                     kvw_parts[half, c, wp, at, :],
                                     start=(h > 0 and (vp, wp) == PRODUCTS[0]), stop=((vp, wp) == PRODUCTS[-1]))
                last.then_inc(product_ready, 1)

        ORDER = ([("job", n) for n in range(KV0)] + [("chunk", 0), ("chunk", 1)]
                 + [("job", n) for n in range(KV0, KV0 + 4)] + [("chunk", 2)]
                 + [("job", n) for n in range(KV0 + 4, KV0 + 8)] + [("chunk", 3)]
                 + [("job", n) for n in range(KV0 + 8, M0)] + [("chunk", 4), ("chunk", 5)]
                 + [("job", n) for n in range(M0, U0 + NU)])

        @block.scalar
        def _(act):
            act.wait_ge(small_in, 48)
            act.activation(tanhs[:], gates[:], ACT.Tanh).then_inc(tanh_ready, 1)
            act.mul(bias_parts[:, 0], bias[:], W16).then_inc(bias_hi_ready, 1)
            for what, n in ORDER:
                if what == "chunk":
                    c = n if n < 4 else n + WOUT_CHUNK - 4
                    raw_wait(act, c)
                    if n >= 4:
                        act.wait_ge(product_ready, WQ0)
                    act.mul(kvw_parts[:, n % 4, 0], raw[:, c % RAW], W16).then_inc(chunk_hi_ready, 1)
                    continue
                if n == U0:
                    act.wait_ge(gain_ready, 1)
                stage_free(act, n)
                act.wait_ge(product_ready, n + 1)
                hi, lo, sums, scale = job(n)
                act.activation(hi, sums, ACT.Copy, scale=scale).then_inc(hi_ready, 1)

        @block.vector
        def _(dve):
            dve.memset(ones_row[:], C_SCALE).then_inc(ones_ready, 1)
            dve.wait_ge(tanh_ready, 1)
            dve.scalar_tensor_tensor(u_gain[:], tanhs[:, 0:1], U_SCALE / (K_SCALE * W16), tanhs[:, 1:2], ALU.mult,
                                     ALU.mult).then_inc(gain_ready, 1)
            dve.wait_ge(bias_hi_ready, 1)
            dve.scalar_tensor_tensor(bias_parts[:, 1], bias[:], W16, bias_parts[:, 0], ALU.mult,
                                     ALU.subtract).then_inc(bias_lo_ready, 1)
            for what, n in ORDER:
                if what == "chunk":
                    c = n if n < 4 else n + WOUT_CHUNK - 4
                    dve.wait_ge(chunk_hi_ready, n + 1)
                    dve.scalar_tensor_tensor(kvw_parts[:, n % 4, 1].rearrange("p t n -> p (t n)"),
                                             raw[:, c % RAW].rearrange("p t n -> p (t n)"), W16,
                                             kvw_parts[:, n % 4, 0].rearrange("p t n -> p (t n)"), ALU.mult,
                                             ALU.subtract).then_inc(chunk_lo_ready, 1)
                    continue
                if n == U0:
                    dve.wait_ge(gain_ready, 1)
                dve.wait_ge(hi_ready, n + 1)
                hi, lo, sums, scale = job(n)
                dve.scalar_tensor_tensor(lo, sums, scale, hi, ALU.mult, ALU.subtract).then_inc(lo_ready, 1)

        @block.gpsimd
        def _(pool):
            pool.memset(fill[:], 0.0).then_inc(fill_zero, 1)
            pool.wait_ge(fill_zero, 1)
            pool.memset(fill[:, :, 0:1], NO_TOKEN).then_inc(fill_ready, 1)
            for e in range(EXPERTS):
                c = EXPERT_CHUNK + e
                raw_wait(pool, c)
                pool.tensor_scalar(raw[:, c % RAW], raw[:, c % RAW], W_SCALE, None, ALU.mult).then_inc(w_scaled, 1)
                pool.wait_ge(w_scaled, e + 1)
                pool.tensor_copy(w_parts[:, e, :, 0, :], raw[:, c % RAW]).then_inc(w_hi_ready, 1)
                pool.wait_ge(w_hi_ready, e + 1)
                pool.tensor_tensor(w_parts[:, e, :, 1, :], raw[:, c % RAW], w_parts[:, e, :, 0, :],
                                   ALU.subtract).then_inc(w_lo_ready, 1)


def attend(nc, ident16, x_in, ln_gamma, ln_beta, m_dram, u_dram, x_mid, x_final, gate_w, gate_b, g_ffn,
           table, placed, ones16):
    with ExitStack() as stack:
        def sb(name, shape, dt=F32):
            return stack.enter_context(nc.sbuf_tensor(name, shape, dt))

        def psum(name, shape, dt=F32):
            return stack.enter_context(nc.psum_tensor(name, shape, dt))

        def sem(name):
            return stack.enter_context(nc.semaphore(name))

        m_sb = sb("m_sb", [P, DT, 2, COLS], F16)
        u_sb = sb("u_sb", [P, KT, 2, D], F16)
        gamma = sb("gamma", [P, D])
        beta = sb("beta", [P, D])
        x_ln = sb("x_ln", [P, 2, D])
        x_res = sb("x_res", [P, 2, D])
        stats = sb("stats", [P, 2, 6])
        moments = sb("moments", [P, 2, 2])
        spread = sb("spread", [P, 2, 1])
        rstd = sb("rstd", [P, 2, 1])
        minus_half = sb("minus_half", [P, 1])
        z = sb("z", [P, 2, D])
        z_parts = sb("z_parts", [P, 2, 2, D], F16)
        zT = sb("zT", [P, 2, 2, DT, P], F16)
        top = sb("top", [P, 2, HEADS])
        expd = sb("expd", [P, 2, COLS])
        total = sb("total", [P, 2, HEADS])
        inverse = sb("inverse", [P, 2, HEADS])
        p_parts = sb("p_parts", [P, 2, COLS], F16)
        pT = sb("pT", [P, KT, 2, P], F16)
        x_out = sb("x_out", [P, 2, D])
        x_stats = sb("x_stats", [P, 2, 6])
        x_moments = sb("x_moments", [P, 2, 2])
        x_spread = sb("x_spread", [P, 2, 1])
        y = sb("y", [P, 2, D])
        y_parts = sb("y_parts", [P, 2, 2, D], F16)
        yT = sb("yT", [P, 2, DT, P], F16)
        gate_raw = sb("gate_raw", [P, DT, GATES])
        gate_scaled = sb("gate_scaled", [P, DT, GATES])
        gate_parts = sb("gate_parts", [P, DT, 2, GATES], F16)
        gate_bias = sb("gate_bias", [P, GATES])
        logits = sb("logits", [P, 2, GATES])
        largest = sb("largest", [P, 2, 8])
        found = sb("found", [P, 2, 8], U32)
        expert = sb("expert", [P, 2, TOP_K])
        gap = sb("gap", [P, 2, TOP_K])
        ratio = sb("ratio", [P, 2, TOP_K])
        norms = sb("norms", [P, 2, 2])
        onehot = sb("onehot", [P, 2, TOP_K, EXPERTS], F16)
        iota_e = sb("iota_e", [P, TOP_K, EXPERTS])
        region = sb("region", [P, TOP_K, EXPERTS])
        iota_t = sb("iota_t", [P, TILES])
        below = sb("below", [P, P], F16)
        g_raw = sb("g_raw", [P, 1])
        g_tanh = sb("g_tanh", [P, 1])
        place = sb("place", [P, TOP_K, EXPERTS])
        mine = sb("mine", [P, TOP_K, EXPERTS])
        row = sb("row", [P, TOP_K])
        no_row = sb("no_row", [P, TOP_K])
        row_f = sb("row_f", [P, TOP_K])
        row_whole = sb("row_whole", [P, TOP_K], I32)
        tile_whole = sb("tile_whole", [P, TOP_K], I32)
        tile_f = sb("tile_f", [P, TOP_K])
        part_f = sb("part_f", [P, TOP_K])
        row_i = sb("row_i", [P, 2, TOP_K], I32)
        kept = sb("kept", [P, TOP_K])
        kept_sum = sb("kept_sum", [P, 1])
        kept_div = sb("kept_div", [P, 1])
        kept_inv = sb("kept_inv", [P, 1])
        payload = sb("payload", [P, 2, TOP_K, 4])

        scores = [psum(f"scores{k}", [P, 512]) for k in range(3)]
        pT_bank = [psum(f"pT_bank{k}", [P, 4, 2, P], F16) for k in range(3)]
        gate_bank = pT_bank[2][:, 2:4].rearrange("p a b c -> p (a b c)").bitcast(F32)[:, 0:GATES]
        rank_bank = pT_bank[2][:, 2:4].rearrange("p a b c -> p (a b c)").bitcast(F32)[:, 16:16 + TOP_K * EXPERTS]
        zT_bank = psum("zT_bank", [P, 2, DT, P], F16)
        mix = psum("mix", [P, D])

        affine_in = sem("affine_in")
        m_in = sem("m_in")
        u_in = sem("u_in")
        x_ln_in = [sem(f"x_ln_in{s}") for s in range(2)]
        x_res_in = [sem(f"x_res_in{s}") for s in range(2)]
        stored = [sem(f"stored{s}") for s in range(2)]
        const_ready = sem("const_ready")
        stats_ready = sem("stats_ready")
        moments_ready = sem("moments_ready")
        spread_ready = sem("spread_ready")
        rstd_ready = sem("rstd_ready")
        z_ready = sem("z_ready")
        scaled_ready = sem("scaled_ready")
        shifted_ready = sem("shifted_ready")
        z_hi_ready = sem("z_hi_ready")
        z_lo_ready = sem("z_lo_ready")
        zT_summed = sem("zT_summed")
        zT_ready = sem("zT_ready")
        scores_ready = sem("scores_ready")
        top_ready = sem("top_ready")
        less_ready = sem("less_ready")
        exp_ready = sem("exp_ready")
        pT_summed = sem("pT_summed")
        pT_ready = sem("pT_ready")
        total_ready = sem("total_ready")
        inverse_ready = sem("inverse_ready")
        p_ready = sem("p_ready")
        p_hi_ready = sem("p_hi_ready")
        p_lo_ready = sem("p_lo_ready")
        mix_ready = sem("mix_ready")
        x_out_ready = sem("x_out_ready")

        gate_in = sem("gate_in")
        gate_scaled_ready = sem("gate_scaled_ready")
        gate_hi_ready = sem("gate_hi_ready")
        gate_lo_ready = sem("gate_lo_ready")
        x_stats_ready = sem("x_stats_ready")
        x_moments_ready = sem("x_moments_ready")
        x_spread_ready = sem("x_spread_ready")
        x_rstd_ready = sem("x_rstd_ready")
        y_ready = sem("y_ready")
        y_hi_ready = sem("y_hi_ready")
        y_lo_ready = sem("y_lo_ready")
        yT_summed = sem("yT_summed")
        yT_ready = sem("yT_ready")
        gate_summed = sem("gate_summed")
        logits_ready = sem("logits_ready")
        largest_ready = sem("largest_ready")
        choice_ready = sem("choice_ready")
        expert_ready = sem("expert_ready")
        gap_ready = sem("gap_ready")
        ratio_ready = sem("ratio_ready")
        norms_ready = sem("norms_ready")
        onehot_ready = sem("onehot_ready")
        g_in = sem("g_in")
        g_ready = sem("g_ready")
        iota_ready = sem("iota_ready")
        rank_summed = sem("rank_summed")
        place_ready = sem("place_ready")
        placing = sem("placing")
        row_i_ready = sem("row_i_ready")
        weight_ready = sem("weight_ready")
        payload_ready = sem("payload_ready")
        placed_ready = sem("placed_ready")
        scattered = [sem(f"scattered{s}") for s in range(2)]

        PLACING = 12

        def live(i):
            return not isinstance(i, int) or 0 <= i < TILES

        def later(i, n):
            return not isinstance(i, int) or i >= n

        def run(engine, step):
            first, last = 6, TILES - 2
            for i in range(first):
                step(i, i % 2)
            with engine.Fori(0, (last - first) // 2) as r:
                for k in range(2):
                    step(2 * r + first + k, k)
            for i in range(last, TILES + 7):
                step(i, i % 2)

        def rows(tensor, i):
            return tensor[bass.ds(i * P, P), :]

        block = stack.enter_context(nc.Block())

        @block.sync
        def _(sp):
            def load_x_ln(i, s):
                sp.dma_start(x_ln[:, s, :], rows(x_in, i)).then_inc(x_ln_in[s], 16)

            def load_x_res(i, s):
                sp.dma_start(x_res[:, s, :], rows(x_in, i)).then_inc(x_res_in[s], 16)

            def load_m(b):
                sp.dma_start(m_sb[:], m_dram[bass.ds(b, 1)].rearrange("a p t l c -> (a p) t l c")).then_inc(m_in, 16)

            def load_u(b):
                u = u_dram[bass.ds(b, 1)].rearrange("a r l n -> (a r) l n")
                sp.dma_start(u_sb[:, 0:KT - 1], u[0:(KT - 1) * P].rearrange("(k p) l n -> p k l n", p=P)).then_inc(u_in, 16)
                sp.dma_start(u_sb[0:LAST, KT - 1], u[(KT - 1) * P:COLS]).then_inc(u_in, 16)

            def store(i, s):
                sp.dma_start(rows(x_mid, i), x_out[:, s, :]).then_inc(stored[s], 16)
                sp.dma_start(rows(x_final, i), x_out[:, s, :]).then_inc(stored[s], 16)

            def step(i, s, more=True, before=True):
                if more:
                    sp.wait_ge(z_ready, i + 1)
                    load_x_ln(i + 2, s)
                if before:
                    sp.wait_ge(x_out_ready, i - 1)
                    store(i - 2, s)
                load_x_res(i, s)

            sp.dma_start(gamma[:], ln_gamma.rearrange("(a d) -> a d", a=1).broadcast_to([P, D])).then_inc(affine_in, 16)
            sp.dma_start(beta[:], ln_beta.rearrange("(a d) -> a d", a=1).broadcast_to([P, D])).then_inc(affine_in, 16)
            load_x_ln(0, 0)
            load_x_ln(1, 1)
            sp.dma_start(gate_bias[:], gate_b.rearrange("(a e) -> a e", a=1).broadcast_to([P, GATES])).then_inc(gate_in, 16)
            sp.dma_start(g_raw[:], g_ffn.rearrange("(a b) -> a b", a=1).broadcast_to([P, 1])).then_inc(g_in, 16)
            for t in range(DT):
                sp.dma_start(gate_raw[:, t, :], gate_w[:, t * P:(t + 1) * P].rearrange("e p -> p e"),
                             allow_slow_non_contiguous=True).then_inc(gate_in, 16)
            load_m(0)
            load_u(0)

            def batch(b, first=False, last=False):
                i0 = b * TPB
                step(i0, 0, before=not first)
                if not first:
                    sp.wait_ge(mix_ready, i0)
                    load_u(b)
                step(i0 + 1, 1, before=not first)
                with sp.Fori(0, TPB // 2 - 2) as q:
                    for k in range(2):
                        step(i0 + 2 * q + 2 + k, k)
                for k in range(2):
                    step(i0 + TPB - 2 + k, k, more=not last)
                if not last:
                    sp.wait_ge(scores_ready, 3 * (i0 + TPB))
                    load_m(b + 1)

            batch(0, first=True)
            with sp.Fori(1, BATCH - 1) as b:
                batch(b)
            batch(BATCH - 1, last=True)
            for i in range(TILES - 2, TILES):
                sp.wait_ge(x_out_ready, i + 1)
                store(i, i % 2)
            for s in range(2):
                sp.wait_ge(stored[s], 32 * TILES // 2)

        @block.tensor
        def _(pe):
            def transpose_z(i, s):
                pe.wait_ge(z_hi_ready, i + 1)
                pe.wait_ge(z_lo_ready, i + 1)
                pe.wait_ge(zT_ready, i)
                if later(i, 4):
                    pe.wait_ge(yT_ready, i - 3)
                for part in range(2):
                    for t in range(DT):
                        last = pe.transpose(zT_bank[:, part, t, :], z_parts[:, s, part, t * P:(t + 1) * P], ident16[:])
                last.then_inc(zT_summed, 1)

            def score(i, s):
                pe.wait_ge(zT_ready, i + 1)
                pe.wait_ge(m_in, 16 * (i // TPB) + 16)
                for k in range(3):
                    if later(i, 1):
                        pe.wait_ge(less_ready, 3 * (i - 1) + k + 1)
                    n, c0 = BANK_HEADS[k] * KEYS, HEAD0[k] * KEYS
                    for t in range(DT):
                        for zp, mp in PRODUCTS:
                            last = pe.matmul(scores[k][:, 0:n], zT[:, s, zp, t, :], m_sb[:, t, mp, c0:c0 + n],
                                             start=(t == 0 and (zp, mp) == PRODUCTS[0]),
                                             stop=(t == DT - 1 and (zp, mp) == PRODUCTS[-1]))
                    last.then_inc(scores_ready, 1)

            def transpose_p(i):
                pe.wait_ge(p_hi_ready, i + 1)
                pe.wait_ge(p_lo_ready, i + 1)
                for g, (k0, k1) in enumerate(PT_GROUPS):
                    if later(i, 1):
                        pe.wait_ge(pT_ready, 3 * i + g - 2)
                    if g == 2 and later(i, 3):
                        pe.wait_ge(logits_ready, i - 2)
                    if g == 2 and later(i, 5):
                        pe.wait_ge(place_ready, i - 4)
                    for k in range(k0, k1):
                        n = P if k < KT - 1 else LAST
                        for part in range(2):
                            last = pe.transpose(pT_bank[g][0:n, k - k0, part, :], p_parts[:, part, k * P:k * P + n],
                                                ident16[:])
                    last.then_inc(pT_summed, 1)

            def mix_values(i):
                pe.wait_ge(u_in, 32 * (i // TPB) + 32)
                pe.wait_ge(x_out_ready, i)
                for g, (k0, k1) in enumerate(PT_GROUPS):
                    pe.wait_ge(pT_ready, 3 * i + g + 1)
                    for k in range(k0, k1):
                        n = P if k < KT - 1 else LAST
                        for pp, up in PRODUCTS:
                            last = pe.matmul(mix[:], pT[0:n, k, pp, :], u_sb[0:n, k, up, :],
                                             start=(k == 0 and (pp, up) == PRODUCTS[0]),
                                             stop=(k == KT - 1 and (pp, up) == PRODUCTS[-1]))
                last.then_inc(mix_ready, 1)

            def transpose_y(i, s):
                pe.wait_ge(y_hi_ready, i + 1)
                pe.wait_ge(y_lo_ready, i + 1)
                pe.wait_ge(zT_ready, i + 4 if not isinstance(i, int) or i + 4 <= TILES else TILES)
                for part in range(2):
                    for t in range(DT):
                        last = pe.transpose(zT_bank[:, part, t, :], y_parts[:, s, part, t * P:(t + 1) * P], ident16[:])
                last.then_inc(yT_summed, 1)

            def gate(i):
                pe.wait_ge(yT_ready, i + 1)
                if isinstance(i, int) and i == 0:
                    pe.wait_ge(gate_lo_ready, 1)
                pe.wait_ge(logits_ready, i)
                if later(i, 3):
                    pe.wait_ge(place_ready, i - 2)
                pe.wait_ge(pT_ready, 3 * (i + 3) if not isinstance(i, int) or i + 3 <= TILES else 3 * TILES)
                for t in range(DT):
                    for yp, gp in PRODUCTS:
                        last = pe.matmul(gate_bank, yT[:, yp, t, :], gate_parts[:, t, gp, :],
                                         start=(t == 0 and (yp, gp) == PRODUCTS[0]),
                                         stop=(t == DT - 1 and (yp, gp) == PRODUCTS[-1]))
                last.then_inc(gate_summed, 1)

            def rank(i, s):
                pe.wait_ge(onehot_ready, i + 1)
                pe.wait_ge(placed_ready, i + 1)
                pe.wait_ge(place_ready, i)
                pe.wait_ge(logits_ready, i + 2 if not isinstance(i, int) or i + 2 <= TILES else TILES)
                pe.wait_ge(pT_ready, 3 * (i + 5) if not isinstance(i, int) or i + 5 <= TILES else 3 * TILES)
                hot = onehot[:, s].rearrange("p k e -> p (k e)")
                pe.matmul(rank_bank, below[:], hot, start=True, stop=False)
                pe.matmul(rank_bank, ones16[:], placed[:, 1 - s], start=False, stop=True).then_inc(rank_summed, 1)

            def step(i, s):
                if live(i):
                    score(i, s)
                if live(i - 1):
                    transpose_p(i - 1)
                if live(i + 1):
                    transpose_z(i + 1, 1 - s)
                if live(i - 1):
                    mix_values(i - 1)
                if live(i - 5):
                    rank(i - 5, 1 - s)
                if live(i - 3):
                    gate(i - 3)
                if live(i - 2):
                    transpose_y(i - 2, s)

            transpose_z(0, 0)
            run(pe, step)

        @block.scalar
        def _(act):
            def split_z(i, s):
                act.wait_ge(shifted_ready, i + 1)
                if not isinstance(i, int) or i >= 2:
                    act.wait_ge(zT_summed, i - 1)
                act.copy(z_parts[:, s, 0, :], z[:, s, :]).then_inc(z_hi_ready, 1)

            def copy_zT(i, s):
                act.wait_ge(zT_summed, i + 1)
                if not isinstance(i, int) or i >= 2:
                    act.wait_ge(scores_ready, 3 * (i - 1))
                act.copy(zT[:, s], zT_bank[:]).then_inc(zT_ready, 1)

            def exponent(i, s, k):
                n, c0 = BANK_HEADS[k] * KEYS, HEAD0[k] * KEYS
                act.wait_ge(less_ready, 3 * i + k + 1)
                act.activation(expd[:, s, c0:c0 + n], expd[:, s, c0:c0 + n], ACT.Exp,
                               scale=1.0 / M_SCALE).then_inc(exp_ready, 1)

            def split_p(i, s):
                act.wait_ge(p_ready, i + 1)
                act.wait_ge(pT_summed, 3 * i)
                act.copy(p_parts[:, 0, :], expd[:, s, :]).then_inc(p_hi_ready, 1)

            def copy_pT(i, g):
                k0, k1 = PT_GROUPS[g]
                act.wait_ge(pT_summed, 3 * i + g + 1)
                act.wait_ge(mix_ready, i)
                if k1 < KT:
                    act.copy(pT[:, k0:k1], pT_bank[g][:, 0:k1 - k0]).then_inc(pT_ready, 1)
                else:
                    act.copy(pT[:, k0:k1 - 1], pT_bank[g][:, 0:k1 - k0 - 1])
                    act.copy(pT[0:LAST, k1 - 1], pT_bank[g][0:LAST, k1 - k0 - 1]).then_inc(pT_ready, 1)

            def split_y(i, s):
                act.wait_ge(y_ready, i + 1)
                if later(i, 2):
                    act.wait_ge(yT_summed, i - 1)
                act.copy(y_parts[:, s, 0, :], y[:, s, :]).then_inc(y_hi_ready, 1)

            def copy_yT(i):
                act.wait_ge(yT_summed, i + 1)
                act.wait_ge(gate_summed, i)
                act.copy(yT[:], zT_bank[:]).then_inc(yT_ready, 1)

            def exponent_gap(i, s):
                act.wait_ge(gap_ready, i + 1)
                act.activation(ratio[:, s], gap[:, s], ACT.Exp).then_inc(ratio_ready, 1)

            def step(i, s):
                if live(i - 3):
                    copy_yT(i - 3)
                if live(i):
                    exponent(i, s, 0)
                if live(i - 2):
                    split_y(i - 2, s)
                if live(i):
                    exponent(i, s, 1)
                if live(i - 1):
                    copy_pT(i - 1, 0)
                if live(i):
                    exponent(i, s, 2)
                if live(i - 1):
                    copy_pT(i - 1, 1)
                    copy_pT(i - 1, 2)
                if live(i + 1):
                    copy_zT(i + 1, 1 - s)
                if live(i + 2):
                    split_z(i + 2, s)
                if live(i):
                    split_p(i, s)
                if live(i - 4):
                    exponent_gap(i - 4, s)

            act.wait_ge(g_in, 16)
            act.activation(g_tanh[:], g_raw[:], ACT.Tanh).then_inc(g_ready, 1)
            split_z(0, 0)
            copy_zT(0, 0)
            split_z(1, 1)
            run(act, step)

        @block.vector
        def _(dve):
            def moments_of(i, s):
                dve.wait_ge(x_ln_in[s], 8 * (i - s) + 16)
                dve.bn_stats(stats[:, s], x_ln[:, s, :]).then_inc(stats_ready, 1)

            def spread_of(i, s):
                dve.bn_aggr(moments[:, s], stats[:, s]).then_inc(moments_ready, 1)
                dve.wait_ge(moments_ready, i + 1)
                dve.tensor_scalar(spread[:, s], moments[:, s, 1:2], 1.0 + EPS, EPS * EPS, ALU.mult,
                                  ALU.add).then_inc(spread_ready, 1)

            def normalize(i, s):
                dve.wait_ge(rstd_ready, i + 1)
                if not isinstance(i, int) or i >= 2:
                    dve.wait_ge(z_lo_ready, i - 1)
                dve.tensor_scalar(z[:, s, :], x_ln[:, s, :], moments[:, s, 0:1], rstd[:, s], ALU.subtract,
                                  ALU.mult).then_inc(z_ready, 1)

            def less_top(i, s, k):
                h0, nh = HEAD0[k], BANK_HEADS[k]
                c0, n = h0 * KEYS, nh * KEYS
                bank = scores[k][:, 0:n].rearrange("p (h j) -> p h j", h=nh)
                dve.wait_ge(scores_ready, 3 * i + k + 1)
                dve.tensor_reduce(top[:, s, h0:h0 + nh], bank, AX_X, ALU.max).then_inc(top_ready, 1)
                dve.wait_ge(top_ready, 3 * i + k + 1)
                dve.tensor_tensor(expd[:, s, c0:c0 + n].rearrange("p (h j) -> p h j", h=nh), bank,
                                  top[:, s, h0:h0 + nh].unsqueeze(2).broadcast_to([P, nh, KEYS]),
                                  ALU.subtract).then_inc(less_ready, 1)

            def probabilities(i, s):
                e = expd[:, s, :].rearrange("p (h j) -> p h j", h=HEADS)
                dve.wait_ge(exp_ready, 3 * i + 3)
                dve.tensor_reduce(total[:, s], e, AX_X, ALU.add).then_inc(total_ready, 1)
                dve.wait_ge(total_ready, i + 1)
                dve.reciprocal(inverse[:, s], total[:, s]).then_inc(inverse_ready, 1)
                dve.wait_ge(inverse_ready, i + 1)
                dve.scalar_tensor_tensor(e, e, P_SCALE, inverse[:, s].unsqueeze(2).broadcast_to([P, HEADS, KEYS]),
                                         ALU.mult, ALU.mult).then_inc(p_ready, 1)

            def low_p(i, s):
                dve.wait_ge(p_hi_ready, i + 1)
                dve.tensor_tensor(p_parts[:, 1, :], expd[:, s, :], p_parts[:, 0, :], ALU.subtract).then_inc(p_lo_ready, 1)

            def residual(i, s):
                dve.wait_ge(mix_ready, i + 1)
                dve.wait_ge(x_res_in[s], 8 * (i - s) + 16)
                if not isinstance(i, int) or i >= 2:
                    dve.wait_ge(stored[s], 16 * (i - s))
                dve.scalar_tensor_tensor(x_out[:, s, :], mix[:], 1.0 / (P_SCALE * U_SCALE), x_res[:, s, :], ALU.mult,
                                         ALU.add).then_inc(x_out_ready, 1)

            def y_moments_of(i, s):
                dve.wait_ge(x_out_ready, i + 1)
                dve.bn_stats(x_stats[:, s], x_out[:, s, :]).then_inc(x_stats_ready, 1)

            def y_spread_of(i, s):
                dve.bn_aggr(x_moments[:, s], x_stats[:, s]).then_inc(x_moments_ready, 1)
                dve.wait_ge(x_moments_ready, i + 1)
                dve.tensor_scalar(x_spread[:, s], x_moments[:, s, 1:2], EPS, None, ALU.add).then_inc(x_spread_ready, 1)

            def y_normalize(i, s):
                dve.wait_ge(x_rstd_ready, i + 1)
                if later(i, 2):
                    dve.wait_ge(y_lo_ready, i - 1)
                dve.tensor_scalar(y[:, s, :], x_out[:, s, :], x_moments[:, s, 0:1], x_moments[:, s, 1:2], ALU.subtract,
                                  ALU.mult).then_inc(y_ready, 1)

            def take_logits(i, s):
                dve.wait_ge(gate_summed, i + 1)
                dve.scalar_tensor_tensor(logits[:, s, :], gate_bank, 1.0 / G_SCALE, gate_bias[:], ALU.mult,
                                         ALU.add).then_inc(logits_ready, 1)
                if later(i, 2):
                    dve.wait_ge(payload_ready, 2 * i - 3)
                dve.tensor_copy(norms[:, s], x_moments[:, s]).then_inc(norms_ready, 1)

            def choose(i, s):
                dve.wait_ge(logits_ready, i + 1)
                dve.nop(nofuse=True)
                dve.max(largest[:, s, :], logits[:, s, :]).then_inc(largest_ready, 1)
                dve.wait_ge(largest_ready, i + 1)
                dve.nop(nofuse=True)
                dve.max_index(found[:, s, :], largest[:, s, :], logits[:, s, :]).then_inc(choice_ready, 1)
                dve.tensor_scalar(gap[:, s], largest[:, s, 0:TOP_K], largest[:, s, 0:1], None,
                                  ALU.subtract).then_inc(gap_ready, 1)
                dve.wait_ge(choice_ready, i + 1)
                dve.tensor_copy(expert[:, s], found[:, s, 0:TOP_K]).then_inc(expert_ready, 1)
                dve.wait_ge(expert_ready, i + 1)
                dve.tensor_tensor(onehot[:, s], iota_e[:], expert[:, s].unsqueeze(2).broadcast_to([P, TOP_K, EXPERTS]),
                                  ALU.is_equal).then_inc(onehot_ready, 1)

            def take_ranks(i, s):
                dve.wait_ge(rank_summed, i + 1)
                dve.wait_ge(gate_summed, i + 3 if not isinstance(i, int) or i + 3 <= TILES else TILES)
                dve.tensor_tensor(place[:].rearrange("p k e -> p (k e)"), rank_bank, region[:].rearrange("p k e -> p (k e)"),
                                  ALU.add).then_inc(place_ready, 1)
                if later(i, 2):
                    dve.wait_ge(scattered[s], 16 * (i - s))
                dve.wait_ge(norms_ready, i + 1)
                dve.tensor_copy(payload[:, s, :, 2:4], norms[:, s].unsqueeze(1).broadcast_to([P, TOP_K, 2])).then_inc(
                    payload_ready, 1)

            def place_rows(i, s):
                def start(instruction):
                    instruction.then_inc(placing, 1)

                def after(n):
                    dve.wait_ge(placing, PLACING * i + n)

                dve.wait_ge(ratio_ready, i + 1)
                start(dve.scalar_tensor_tensor(kept[:], expert[:, s], float(EXPERTS), ratio[:, s], ALU.is_lt,
                                               ALU.mult))
                dve.wait_ge(place_ready, i + 1)
                start(dve.tensor_tensor(mine[:], place[:], onehot[:, s], ALU.mult))
                start(dve.tensor_scalar(no_row[:], expert[:, s], float(EXPERTS), NO_ROW, ALU.is_ge,
                                        ALU.mult))
                after(1)
                start(dve.tensor_reduce(kept_sum[:], kept[:], AX_X, ALU.add))
                after(2)
                start(dve.tensor_reduce(row[:], mine[:], AX_X, ALU.add))
                after(4)
                start(dve.scalar_tensor_tensor(kept_div[:], kept_sum[:], 0.0, kept_sum[:], ALU.is_equal,
                                               ALU.add))
                after(5)
                start(dve.tensor_tensor(row_f[:], row[:], no_row[:], ALU.add))
                after(6)
                start(dve.reciprocal(kept_inv[:], kept_div[:]))
                after(7)
                start(dve.tensor_copy(row_whole[:], row_f[:]))
                dve.tensor_tensor(placed[:, s], placed[:, 1 - s], onehot[:, s].rearrange("p k e -> p (k e)"),
                                  ALU.add).then_inc(placed_ready, 1)
                after(9)
                start(dve.tensor_scalar(tile_whole[:], row_whole[:], 7, None, ALU.arith_shift_right))
                dve.tensor_scalar(payload[:, s, :, 1], kept[:], kept_inv[:], g_tanh[:], ALU.mult,
                                  ALU.mult).then_inc(weight_ready, 1)
                after(10)
                start(dve.tensor_copy(tile_f[:], tile_whole[:]))
                dve.tensor_copy(payload[:, s, :, 0], iota_t[:, bass.ds(i, 1)].broadcast_to([P, TOP_K])).then_inc(
                    payload_ready, 1)
                after(11)
                start(dve.scalar_tensor_tensor(part_f[:], tile_f[:], -float(P), row_f[:], ALU.mult,
                                               ALU.add))
                after(12)
                dve.scalar_tensor_tensor(row_i[:, s], part_f[:], float(TABLE_TILES), tile_f[:], ALU.mult,
                                         ALU.add).then_inc(row_i_ready, 1)

            def step(i, s):
                if live(i - 2):
                    residual(i - 2, s)
                    y_moments_of(i - 2, s)
                if live(i + 2):
                    moments_of(i + 2, s)
                if live(i - 6):
                    take_ranks(i - 6, s)
                if live(i - 4):
                    take_logits(i - 4, s)
                if live(i - 2):
                    dve.wait_ge(x_stats_ready, i - 1)
                if live(i + 2):
                    dve.wait_ge(stats_ready, i + 3)
                if live(i - 4):
                    dve.wait_ge(norms_ready, i - 3)
                dve.nop(nofuse=True)
                if live(i - 2):
                    y_spread_of(i - 2, s)
                if live(i + 2):
                    spread_of(i + 2, s)
                if live(i):
                    less_top(i, s, 0)
                if live(i - 2):
                    y_normalize(i - 2, s)
                if live(i + 2):
                    normalize(i + 2, s)
                if live(i):
                    less_top(i, s, 1)
                    less_top(i, s, 2)
                if live(i - 6):
                    place_rows(i - 6, s)
                if live(i - 4):
                    choose(i - 4, s)
                if live(i):
                    probabilities(i, s)
                    low_p(i, s)

            dve.memset(minus_half[:], -0.5).then_inc(const_ready, 1)
            dve.wait_ge(gate_in, 16 * (DT + 1))
            dve.tensor_scalar(gate_scaled[:], gate_raw[:], G_SCALE, None, ALU.mult).then_inc(gate_scaled_ready, 1)
            dve.wait_ge(gate_scaled_ready, 1)
            dve.tensor_copy(gate_parts[:, :, 0, :], gate_scaled[:]).then_inc(gate_hi_ready, 1)
            dve.wait_ge(gate_hi_ready, 1)
            dve.tensor_tensor(gate_parts[:, :, 1, :], gate_scaled[:], gate_parts[:, :, 0, :],
                              ALU.subtract).then_inc(gate_lo_ready, 1)
            dve.wait_ge(iota_ready, 4)
            dve.wait_ge(g_ready, 1)
            dve.memset(placed[:], 0.0).then_inc(placed_ready, 1)
            dve.wait_ge(placed_ready, 1)
            for i in range(2):
                moments_of(i, i)
                dve.wait_ge(stats_ready, i + 1)
                spread_of(i, i)
                normalize(i, i)
            run(dve, step)

        @block.gpsimd
        def _(pool):
            def layernorm(i, s):
                pool.wait_ge(spread_ready, i + 1)
                pool.tensor_tensor(rstd[:, s], spread[:, s], minus_half[:], ALU.pow).then_inc(rstd_ready, 1)
                pool.wait_ge(z_ready, i + 1)
                pool.tensor_tensor(z[:, s, :], z[:, s, :], gamma[:], ALU.mult).then_inc(scaled_ready, 1)
                pool.wait_ge(scaled_ready, i + 1)
                pool.tensor_tensor(z[:, s, :], z[:, s, :], beta[:], ALU.add).then_inc(shifted_ready, 1)

            def z_low(i, s):
                pool.wait_ge(z_hi_ready, i + 1)
                pool.tensor_tensor(z_parts[:, s, 1, :], z[:, s, :], z_parts[:, s, 0, :], ALU.subtract).then_inc(z_lo_ready, 1)

            def y_rstd(i, s):
                pool.wait_ge(x_spread_ready, i + 1)
                pool.tensor_tensor(x_moments[:, s, 1:2], x_spread[:, s], minus_half[:], ALU.pow).then_inc(x_rstd_ready, 1)

            def y_low(i, s):
                pool.wait_ge(y_hi_ready, i + 1)
                pool.tensor_tensor(y_parts[:, s, 1, :], y[:, s, :], y_parts[:, s, 0, :], ALU.subtract).then_inc(y_lo_ready, 1)

            def scatter(i, s):
                pool.wait_ge(row_i_ready, i + 1)
                pool.wait_ge(weight_ready, i + 1)
                pool.wait_ge(payload_ready, 2 * i + 2)
                pool.nop(nofuse=True)
                for k in range(TOP_K):
                    pool.indirect_dma_start(table, bass.IndirectOffsetOnAxis(ap=row_i[:, s, k:k + 1], axis=0),
                                            payload[:, s, k, :], None, bounds_check=TABLE_ROWS - 1,
                                            oob_is_err=False).then_inc(scattered[s], 16)

            def step(i, s):
                if live(i - 2):
                    y_rstd(i - 2, s)
                if live(i + 2):
                    layernorm(i + 2, s)
                if live(i - 2):
                    y_low(i - 2, s)
                if live(i + 2):
                    z_low(i + 2, s)
                if live(i - 6):
                    scatter(i - 6, s)

            for k in range(TOP_K):
                pool.iota(iota_e[:, k], pattern=[[1, EXPERTS]], base=0, channel_multiplier=0,
                          allow_small_or_imprecise_dtypes=True)
                last = pool.iota(region[:, k], pattern=[[REGION_ROWS, EXPERTS]], base=k * REGIONS * REGION_ROWS,
                                 channel_multiplier=0, allow_small_or_imprecise_dtypes=True)
            last.then_inc(iota_ready, 1)
            pool.iota(iota_t[:], pattern=[[P, TILES]], base=0, channel_multiplier=1,
                      allow_small_or_imprecise_dtypes=True).then_inc(iota_ready, 1)
            pool.memset(below[:], 1.0).then_inc(iota_ready, 1)
            pool.wait_ge(iota_ready, 3)
            pool.affine_select(out=below[:], in_=below[:], compare_op=ALU.is_gt, fill=0.0, base=0,
                               pattern=[[1, P]], channel_multiplier=-1).then_inc(iota_ready, 1)
            pool.wait_ge(const_ready, 1)
            pool.wait_ge(affine_in, 32)
            for i in range(2):
                layernorm(i, i)
                z_low(i, i)
            run(pool, step)
            for s in range(2):
                pool.wait_ge(scattered[s], 16 * TOP_K * TILES // 2)


def list_tiles(nc, ones16, placed, table, expert_b, expert_bias, tile_expert, inner_passes, slots):
    with ExitStack() as stack:
        def sb(name, shape, dt=F32):
            return stack.enter_context(nc.sbuf_tensor(name, shape, dt))

        def sem(name):
            return stack.enter_context(nc.semaphore(name))

        table_sb = sb("table_sb", [P, TABLE_TILES, 4])
        tokens = sb("tokens", [P, TOP_K, EXPERTS], I32)
        tiles_i = sb("tiles_i", [P, TOP_K, EXPERTS], I32)
        tiles_f = sb("tiles_f", [P, TOP_K, EXPERTS])
        ends = [sb(f"ends{n}", [P, TOP_K, EXPERTS]) for n in range(3)]
        starts = sb("starts", [P, TOP_K, LISTED + 4], I32)
        iota_j = sb("iota_j", [P, PASSES, LISTED, EXPERTS])
        iota_r = sb("iota_r", [P, TOP_K, PASSES])
        past = sb("past", [P, TOP_K, PASSES * LISTED, EXPERTS])
        owner = sb("owner", [P, TOP_K, PASSES * LISTED])
        begun = sb("begun", [P, TOP_K, PASSES])
        passes = sb("passes", [P, TOP_K])
        sums = stack.enter_context(nc.psum_tensor("sums", [P, TOP_K * EXPERTS], F32))
        bias_in = sem("bias_in")
        table_in = sem("table_in")
        summed = sem("summed")
        iotas = sem("iotas")
        done = sem("done")
        block = stack.enter_context(nc.Block())

        @block.sync
        def _(sp):
            sp.dma_start(table_sb[:], table.rearrange("(p t) w -> p t w", p=P)).then_inc(table_in, 16)
            sp.dma_start(expert_bias[:], expert_b.rearrange("(a e) d -> a e d", a=1).broadcast_to(
                [P, EXPERTS, D])).then_inc(bias_in, 16)
            sp.wait_ge(bias_in, 16)

        @block.tensor
        def _(pe):
            pe.matmul(sums[:], ones16[:], placed[:, (TILES - 1) % 2], start=True, stop=True).then_inc(summed, 1)

        @block.gpsimd
        def _(pool):
            pool.iota(iota_j[:], pattern=[[RING, PASSES], [1, LISTED], [0, EXPERTS]], base=0, channel_multiplier=0,
                      allow_small_or_imprecise_dtypes=True).then_inc(iotas, 1)
            pool.iota(iota_r[:], pattern=[[0, TOP_K], [RING, PASSES]], base=0, channel_multiplier=0,
                      allow_small_or_imprecise_dtypes=True).then_inc(iotas, 1)

        @block.vector
        def _(dve):
            count = [0]

            def after(instruction):
                instruction.then_inc(done, 1)
                count[0] += 1
                dve.wait_ge(done, count[0])

            dve.wait_ge(summed, 1)
            after(dve.tensor_scalar(tokens[:].rearrange("p k e -> p (k e)"), sums[:], float(P - 1), None, ALU.add))
            after(dve.tensor_scalar(tiles_i[:], tokens[:], 7, None, ALU.arith_shift_right))
            after(dve.tensor_copy(tiles_f[:], tiles_i[:]))
            last, n = tiles_f, 1
            for to in ends:
                after(dve.tensor_copy(to[:, :, 0:n], last[:, :, 0:n]))
                after(dve.tensor_tensor(to[:, :, n:], last[:, :, n:], last[:, :, 0:EXPERTS - n], ALU.add))
                last, n = to, 2 * n
            after(dve.tensor_tensor(starts[:, :, 0:EXPERTS], last[:], tiles_f[:], ALU.subtract))
            after(dve.tensor_copy(starts[:, :, EXPERTS:REGIONS], last[:, :, EXPERTS - 1:EXPERTS]))
            dve.wait_ge(iotas, 2)
            for k in range(TOP_K):
                end = last[:, k].unsqueeze(1).broadcast_to([P, PASSES * LISTED, EXPERTS])
                after(dve.tensor_tensor(past[:, k], iota_j[:].rearrange("p r s e -> p (r s) e"), end, ALU.is_ge))
            after(dve.tensor_reduce(owner[:], past[:], AX_X, ALU.add))
            after(dve.tensor_scalar(tile_expert[:].rearrange("p k r s -> p k (r s)"), owner[:], float(EXPERTS - 1), None,
                                    ALU.min))
            total = last[:, :, EXPERTS - 1:EXPERTS].broadcast_to([P, TOP_K, PASSES])
            after(dve.tensor_tensor(begun[:], iota_r[:], total, ALU.is_lt))
            after(dve.tensor_reduce(passes[:], begun[:], AX_X, ALU.add))
            after(dve.tensor_scalar(inner_passes[:], passes[:], 2.0, -2.0, ALU.max, ALU.add))
            dve.wait_ge(table_in, 16)
            for k in range(TOP_K):
                for e in range(REGIONS):
                    start = dve.value_load(starts[0:1, k, e:e + 1], min_val=0, max_val=SLOT_TILES)
                    t0 = (k * REGIONS + e) * SLOT_TILES
                    after(dve.tensor_copy(slots[:, k, bass.ds(start, SLOT_TILES), :], table_sb[:, t0:t0 + SLOT_TILES, :]))


def run_experts(nc, k, ident16, w_parts, tile_expert, inner_passes, slots, expert_bias, x_mid, x_sum, x_final):
    R = RING
    same = x_sum is x_mid
    with ExitStack() as stack:
        def sb(name, shape, dt=F32):
            return stack.enter_context(nc.sbuf_tensor(f"{name}_{k}", shape, dt))

        def sem(name):
            return stack.enter_context(nc.semaphore(f"{name}_{k}"))

        token = sb("token", [P, R, 1], I32)
        token_out = sb("token_out", [P, R, 1], I32)
        x_got = sb("x_got", [P, R, D])
        sum_got = x_got if same else sb("sum_got", [P, R, D])
        y = sb("y", [P, 2, D])
        y_parts = sb("y_parts", [P, 2, 2, D], F16)
        yT = sb("yT", [P, 2, 2, DT, P], F16)
        biased = sb("biased", [P, 2, D])
        result = sb("result", [P, R, D])
        yT_bank = [stack.enter_context(nc.psum_tensor(f"yT_bank{s}_{k}", [P, 2, DT, P], F16)) for s in range(2)]
        out_bank = [stack.enter_context(nc.psum_tensor(f"out_bank{s}_{k}", [P, D], F32)) for s in range(2)]

        cleared = sem("cleared")
        token_ready = sem("token_ready")
        got = [sem(f"got{s}") for s in range(R)]
        y_ready = sem("y_ready")
        y_hi_ready = sem("y_hi_ready")
        y_lo_ready = sem("y_lo_ready")
        yT_summed = sem("yT_summed")
        yT_ready = sem("yT_ready")
        expert_summed = sem("expert_summed")
        biased_ready = sem("biased_ready")
        token_out_ready = sem("token_out_ready")
        result_ready = sem("result_ready")
        put = [sem(f"put{s}") for s in range(R)]
        GATHERS = 16 if same else 32

        def at(r, s, n):
            q, place = divmod(s + n, R)
            return r + q, place, R * r + s + n

        def later(j, n):
            return not isinstance(j, int) or j >= n

        def experts(engine, r):
            row = tile_expert[0:1, k, bass.ds(r, 1), 0:R].rearrange("p a s -> p (a s)")
            return nc.values_load_multi_w_load_instructions(row, (engine.engine,), min_val=0, max_val=EXPERTS - 1,
                                                            skip_runtime_bounds_check_because="list_tiles clamps it")[1]

        def run(engine, step, lead, lag):
            last = engine.value_load(inner_passes[0:1, k:k + 1], min_val=0, max_val=PASSES - 2) + 1
            pass_experts = experts(engine, 0)
            for s in range(-lead, R):
                step(0, s, lambda n: s + n >= 0, pass_experts)
            with engine.Fori(1, PASSES - 1) as r:
                with engine.If(r < last):
                    pass_experts = experts(engine, r)
                    for s in range(R):
                        step(r, s, lambda n: True, pass_experts)
            pass_experts = experts(engine, last)
            for s in range(R + lag):
                step(last, s, lambda n: s + n < R, pass_experts)
            return last

        block = stack.enter_context(nc.Block())

        @block.gpsimd
        def _(pool):
            def gather(r, s, j):
                pool.wait_ge(token_ready, j + 1)
                if later(j, R):
                    pool.wait_ge(result_ready, j - R + 1)
                pool.nop(nofuse=True)
                rows = bass.IndirectOffsetOnAxis(ap=token[:, s, :], axis=0)
                pool.indirect_dma_start(x_got[:, s, :], None, x_mid, rows, bounds_check=TOKENS - 1,
                                        oob_is_err=False).then_inc(got[s], 16)
                if not same:
                    pool.indirect_dma_start(sum_got[:, s, :], None, x_sum, rows, bounds_check=TOKENS - 1,
                                            oob_is_err=False).then_inc(got[s], 16)

            def scatter(r, s, j):
                pool.wait_ge(token_out_ready, j + 1)
                pool.wait_ge(result_ready, j + 1)
                pool.nop(nofuse=True)
                pool.indirect_dma_start(x_final, bass.IndirectOffsetOnAxis(ap=token_out[:, s, :], axis=0),
                                        result[:, s, :], None, bounds_check=TOKENS - 1,
                                        oob_is_err=False).then_inc(put[s], 16)

            def step(r, s, live, _):
                if live(4):
                    gather(*at(r, s, 4))
                if live(-1):
                    scatter(*at(r, s, -1))

            pool.wait_ge(cleared, 2)
            last = run(pool, step, 4, 1)
            for s in range(R):
                pool.wait_ge(put[s], 16 * last + 16)

        @block.tensor
        def _(pe):
            def transpose_y(j, s):
                pe.wait_ge(y_hi_ready, j + 1)
                pe.wait_ge(y_lo_ready, j + 1)
                if later(j, 2):
                    pe.wait_ge(yT_ready, j - 1)
                for part in range(2):
                    for t in range(DT):
                        last = pe.transpose(yT_bank[s][:, part, t, :], y_parts[:, s, part, t * P:(t + 1) * P], ident16[:])
                last.then_inc(yT_summed, 1)

            def multiply(j, s, e):
                pe.wait_ge(yT_ready, j + 1)
                if later(j, 2):
                    pe.wait_ge(biased_ready, j - 1)
                for t in range(DT):
                    for yp, wp in PRODUCTS:
                        last = pe.matmul(out_bank[s][:], yT[:, s, yp, t, :],
                                         w_parts[:, bass.ds(e, 1), t, wp, :].rearrange("p a n -> p (a n)"),
                                         start=(t == 0 and (yp, wp) == PRODUCTS[0]),
                                         stop=(t == DT - 1 and (yp, wp) == PRODUCTS[-1]))
                last.then_inc(expert_summed, 1)

            def step(r, s, live, pass_experts):
                if live(1):
                    transpose_y(R * r + s + 1, (s + 1) % 2)
                if live(0):
                    multiply(R * r + s, s % 2, pass_experts[s])

            run(pe, step, 1, 0)

        @block.scalar
        def _(act):
            def copy_yT(j, s):
                act.wait_ge(yT_summed, j + 1)
                if later(j, 2):
                    act.wait_ge(expert_summed, j - 1)
                act.copy(yT[:, s], yT_bank[s][:]).then_inc(yT_ready, 1)

            def high_y(j, s):
                act.wait_ge(y_ready, j + 1)
                if later(j, 2):
                    act.wait_ge(yT_summed, j - 1)
                act.copy(y_parts[:, s, 0, :], y[:, s, :]).then_inc(y_hi_ready, 1)

            def step(r, s, live, _):
                if live(1):
                    copy_yT(R * r + s + 1, (s + 1) % 2)
                if live(2):
                    high_y(R * r + s + 2, s % 2)

            run(act, step, 2, 0)

        @block.vector
        def _(dve):
            def name_token(r, s, j):
                if later(j, R):
                    dve.wait_ge(got[s], GATHERS * r)
                    dve.nop(nofuse=True)
                dve.tensor_copy(token[:, s, :], slots[:, k, bass.ds(j, 1), 0:1].rearrange("p a b -> p (a b)")).then_inc(
                    token_ready, 1)

            def normalize(r, s, j):
                dve.wait_ge(got[s], GATHERS * r + GATHERS)
                if later(j, 2):
                    dve.wait_ge(y_lo_ready, j - 1)
                own = slots[:, k, bass.ds(j, 1), 2:4].rearrange("p a b -> p (a b)")
                dve.tensor_scalar(y[:, s % 2, :], x_got[:, s, :], own[:, 0:1], own[:, 1:2], ALU.subtract,
                                  ALU.mult).then_inc(y_ready, 1)

            def low_y(r, s, j):
                dve.wait_ge(y_hi_ready, j + 1)
                dve.tensor_tensor(y_parts[:, s % 2, 1, :], y[:, s % 2, :], y_parts[:, s % 2, 0, :],
                                  ALU.subtract).then_inc(y_lo_ready, 1)

            def finish(r, s, j, e):
                dve.wait_ge(expert_summed, j + 1)
                dve.scalar_tensor_tensor(biased[:, s % 2, :], out_bank[s % 2][:], 1.0 / W_SCALE,
                                         expert_bias[:, bass.ds(e, 1), :].rearrange("p a n -> p (a n)"), ALU.mult,
                                         ALU.add).then_inc(biased_ready, 1)
                if later(j, R):
                    dve.wait_ge(put[s], 16 * r)
                    dve.nop(nofuse=True)
                own = slots[:, k, bass.ds(j, 1), 0:2].rearrange("p a b -> p (a b)")
                dve.tensor_copy(token_out[:, s, :], own[:, 0:1]).then_inc(token_out_ready, 1)
                dve.wait_ge(biased_ready, j + 1)
                dve.scalar_tensor_tensor(result[:, s, :], biased[:, s % 2, :], own[:, 1:2], sum_got[:, s, :], ALU.mult,
                                         ALU.add).then_inc(result_ready, 1)

            def step(r, s, live, pass_experts):
                if live(3):
                    normalize(*at(r, s, 3))
                if live(0):
                    finish(r, s, R * r + s, pass_experts[s])
                if live(5):
                    name_token(*at(r, s, 5))
                if live(3):
                    low_y(*at(r, s, 3))

            dve.memset(x_got[:], 0.0).then_inc(cleared, 1)
            dve.memset(sum_got[:] if not same else biased[:], 0.0).then_inc(cleared, 1)
            dve.wait_ge(cleared, 2)
            run(dve, step, 5, 0)


def flamingo_block(nc, x, ctx_1024, g_xattn, g_ffn, L0_xattn_ln_gamma, L0_xattn_ln_beta, L0_xattn_w_q,
                   L0_xattn_w_kv, L0_xattn_w_out, L0_xattn_b_out, L0_xattn_gate, L0_ffn_gate_w, L0_ffn_gate_b,
                   L0_ffn_expert_w, L0_ffn_expert_b, identity, out):
    x_in = x.rearrange("b s d -> (b s) d")
    x_final = out.rearrange("b s d -> (b s) d")
    m_dram = nc.dram_tensor("m_dram", [BATCH, P, DT, 2, COLS], F16, kind="Internal").ap()
    u_dram = nc.dram_tensor("u_dram", [BATCH, COLS, 2, D], F16, kind="Internal").ap()
    x_mid = nc.dram_tensor("x_mid", [TOKENS, D], F32, kind="Internal").ap()
    table = nc.dram_tensor("table", [TABLE_ROWS, 4], F32, kind="Internal").ap()
    with ExitStack() as stack:
        ident = stack.enter_context(nc.sbuf_tensor("ident", [P, P], F32))
        ident16 = stack.enter_context(nc.sbuf_tensor("ident16", [P, P], F16))
        ones16 = stack.enter_context(nc.sbuf_tensor("ones16", [P, P], F16))
        placed = stack.enter_context(nc.sbuf_tensor("placed", [P, 2, TOP_K * EXPERTS], F16))
        w_parts = stack.enter_context(nc.sbuf_tensor("w_parts", [P, EXPERTS, DT, 2, D], F16))
        ident_in = stack.enter_context(nc.semaphore("ident_in"))
        ident16_ready = stack.enter_context(nc.semaphore("ident16_ready"))
        with nc.Block() as block:
            @block.sync
            def _(sp):
                sp.dma_start(ident[:], identity).then_inc(ident_in, 16)

            @block.vector
            def _(dve):
                dve.wait_ge(ident_in, 16)
                dve.tensor_copy(ident16[:], ident[:]).then_inc(ident16_ready, 1)
                dve.memset(ones16[:], 1.0).then_inc(ident16_ready, 1)
                dve.wait_ge(ident16_ready, 2)

        fold_context(nc, ident, L0_xattn_w_q, L0_xattn_w_kv, L0_xattn_w_out, L0_xattn_b_out, L0_xattn_gate,
                     g_xattn, ctx_1024, m_dram, u_dram, L0_ffn_expert_w, w_parts, table)
        attend(nc, ident16, x_in, L0_xattn_ln_gamma, L0_xattn_ln_beta, m_dram, u_dram, x_mid, x_final,
               L0_ffn_gate_w, L0_ffn_gate_b, g_ffn, table, placed, ones16)
        tile_expert = stack.enter_context(nc.sbuf_tensor("tile_expert", [P, TOP_K, PASSES, LISTED], I32))
        inner_passes = stack.enter_context(nc.sbuf_tensor("inner_passes", [P, TOP_K], I32))
        slots = stack.enter_context(nc.sbuf_tensor("slots", [P, TOP_K, 2 * SLOT_TILES, 4], F32))
        expert_bias = stack.enter_context(nc.sbuf_tensor("expert_bias", [P, EXPERTS, D], F32))
        list_tiles(nc, ones16, placed, table, L0_ffn_expert_b, expert_bias, tile_expert, inner_passes, slots)
        run_experts(nc, 0, ident16, w_parts, tile_expert, inner_passes, slots, expert_bias, x_mid, x_mid, x_final)
        run_experts(nc, 1, ident16, w_parts, tile_expert, inner_passes, slots, expert_bias, x_mid, x_final, x_final)


_INS = ['x', 'ctx_1024', 'g_xattn', 'g_ffn', 'L0_xattn_ln_gamma', 'L0_xattn_ln_beta', 'L0_xattn_w_q',
        'L0_xattn_w_kv', 'L0_xattn_w_out', 'L0_xattn_b_out', 'L0_xattn_gate', 'L0_ffn_gate_w', 'L0_ffn_gate_b',
        'L0_ffn_expert_w', 'L0_ffn_expert_b']


def kernel(**inputs):
    import numpy as _np
    import concourse.bacc as _bacc
    from concourse import mybir as _mybir
    from concourse.bass_utils import run_bass_kernel_spmd as _run

    nc = _bacc.Bacc("TRN2", target_bir_lowering=False, num_devices=1)
    arrays, args = {}, []
    given = [(name, _np.ascontiguousarray(inputs[name])) for name in _INS]
    given.append(("identity", _np.eye(128, dtype=_np.float32)))
    for name, a in given:
        arrays[f"in_{name}_dram"] = a
        args.append(nc.dram_tensor(f"in_{name}_dram", a.shape, _mybir.dt.from_np(a.dtype), kind="ExternalInput").ap())
    args.append(nc.dram_tensor("out_0_dram", (4, 2048, 512), _mybir.dt.float32, kind="ExternalOutput").ap())
    flamingo_block(nc, *args)
    r = _run(nc, [arrays], core_ids=[0])
    return r.results[0]["out_0_dram"]
```

```python
from contextlib import ExitStack

import concourse.bass as bass
from concourse import mybir
from concourse.alu_op_type import AluOpType as ALU

F32 = mybir.dt.float32
F16 = mybir.dt.float16
I32 = mybir.dt.int32
U32 = mybir.dt.uint32
ACT = mybir.ActivationFunctionType
AX_X = mybir.AxisListType.X

P = 128
D = 512
DT = D // P
HEADS = 16
DH = 64
INNER = HEADS * DH
PAIRS = INNER // P
BATCH = 4
SEQ = 2048
KEYS = 77
TOKENS = BATCH * SEQ
TILES = TOKENS // P
TPB = SEQ // P
COLS = HEADS * KEYS
KT = -(-COLS // P)
LAST = COLS - (KT - 1) * P
BANK_HEADS = (6, 5, 5)
HEAD0 = (0, 6, 11)
PT_GROUPS = ((0, 4), (4, 8), (8, 10))
EPS = 1e-5
EXPERTS = 8
GATES = EXPERTS + 2
TOP_K = 2
REGIONS = EXPERTS + 1
SLOT_TILES = TILES + EXPERTS
REGION_ROWS = SLOT_TILES * P
TABLE_ROWS = TOP_K * REGIONS * REGION_ROWS
TABLE_TILES = TABLE_ROWS // P
NO_ROW = float(1 << 25)
RING = 6
PASSES = SLOT_TILES // RING
LISTED = 8
NO_TOKEN = float(TOKENS)

M_SCALE = 64.0
U_SCALE = 64.0
P_SCALE = 4096.0
G_SCALE = 64.0
W_SCALE = 64.0
PRODUCTS = ((0, 0), (0, 1), (1, 0))


def load_m(engine, m_sb, m_dram, b):
    return engine.dma_start(m_sb.rearrange("p a t l c -> p (a t) l c"), m_dram[bass.ds(b, 1)].rearrange("a p t l c -> (a p) t l c"))


def load_u(engine, u_sb, u_dram, b):
    u = u_dram[bass.ds(b, 1)].rearrange("a r l n -> (a r) l n")
    yield engine.dma_start(u_sb[:, 0:KT - 1], u[0:(KT - 1) * P].rearrange("(k p) l n -> p k l n", p=P))
    yield engine.dma_start(u_sb[0:LAST, KT - 1], u[(KT - 1) * P:COLS])


def fold_context(nc, ident, wq, wkv, wout, b_out, gate, g_xattn, ctx, m_dram, u_dram, m_sb, u_sb, table):
    NB = 8
    MS, US = 4, 8
    RAW = 4
    FILL = 54
    FILLS = TABLE_TILES // FILL
    C_SCALE, W16, K_SCALE = 16.0, 64.0, 16.0
    WQ_CHUNK, WOUT_CHUNK, CHUNKS = 4, 6, 10
    K0 = DT
    V0 = K0 + PAIRS
    WQ0 = V0 + PAIRS
    M0 = WQ0 + PAIRS
    NM = DT * HEADS
    U0 = M0 + NM
    NU = BATCH * HEADS
    CK = BATCH * KEYS
    HALVES = (slice(0, DH), slice(DH, P))
    with ExitStack() as stack:
        def sb(name, shape, dt=F32):
            return stack.enter_context(nc.sbuf_tensor(name, shape, dt))

        def sem(name):
            return stack.enter_context(nc.semaphore(name))

        raw = sb("raw", [P, RAW, DT, D])
        ctx_sb = sb("ctx_sb", [KEYS, BATCH, D])
        ctxT = sb("ctxT", [P, 2, DT, CK], F16)
        kvw_parts = sb("kvw_parts", [P, 4, 2, DT, D], F16)
        wq_stack = sb("wq_stack", [P, HEADS, D], F16)
        k_twice = sb("k_twice", [P, 2, HEADS, CK], F16)
        v_stack = sb("v_stack", [P, HEADS, CK], F16)
        m_stage = sb("m_stage", [P, MS, BATCH, 2, 4 * KEYS], F16)
        u_stage = m_sb[0:KEYS, 1].rearrange("p t l c -> p (t l c)")[:, 0:US * 2 * D].rearrange(
            "p (u l n) -> p u l n", u=US, l=2)
        fill = sb("fill", [P, FILL, 4])
        bias = sb("bias", [1, D])
        bias_parts = sb("bias_parts", [1, 2, D], F16)
        ones_row = sb("ones_row", [1, KEYS], F16)
        gates = sb("gates", [P, 2])
        tanhs = sb("tanhs", [P, 2])
        u_gain = sb("u_gain", [P, 1])
        banks = [stack.enter_context(nc.psum_tensor(f"fold{i}", [P, 512], F32)) for i in range(NB)]

        ctx_in = sem("ctx_in")
        raw_in = [sem(f"raw_in{i}") for i in range(RAW)]
        small_in = sem("small_in")
        tanh_ready = sem("tanh_ready")
        gain_ready = sem("gain_ready")
        ones_ready = sem("ones_ready")
        bias_hi_ready = sem("bias_hi_ready")
        bias_lo_ready = sem("bias_lo_ready")
        chunk_hi_ready = sem("chunk_hi_ready")
        chunk_lo_ready = sem("chunk_lo_ready")
        wout_scaled = sem("wout_scaled")
        wout_lo_ready = sem("wout_lo_ready")
        product_ready = sem("product_ready")
        hi_ready = sem("hi_ready")
        lo_ready = sem("lo_ready")
        m_stored = [sem(f"m_stored{i}") for i in range(MS)]
        u_stored = [sem(f"u_stored{i}") for i in range(US)]
        fill_zero = sem("fill_zero")
        fill_ready = sem("fill_ready")
        table_clear = sem("table_clear")

        def raw_wait(engine, c):
            loads = [2 if n >= WOUT_CHUNK else 1 for n in range(c % RAW, c + 1, RAW)]
            engine.wait_ge(raw_in[c % RAW], 16 * sum(loads))

        def stacked(to, m, bank, scale):
            return [(to[HALVES[a], 2 * m + a], to[HALVES[1 - a], 2 * m + a], to[HALVES[a], 2 * m + a],
                     bank[HALVES[a], :], scale) for a in range(2)]

        def twice(to, m, bank, scale):
            return [(to[half, 0, 2 * m + a], to[half, 1, 2 * m + a], to[HALVES[a], 0, 2 * m + a],
                     bank[HALVES[a], :], scale) for a in range(2) for half in HALVES]

        def job(n):
            bank = banks[n % NB]
            if n < K0:
                return [(ctxT[:, 0, n], ctxT[:, 1, n], ctxT[:, 0, n], bank[:, 0:CK], C_SCALE)]
            if n < V0:
                return twice(k_twice, n - K0, bank[:, 0:CK], K_SCALE / (C_SCALE * W16))
            if n < WQ0:
                return stacked(v_stack, n - V0, bank[:, 0:CK], K_SCALE / (C_SCALE * W16))
            if n < M0:
                return stacked(wq_stack, n - WQ0, bank[:], W16)
            if n < U0:
                g, hh = divmod(n - M0, 4)
                cols = slice(hh * KEYS, (hh + 1) * KEYS)
                hi = m_stage[:, g % MS, :, 0, cols]
                return [(hi, m_stage[:, g % MS, :, 1, cols], hi,
                         bank[:, 0:CK].rearrange("p (b j) -> p b j", b=BATCH),
                         M_SCALE * DH ** -0.5 / (K_SCALE * W16))]
            u = (n - U0) % US
            return [(u_stage[:, u, 0], u_stage[:, u, 1], u_stage[:, u, 0], bank[0:KEYS, :], u_gain[0:KEYS, :])]

        def u_pieces(n):
            b, h = divmod(n, HEADS)
            if b > 0:
                return [(slice(0, KEYS), u_dram[b, h * KEYS:(h + 1) * KEYS])]
            k, row = divmod(h * KEYS, P)
            fit = min(KEYS, P - row)
            pieces = [(slice(0, fit), u_sb[row:row + fit, k])]
            if fit < KEYS:
                pieces.append((slice(fit, KEYS), u_sb[0:KEYS - fit, k + 1]))
            return pieces

        def u_stores(n, last):
            return 16 * sum(len(u_pieces(j)) for j in range(n % US, last + 1, US))

        def stage_free(engine, n):
            if M0 <= n < U0:
                g, hh = divmod(n - M0, 4)
                if hh == 0 and g >= MS:
                    engine.wait_ge(m_stored[g % MS], 16 * 3 * (g // MS))
            elif n >= U0 + US:
                u = n - U0
                engine.wait_ge(u_stored[u % US], u_stores(u, u - US))

        block = stack.enter_context(nc.Block())

        @block.sync
        def _(sp):
            def load_chunk(c):
                if c < WOUT_CHUNK:
                    src = wkv[:, c * D:(c + 1) * D] if c < WQ_CHUNK else wq[:, (c - WQ_CHUNK) * D:(c - WQ_CHUNK + 1) * D]
                    sp.dma_start(raw[:, c % RAW], src.rearrange("(t p) n -> p t n", p=P)).then_inc(raw_in[c % RAW], 16)
                    return
                src = wout[(c - WOUT_CHUNK) * 4 * DH:(c - WOUT_CHUNK + 1) * 4 * DH, :]
                for half in HALVES:
                    sp.dma_start(raw[half, c % RAW], src.rearrange("(t p) n -> p t n", p=DH)).then_inc(
                        raw_in[c % RAW], 16)

            sp.dma_start(ctx_sb[:], ctx.rearrange("b j d -> j b d")).then_inc(ctx_in, 16)
            sp.dma_start(gates[:, 0:1], gate.rearrange("(a b) -> a b", a=1).broadcast_to([P, 1])).then_inc(small_in, 16)
            sp.dma_start(gates[:, 1:2], g_xattn.rearrange("(a b) -> a b", a=1).broadcast_to([P, 1])).then_inc(small_in, 16)
            sp.dma_start(bias[:], b_out.rearrange("(a d) -> a d", a=1)).then_inc(small_in, 16)
            for c in range(RAW):
                load_chunk(c)
            for c in range(WQ_CHUNK, WQ_CHUNK + 4):
                sp.wait_ge(chunk_lo_ready, c - RAW + 1)
                load_chunk(c)
            sp.wait_ge(fill_ready, 1)
            sp.dma_start(table.rearrange("(p c r) w -> p c (r w)", p=P, c=FILLS),
                         fill[:].rearrange("p r w -> p (r w)").unsqueeze(1).broadcast_to([P, FILLS, FILL * 4]),
                         ).then_inc(table_clear, 16)
            sp.wait_ge(product_ready, M0)
            for c in (8, 9):
                load_chunk(c)
            for g in range(NM // 4):
                dt, quad = divmod(g, 4)
                sp.wait_ge(hi_ready, M0 + 4 * g + 4)
                sp.wait_ge(lo_ready, M0 + 4 * g + 4)
                cols = slice(quad * 4 * KEYS, (quad + 1) * 4 * KEYS)
                sp.dma_start(m_sb[:, 0, dt, :, cols], m_stage[:, g % MS, 0]).then_inc(m_stored[g % MS], 16)
                for part in range(2):
                    sp.dma_start(m_dram[1:, :, dt, part, cols].rearrange("b p c -> p b c"),
                                 m_stage[:, g % MS, 1:, part]).then_inc(m_stored[g % MS], 16)
            for n in range(NU):
                sp.wait_ge(hi_ready, U0 + n + 1)
                sp.wait_ge(lo_ready, U0 + n + 1)
                for piece, to in u_pieces(n):
                    sp.dma_start(to, u_stage[piece, n % US]).then_inc(u_stored[n % US], 16)
            for g in range(MS):
                sp.wait_ge(m_stored[g], 16 * 3 * NM // 4 // MS)
            for s in range(US):
                sp.wait_ge(u_stored[s], u_stores(s, NU - 1))
            sp.wait_ge(table_clear, 16)

        @block.tensor
        def _(pe):
            def bank(n):
                if n >= NB:
                    pe.wait_ge(hi_ready, n - NB + 1)
                    pe.wait_ge(lo_ready, n - NB + 1)
                return banks[n % NB]

            pe.wait_ge(ctx_in, 16)
            for t in range(DT):
                out = bank(t)
                for b in range(BATCH):
                    last = pe.transpose(out[:, b * KEYS:(b + 1) * KEYS], ctx_sb[:, b, t * P:(t + 1) * P],
                                        ident[0:KEYS, 0:KEYS])
                last.then_inc(product_ready, 1)
            pe.wait_ge(hi_ready, DT)
            pe.wait_ge(lo_ready, DT)
            for m in range(2 * PAIRS):
                out = bank(K0 + m)
                c, col = divmod(m * P, D)
                pe.wait_ge(chunk_hi_ready, c + 1)
                pe.wait_ge(chunk_lo_ready, c + 1)
                for t in range(DT):
                    for wp, cp in PRODUCTS:
                        last = pe.matmul(out[:, 0:CK], kvw_parts[:, c, wp, t, col:col + P], ctxT[:, cp, t, :],
                                         start=(t == 0 and (wp, cp) == PRODUCTS[0]),
                                         stop=(t == DT - 1 and (wp, cp) == PRODUCTS[-1]))
                last.then_inc(product_ready, 1)
            for m in range(PAIRS):
                out = bank(WQ0 + m)
                c, at = divmod(m * P, D)
                raw_wait(pe, WQ_CHUNK + c)
                for t in range(DT):
                    last = pe.transpose(out[:, t * P:(t + 1) * P], raw[:, (WQ_CHUNK + c) % RAW, t, at:at + P], ident[:])
                last.then_inc(product_ready, 1)
            pe.wait_ge(hi_ready, M0)
            pe.wait_ge(lo_ready, M0)
            for n in range(NM):
                dt, h = divmod(n, HEADS)
                out = bank(M0 + n)
                for part in range(2):
                    last = pe.matmul(out[:, 0:CK], wq_stack[:, h, dt * P:(dt + 1) * P], k_twice[:, part, h, :],
                                     start=(part == 0), stop=(part == 1))
                last.then_inc(product_ready, 1)
            pe.wait_ge(chunk_hi_ready, 8)
            pe.wait_ge(wout_lo_ready, 4)
            pe.wait_ge(ones_ready, 1)
            pe.wait_ge(bias_lo_ready, 1)
            for n in range(NU):
                b, h = divmod(n, HEADS)
                out = bank(U0 + n)
                if h == 0:
                    for part in range(2):
                        pe.matmul(out[0:KEYS, :], ones_row[:], bias_parts[:, part], start=(part == 0), stop=False)
                for part in range(2):
                    last = pe.matmul(out[0:KEYS, :], v_stack[:, h, b * KEYS:(b + 1) * KEYS],
                                     kvw_parts[:, h // 4, part, h % 4, :], start=(h > 0 and part == 0), stop=(part == 1))
                last.then_inc(product_ready, 1)

        def jobs(first, end):
            return [("job", n) for n in range(first, end)]

        ORDER = (jobs(0, K0) + [("chunk", 0), ("chunk", 1)] + jobs(K0, K0 + 4) + [("chunk", 2)]
                 + jobs(K0 + 4, K0 + 8) + [("chunk", 3)] + jobs(K0 + 8, WQ0) + [("chunk", 4), ("chunk", 5)]
                 + jobs(WQ0, M0 + 4) + [("chunk", 6)] + jobs(M0 + 4, M0 + 16) + [("chunk", 7)]
                 + jobs(M0 + 16, U0 + NU))

        @block.scalar
        def _(act):
            act.wait_ge(small_in, 48)
            act.activation(tanhs[:], gates[:], ACT.Tanh).then_inc(tanh_ready, 1)
            act.mul(bias_parts[:, 0], bias[:], W16).then_inc(bias_hi_ready, 1)
            for what, n in ORDER:
                if what == "chunk":
                    c = n if n < 4 else n + WOUT_CHUNK - 4
                    raw_wait(act, c)
                    if n >= 4:
                        act.wait_ge(product_ready, WQ0)
                    act.mul(kvw_parts[:, n % 4, 0], raw[:, c % RAW], W16).then_inc(chunk_hi_ready, 1)
                    continue
                if n == U0:
                    act.wait_ge(gain_ready, 1)
                stage_free(act, n)
                act.wait_ge(product_ready, n + 1)
                for hi, lo, hi_there, sums, scale in job(n):
                    last = act.activation(hi, sums, ACT.Copy, scale=scale)
                last.then_inc(hi_ready, 1)

        @block.vector
        def _(dve):
            dve.memset(ones_row[:], C_SCALE).then_inc(ones_ready, 1)
            dve.wait_ge(tanh_ready, 1)
            dve.scalar_tensor_tensor(u_gain[:], tanhs[:, 0:1], U_SCALE / (K_SCALE * W16), tanhs[:, 1:2], ALU.mult,
                                     ALU.mult).then_inc(gain_ready, 1)
            dve.wait_ge(bias_hi_ready, 1)
            dve.scalar_tensor_tensor(bias_parts[:, 1], bias[:], W16, bias_parts[:, 0], ALU.mult,
                                     ALU.subtract).then_inc(bias_lo_ready, 1)
            for what, n in ORDER:
                if what == "chunk":
                    if n < WQ_CHUNK:
                        dve.wait_ge(chunk_hi_ready, n + 1)
                        dve.scalar_tensor_tensor(kvw_parts[:, n, 1].rearrange("p t n -> p (t n)"),
                                                 raw[:, n % RAW].rearrange("p t n -> p (t n)"), W16,
                                                 kvw_parts[:, n, 0].rearrange("p t n -> p (t n)"), ALU.mult,
                                                 ALU.subtract).then_inc(chunk_lo_ready, 1)
                    continue
                if n == U0:
                    dve.wait_ge(gain_ready, 1)
                dve.wait_ge(hi_ready, n + 1)
                for hi, lo, hi_there, sums, scale in job(n):
                    last = dve.scalar_tensor_tensor(lo, sums, scale, hi_there, ALU.mult, ALU.subtract)
                last.then_inc(lo_ready, 1)

        @block.gpsimd
        def _(pool):
            pool.memset(fill[:], 0.0).then_inc(fill_zero, 1)
            pool.wait_ge(fill_zero, 1)
            pool.memset(fill[:, :, 0:1], NO_TOKEN).then_inc(fill_ready, 1)
            for n in range(4):
                slot = (WOUT_CHUNK + n) % RAW
                pool.wait_ge(chunk_hi_ready, 4 + n + 1)
                pool.tensor_scalar(raw[:, slot], raw[:, slot], W16, None, ALU.mult).then_inc(wout_scaled, 1)
                pool.wait_ge(wout_scaled, n + 1)
                pool.tensor_tensor(kvw_parts[:, n, 1], raw[:, slot], kvw_parts[:, n, 0], ALU.subtract).then_inc(
                    wout_lo_ready, 1)



def attend(nc, ident16, x_in, ln_gamma, ln_beta, m_dram, u_dram, m_sb, u_sb, x_mid, x_final, gate_w, gate_b,
           g_ffn, table, placed, ones16, expert_w, w_parts):
    with ExitStack() as stack:
        def sb(name, shape, dt=F32):
            return stack.enter_context(nc.sbuf_tensor(name, shape, dt))

        def psum(name, shape, dt=F32):
            return stack.enter_context(nc.psum_tensor(name, shape, dt))

        def sem(name):
            return stack.enter_context(nc.semaphore(name))

        w_raw = sb("w_raw", [P, 2, D // 2])
        gamma = sb("gamma", [P, D])
        beta = sb("beta", [P, D])
        x_ln = sb("x_ln", [P, 2, D])
        x_res = sb("x_res", [P, 2, D])
        stats = sb("stats", [P, 2, 6])
        moments = sb("moments", [P, 2, 2])
        spread = sb("spread", [P, 2, 1])
        rstd = sb("rstd", [P, 2, 1])
        minus_half = sb("minus_half", [P, 1])
        z = sb("z", [P, 2, D])
        z_parts = sb("z_parts", [P, 2, 2, D], F16)
        zT = sb("zT", [P, 2, 2, DT, P], F16)
        top = sb("top", [P, 2, HEADS])
        expd = sb("expd", [P, 2, COLS])
        total = sb("total", [P, 2, HEADS])
        inverse = sb("inverse", [P, 2, HEADS])
        p_parts = sb("p_parts", [P, 2, COLS], F16)
        pT = sb("pT", [P, KT, 2, P], F16)
        x_out = sb("x_out", [P, 2, D])
        x_stats = sb("x_stats", [P, 2, 6])
        x_moments = sb("x_moments", [P, 2, 2])
        x_spread = sb("x_spread", [P, 2, 1])
        y = sb("y", [P, 2, D])
        y_parts = sb("y_parts", [P, 2, 2, D], F16)
        yT = sb("yT", [P, 2, DT, P], F16)
        gate_raw = sb("gate_raw", [P, DT, GATES])
        gate_scaled = sb("gate_scaled", [P, DT, GATES])
        gate_parts = sb("gate_parts", [P, DT, 2, GATES], F16)
        gate_bias = sb("gate_bias", [P, GATES])
        logits = sb("logits", [P, 2, GATES])
        largest = sb("largest", [P, 2, 8])
        found = sb("found", [P, 2, 8], U32)
        expert = sb("expert", [P, 2, TOP_K])
        gap = sb("gap", [P, 2, TOP_K])
        ratio = sb("ratio", [P, 2, TOP_K])
        norms = sb("norms", [P, 2, 2])
        onehot = sb("onehot", [P, 2, TOP_K, EXPERTS], F16)
        iota_e = sb("iota_e", [P, TOP_K, EXPERTS])
        region = sb("region", [P, TOP_K, EXPERTS])
        iota_t = sb("iota_t", [P, TILES])
        below = sb("below", [P, P], F16)
        g_raw = sb("g_raw", [P, 1])
        g_tanh = sb("g_tanh", [P, 1])
        place = sb("place", [P, TOP_K, EXPERTS])
        mine = sb("mine", [P, TOP_K, EXPERTS])
        row = sb("row", [P, TOP_K])
        no_row = sb("no_row", [P, TOP_K])
        row_f = sb("row_f", [P, TOP_K])
        row_whole = sb("row_whole", [P, TOP_K], I32)
        tile_whole = sb("tile_whole", [P, TOP_K], I32)
        tile_f = sb("tile_f", [P, TOP_K])
        part_f = sb("part_f", [P, TOP_K])
        row_i = sb("row_i", [P, 2, TOP_K], I32)
        kept = sb("kept", [P, TOP_K])
        kept_sum = sb("kept_sum", [P, 1])
        kept_div = sb("kept_div", [P, 1])
        kept_inv = sb("kept_inv", [P, 1])
        payload = sb("payload", [P, 2, TOP_K, 4])

        scores = [psum(f"scores{k}", [P, 512]) for k in range(3)]
        pT_bank = [psum(f"pT_bank{k}", [P, 4, 2, P], F16) for k in range(3)]
        gate_bank = pT_bank[2][:, 2:4].rearrange("p a b c -> p (a b c)").bitcast(F32)[:, 0:GATES]
        rank_bank = pT_bank[2][:, 2:4].rearrange("p a b c -> p (a b c)").bitcast(F32)[:, 16:16 + TOP_K * EXPERTS]
        zT_bank = psum("zT_bank", [P, 2, DT, P], F16)
        mix = psum("mix", [P, D])

        affine_in = sem("affine_in")
        w_in = [sem(f"w_in{s}") for s in range(2)]
        w_split = sem("w_split")
        m_in = sem("m_in")
        u_in = sem("u_in")
        x_ln_in = [sem(f"x_ln_in{s}") for s in range(2)]
        x_res_in = [sem(f"x_res_in{s}") for s in range(2)]
        stored = [sem(f"stored{s}") for s in range(2)]
        const_ready = sem("const_ready")
        stats_ready = sem("stats_ready")
        moments_ready = sem("moments_ready")
        spread_ready = sem("spread_ready")
        rstd_ready = sem("rstd_ready")
        z_ready = sem("z_ready")
        scaled_ready = sem("scaled_ready")
        shifted_ready = sem("shifted_ready")
        z_hi_ready = sem("z_hi_ready")
        z_lo_ready = sem("z_lo_ready")
        zT_summed = sem("zT_summed")
        zT_ready = sem("zT_ready")
        scores_ready = sem("scores_ready")
        top_ready = sem("top_ready")
        less_ready = sem("less_ready")
        exp_ready = sem("exp_ready")
        pT_summed = sem("pT_summed")
        pT_ready = sem("pT_ready")
        total_ready = sem("total_ready")
        inverse_ready = sem("inverse_ready")
        p_ready = sem("p_ready")
        p_hi_ready = sem("p_hi_ready")
        p_lo_ready = sem("p_lo_ready")
        mix_ready = sem("mix_ready")
        x_out_ready = sem("x_out_ready")

        gate_in = sem("gate_in")
        gate_scaled_ready = sem("gate_scaled_ready")
        gate_hi_ready = sem("gate_hi_ready")
        gate_lo_ready = sem("gate_lo_ready")
        x_stats_ready = sem("x_stats_ready")
        x_moments_ready = sem("x_moments_ready")
        x_spread_ready = sem("x_spread_ready")
        x_rstd_ready = sem("x_rstd_ready")
        y_ready = sem("y_ready")
        y_hi_ready = sem("y_hi_ready")
        y_lo_ready = sem("y_lo_ready")
        yT_summed = sem("yT_summed")
        yT_ready = sem("yT_ready")
        gate_summed = sem("gate_summed")
        logits_ready = sem("logits_ready")
        largest_ready = sem("largest_ready")
        choice_ready = sem("choice_ready")
        expert_ready = sem("expert_ready")
        gap_ready = sem("gap_ready")
        ratio_ready = sem("ratio_ready")
        norms_ready = sem("norms_ready")
        onehot_ready = sem("onehot_ready")
        g_in = sem("g_in")
        g_ready = sem("g_ready")
        iota_ready = sem("iota_ready")
        rank_summed = sem("rank_summed")
        place_ready = sem("place_ready")
        placing = sem("placing")
        row_i_ready = sem("row_i_ready")
        weight_ready = sem("weight_ready")
        payload_ready = sem("payload_ready")
        placed_ready = sem("placed_ready")
        scattered = [sem(f"scattered{s}") for s in range(2)]

        PLACING = 12

        def live(i):
            return not isinstance(i, int) or 0 <= i < TILES

        def later(i, n):
            return not isinstance(i, int) or i >= n

        def run(engine, step):
            first, last = 6, TILES - 2
            for i in range(first):
                step(i, i % 2)
            with engine.Fori(0, (last - first) // 2) as r:
                for k in range(2):
                    step(2 * r + first + k, k)
            for i in range(last, TILES + 7):
                step(i, i % 2)

        def rows(tensor, i):
            return tensor[bass.ds(i * P, P), :]

        block = stack.enter_context(nc.Block())

        @block.sync
        def _(sp):
            def load_x_ln(i, s):
                sp.dma_start(x_ln[:, s, :], rows(x_in, i)).then_inc(x_ln_in[s], 16)

            def load_x_res(i, s):
                sp.dma_start(x_res[:, s, :], rows(x_in, i)).then_inc(x_res_in[s], 16)

            def load_w(i, s):
                if later(i, 2):
                    sp.wait_ge(w_split, 3 * (i - 1))
                w_rows = expert_w.rearrange("e (t p) (h n) -> (e t) h p n", p=P, h=2)
                sp.dma_start(w_raw[:, s, :], w_rows[bass.ds(i // 2, 1), s].rearrange("a p n -> (a p) n")).then_inc(
                    w_in[s], 16)

            def store(i, s):
                sp.dma_start(rows(x_mid, i), x_out[:, s, :]).then_inc(stored[s], 16)
                sp.dma_start(rows(x_final, i), x_out[:, s, :]).then_inc(stored[s], 16)

            def step(i, s, more=True, before=True):
                if before:
                    sp.wait_ge(x_out_ready, i - 1)
                    store(i - 2, s)
                load_x_res(i, s)
                load_w(i, s)
                if more:
                    sp.wait_ge(z_ready, i + 3)
                    load_x_ln(i + 4, s)

            load_x_ln(0, 0)
            load_x_ln(1, 1)
            sp.dma_start(gamma[:], ln_gamma.rearrange("(a d) -> a d", a=1).broadcast_to([P, D])).then_inc(affine_in, 16)
            sp.dma_start(beta[:], ln_beta.rearrange("(a d) -> a d", a=1).broadcast_to([P, D])).then_inc(affine_in, 16)
            sp.dma_start(gate_bias[:], gate_b.rearrange("(a e) -> a e", a=1).broadcast_to([P, GATES])).then_inc(gate_in, 16)
            sp.dma_start(g_raw[:], g_ffn.rearrange("(a b) -> a b", a=1).broadcast_to([P, 1])).then_inc(g_in, 16)
            for t in range(DT):
                sp.dma_start(gate_raw[:, t, :], gate_w[:, t * P:(t + 1) * P].rearrange("e p -> p e"),
                             allow_slow_non_contiguous=True).then_inc(gate_in, 16)

            def batch(b, first=False, last=False):
                i0 = b * TPB
                step(i0, 0, before=not first)
                if not first:
                    sp.wait_ge(mix_ready, i0)
                    for load in load_u(sp, u_sb, u_dram, b):
                        load.then_inc(u_in, 16)
                step(i0 + 1, 1, before=not first)
                with sp.Fori(0, TPB // 2 - 3) as q:
                    for k in range(2):
                        step(i0 + 2 * q + 2 + k, k)
                if not last:
                    if not first:
                        sp.wait_ge(scores_ready, 3 * i0)
                    load_m(sp, m_sb[:, bass.ds((b + 1) % 2, 1)], m_dram, b + 1).then_inc(m_in, 16)
                for k in range(4):
                    step(i0 + TPB - 4 + k, k % 2, more=not last)

            for i in range(2):
                sp.wait_ge(z_ready, i + 1)
                load_x_ln(i + 2, i)
            batch(0, first=True)
            with sp.Fori(1, BATCH - 1) as b:
                batch(b)
            batch(BATCH - 1, last=True)
            for i in range(TILES - 2, TILES):
                sp.wait_ge(x_out_ready, i + 1)
                store(i, i % 2)
            for s in range(2):
                sp.wait_ge(stored[s], 32 * TILES // 2)

        @block.tensor
        def _(pe):
            def transpose_z(i, s):
                pe.wait_ge(z_hi_ready, i + 1)
                pe.wait_ge(z_lo_ready, i + 1)
                pe.wait_ge(zT_ready, i)
                if later(i, 4):
                    pe.wait_ge(yT_ready, i - 3)
                for part in range(2):
                    for t in range(DT):
                        last = pe.transpose(zT_bank[:, part, t, :], z_parts[:, s, part, t * P:(t + 1) * P], ident16[:])
                last.then_inc(zT_summed, 1)

            def score(i, s):
                pe.wait_ge(zT_ready, i + 1)
                if later(i, TPB):
                    pe.wait_ge(m_in, 16 * (i // TPB))
                for k in range(3):
                    if later(i, 1):
                        pe.wait_ge(less_ready, 3 * (i - 1) + k + 1)
                    n, c0 = BANK_HEADS[k] * KEYS, HEAD0[k] * KEYS
                    for t in range(DT):
                        for zp, mp in PRODUCTS:
                            m = m_sb[:, bass.ds(i // TPB % 2, 1), t, mp, c0:c0 + n].rearrange("p a c -> p (a c)")
                            last = pe.matmul(scores[k][:, 0:n], zT[:, s, zp, t, :], m,
                                             start=(t == 0 and (zp, mp) == PRODUCTS[0]),
                                             stop=(t == DT - 1 and (zp, mp) == PRODUCTS[-1]))
                    last.then_inc(scores_ready, 1)

            def transpose_p(i):
                pe.wait_ge(p_hi_ready, i + 1)
                pe.wait_ge(p_lo_ready, i + 1)
                for g, (k0, k1) in enumerate(PT_GROUPS):
                    if later(i, 1):
                        pe.wait_ge(pT_ready, 3 * i + g - 2)
                    if g == 2 and later(i, 3):
                        pe.wait_ge(logits_ready, i - 2)
                    if g == 2 and later(i, 5):
                        pe.wait_ge(place_ready, i - 4)
                    for k in range(k0, k1):
                        n = P if k < KT - 1 else LAST
                        for part in range(2):
                            last = pe.transpose(pT_bank[g][0:n, k - k0, part, :], p_parts[:, part, k * P:k * P + n],
                                                ident16[:])
                    last.then_inc(pT_summed, 1)

            def mix_values(i):
                if later(i, TPB):
                    pe.wait_ge(u_in, 32 * (i // TPB))
                pe.wait_ge(x_out_ready, i)
                for g, (k0, k1) in enumerate(PT_GROUPS):
                    pe.wait_ge(pT_ready, 3 * i + g + 1)
                    for k in range(k0, k1):
                        n = P if k < KT - 1 else LAST
                        for pp, up in PRODUCTS:
                            last = pe.matmul(mix[:], pT[0:n, k, pp, :], u_sb[0:n, k, up, :],
                                             start=(k == 0 and (pp, up) == PRODUCTS[0]),
                                             stop=(k == KT - 1 and (pp, up) == PRODUCTS[-1]))
                last.then_inc(mix_ready, 1)

            def transpose_y(i, s):
                pe.wait_ge(y_hi_ready, i + 1)
                pe.wait_ge(y_lo_ready, i + 1)
                pe.wait_ge(zT_ready, i + 4 if not isinstance(i, int) or i + 4 <= TILES else TILES)
                for part in range(2):
                    for t in range(DT):
                        last = pe.transpose(zT_bank[:, part, t, :], y_parts[:, s, part, t * P:(t + 1) * P], ident16[:])
                last.then_inc(yT_summed, 1)

            def gate(i):
                pe.wait_ge(yT_ready, i + 1)
                if isinstance(i, int) and i == 0:
                    pe.wait_ge(gate_lo_ready, 1)
                pe.wait_ge(logits_ready, i)
                if later(i, 3):
                    pe.wait_ge(place_ready, i - 2)
                pe.wait_ge(pT_ready, 3 * (i + 3) if not isinstance(i, int) or i + 3 <= TILES else 3 * TILES)
                for t in range(DT):
                    for yp, gp in PRODUCTS:
                        last = pe.matmul(gate_bank, yT[:, yp, t, :], gate_parts[:, t, gp, :],
                                         start=(t == 0 and (yp, gp) == PRODUCTS[0]),
                                         stop=(t == DT - 1 and (yp, gp) == PRODUCTS[-1]))
                last.then_inc(gate_summed, 1)

            def rank(i, s):
                pe.wait_ge(onehot_ready, i + 1)
                pe.wait_ge(placed_ready, i + 1)
                pe.wait_ge(place_ready, i)
                pe.wait_ge(logits_ready, i + 2 if not isinstance(i, int) or i + 2 <= TILES else TILES)
                pe.wait_ge(pT_ready, 3 * (i + 5) if not isinstance(i, int) or i + 5 <= TILES else 3 * TILES)
                hot = onehot[:, s].rearrange("p k e -> p (k e)")
                pe.matmul(rank_bank, below[:], hot, start=True, stop=False)
                pe.matmul(rank_bank, ones16[:], placed[:, 1 - s], start=False, stop=True).then_inc(rank_summed, 1)

            def step(i, s):
                if live(i):
                    score(i, s)
                if live(i - 1):
                    transpose_p(i - 1)
                if live(i + 1):
                    transpose_z(i + 1, 1 - s)
                if live(i - 1):
                    mix_values(i - 1)
                if live(i - 5):
                    rank(i - 5, 1 - s)
                if live(i - 3):
                    gate(i - 3)
                if live(i - 2):
                    transpose_y(i - 2, s)

            transpose_z(0, 0)
            run(pe, step)

        @block.scalar
        def _(act):
            def split_z(i, s):
                act.wait_ge(shifted_ready, i + 1)
                if not isinstance(i, int) or i >= 2:
                    act.wait_ge(zT_summed, i - 1)
                act.copy(z_parts[:, s, 0, :], z[:, s, :]).then_inc(z_hi_ready, 1)

            def copy_zT(i, s):
                act.wait_ge(zT_summed, i + 1)
                if not isinstance(i, int) or i >= 2:
                    act.wait_ge(scores_ready, 3 * (i - 1))
                act.copy(zT[:, s], zT_bank[:]).then_inc(zT_ready, 1)

            def exponent(i, s, k):
                n, c0 = BANK_HEADS[k] * KEYS, HEAD0[k] * KEYS
                act.wait_ge(less_ready, 3 * i + k + 1)
                act.activation(expd[:, s, c0:c0 + n], expd[:, s, c0:c0 + n], ACT.Exp,
                               scale=1.0 / M_SCALE).then_inc(exp_ready, 1)

            def split_p(i, s):
                act.wait_ge(p_ready, i + 1)
                act.wait_ge(pT_summed, 3 * i)
                act.copy(p_parts[:, 0, :], expd[:, s, :]).then_inc(p_hi_ready, 1)

            def copy_pT(i, g):
                k0, k1 = PT_GROUPS[g]
                act.wait_ge(pT_summed, 3 * i + g + 1)
                act.wait_ge(mix_ready, i)
                if k1 < KT:
                    act.copy(pT[:, k0:k1], pT_bank[g][:, 0:k1 - k0]).then_inc(pT_ready, 1)
                else:
                    act.copy(pT[:, k0:k1 - 1], pT_bank[g][:, 0:k1 - k0 - 1])
                    act.copy(pT[0:LAST, k1 - 1], pT_bank[g][0:LAST, k1 - k0 - 1]).then_inc(pT_ready, 1)

            def split_y(i, s):
                act.wait_ge(y_ready, i + 1)
                if later(i, 2):
                    act.wait_ge(yT_summed, i - 1)
                act.copy(y_parts[:, s, 0, :], y[:, s, :]).then_inc(y_hi_ready, 1)

            def copy_yT(i):
                act.wait_ge(yT_summed, i + 1)
                act.wait_ge(gate_summed, i)
                act.copy(yT[:], zT_bank[:]).then_inc(yT_ready, 1)

            def exponent_gap(i, s):
                act.wait_ge(gap_ready, i + 1)
                act.activation(ratio[:, s], gap[:, s], ACT.Exp).then_inc(ratio_ready, 1)

            def step(i, s):
                if live(i - 3):
                    copy_yT(i - 3)
                if live(i):
                    exponent(i, s, 0)
                if live(i - 2):
                    split_y(i - 2, s)
                if live(i):
                    exponent(i, s, 1)
                if live(i - 1):
                    copy_pT(i - 1, 0)
                if live(i):
                    exponent(i, s, 2)
                if live(i - 1):
                    copy_pT(i - 1, 1)
                    copy_pT(i - 1, 2)
                if live(i + 1):
                    copy_zT(i + 1, 1 - s)
                if live(i + 2):
                    split_z(i + 2, s)
                if live(i):
                    split_p(i, s)
                if live(i - 4):
                    exponent_gap(i - 4, s)

            split_z(0, 0)
            copy_zT(0, 0)
            split_z(1, 1)
            act.wait_ge(g_in, 16)
            act.activation(g_tanh[:], g_raw[:], ACT.Tanh).then_inc(g_ready, 1)
            run(act, step)

        @block.vector
        def _(dve):
            def moments_of(i, s):
                dve.wait_ge(x_ln_in[s], 8 * (i - s) + 16)
                dve.bn_stats(stats[:, s], x_ln[:, s, :]).then_inc(stats_ready, 1)

            def spread_of(i, s):
                dve.bn_aggr(moments[:, s], stats[:, s]).then_inc(moments_ready, 1)
                dve.wait_ge(moments_ready, i + 1)
                dve.tensor_scalar(spread[:, s], moments[:, s, 1:2], 1.0 + EPS, EPS * EPS, ALU.mult,
                                  ALU.add).then_inc(spread_ready, 1)

            def normalize(i, s):
                dve.wait_ge(rstd_ready, i + 1)
                if not isinstance(i, int) or i >= 2:
                    dve.wait_ge(z_lo_ready, i - 1)
                dve.tensor_scalar(z[:, s, :], x_ln[:, s, :], moments[:, s, 0:1], rstd[:, s], ALU.subtract,
                                  ALU.mult).then_inc(z_ready, 1)

            def less_top(i, s, k):
                h0, nh = HEAD0[k], BANK_HEADS[k]
                c0, n = h0 * KEYS, nh * KEYS
                bank = scores[k][:, 0:n].rearrange("p (h j) -> p h j", h=nh)
                dve.wait_ge(scores_ready, 3 * i + k + 1)
                dve.tensor_reduce(top[:, s, h0:h0 + nh], bank, AX_X, ALU.max).then_inc(top_ready, 1)
                dve.wait_ge(top_ready, 3 * i + k + 1)
                dve.tensor_tensor(expd[:, s, c0:c0 + n].rearrange("p (h j) -> p h j", h=nh), bank,
                                  top[:, s, h0:h0 + nh].unsqueeze(2).broadcast_to([P, nh, KEYS]),
                                  ALU.subtract).then_inc(less_ready, 1)

            def probabilities(i, s):
                e = expd[:, s, :].rearrange("p (h j) -> p h j", h=HEADS)
                dve.wait_ge(exp_ready, 3 * i + 3)
                dve.tensor_reduce(total[:, s], e, AX_X, ALU.add).then_inc(total_ready, 1)
                dve.wait_ge(total_ready, i + 1)
                dve.reciprocal(inverse[:, s], total[:, s]).then_inc(inverse_ready, 1)
                dve.wait_ge(inverse_ready, i + 1)
                dve.scalar_tensor_tensor(e, e, P_SCALE, inverse[:, s].unsqueeze(2).broadcast_to([P, HEADS, KEYS]),
                                         ALU.mult, ALU.mult).then_inc(p_ready, 1)

            def low_p(i, s):
                dve.wait_ge(p_hi_ready, i + 1)
                dve.tensor_tensor(p_parts[:, 1, :], expd[:, s, :], p_parts[:, 0, :], ALU.subtract).then_inc(p_lo_ready, 1)

            def residual(i, s):
                dve.wait_ge(mix_ready, i + 1)
                dve.wait_ge(x_res_in[s], 8 * (i - s) + 16)
                if not isinstance(i, int) or i >= 2:
                    dve.wait_ge(stored[s], 16 * (i - s))
                dve.scalar_tensor_tensor(x_out[:, s, :], mix[:], 1.0 / (P_SCALE * U_SCALE), x_res[:, s, :], ALU.mult,
                                         ALU.add).then_inc(x_out_ready, 1)

            def y_moments_of(i, s):
                dve.wait_ge(x_out_ready, i + 1)
                dve.bn_stats(x_stats[:, s], x_out[:, s, :]).then_inc(x_stats_ready, 1)

            def y_spread_of(i, s):
                dve.bn_aggr(x_moments[:, s], x_stats[:, s]).then_inc(x_moments_ready, 1)
                dve.wait_ge(x_moments_ready, i + 1)
                dve.tensor_scalar(x_spread[:, s], x_moments[:, s, 1:2], EPS, None, ALU.add).then_inc(x_spread_ready, 1)

            def y_normalize(i, s):
                dve.wait_ge(x_rstd_ready, i + 1)
                if later(i, 2):
                    dve.wait_ge(y_lo_ready, i - 1)
                dve.tensor_scalar(y[:, s, :], x_out[:, s, :], x_moments[:, s, 0:1], x_moments[:, s, 1:2], ALU.subtract,
                                  ALU.mult).then_inc(y_ready, 1)

            def take_logits(i, s):
                dve.wait_ge(gate_summed, i + 1)
                dve.scalar_tensor_tensor(logits[:, s, :], gate_bank, 1.0 / G_SCALE, gate_bias[:], ALU.mult,
                                         ALU.add).then_inc(logits_ready, 1)
                if later(i, 2):
                    dve.wait_ge(payload_ready, 2 * i - 3)
                dve.tensor_copy(norms[:, s], x_moments[:, s]).then_inc(norms_ready, 1)

            def choose(i, s):
                dve.wait_ge(logits_ready, i + 1)
                dve.nop(nofuse=True)
                dve.max(largest[:, s, :], logits[:, s, :]).then_inc(largest_ready, 1)
                dve.wait_ge(largest_ready, i + 1)
                dve.nop(nofuse=True)
                dve.max_index(found[:, s, :], largest[:, s, :], logits[:, s, :]).then_inc(choice_ready, 1)
                dve.tensor_scalar(gap[:, s], largest[:, s, 0:TOP_K], largest[:, s, 0:1], None,
                                  ALU.subtract).then_inc(gap_ready, 1)
                dve.wait_ge(choice_ready, i + 1)
                if isinstance(i, int) and i == 0:
                    dve.wait_ge(iota_ready, 4)
                dve.tensor_copy(expert[:, s], found[:, s, 0:TOP_K]).then_inc(expert_ready, 1)
                dve.wait_ge(expert_ready, i + 1)
                dve.tensor_tensor(onehot[:, s], iota_e[:], expert[:, s].unsqueeze(2).broadcast_to([P, TOP_K, EXPERTS]),
                                  ALU.is_equal).then_inc(onehot_ready, 1)

            def take_ranks(i, s):
                dve.wait_ge(rank_summed, i + 1)
                dve.wait_ge(gate_summed, i + 3 if not isinstance(i, int) or i + 3 <= TILES else TILES)
                dve.tensor_tensor(place[:].rearrange("p k e -> p (k e)"), rank_bank, region[:].rearrange("p k e -> p (k e)"),
                                  ALU.add).then_inc(place_ready, 1)
                if later(i, 2):
                    dve.wait_ge(scattered[s], 16 * (i - s))
                dve.wait_ge(norms_ready, i + 1)
                dve.tensor_copy(payload[:, s, :, 2:4], norms[:, s].unsqueeze(1).broadcast_to([P, TOP_K, 2])).then_inc(
                    payload_ready, 1)

            def place_rows(i, s):
                def start(instruction):
                    instruction.then_inc(placing, 1)

                def after(n):
                    dve.wait_ge(placing, PLACING * i + n)

                dve.wait_ge(ratio_ready, i + 1)
                start(dve.scalar_tensor_tensor(kept[:], expert[:, s], float(EXPERTS), ratio[:, s], ALU.is_lt,
                                               ALU.mult))
                dve.wait_ge(place_ready, i + 1)
                start(dve.tensor_tensor(mine[:], place[:], onehot[:, s], ALU.mult))
                start(dve.tensor_scalar(no_row[:], expert[:, s], float(EXPERTS), NO_ROW, ALU.is_ge,
                                        ALU.mult))
                after(1)
                start(dve.tensor_reduce(kept_sum[:], kept[:], AX_X, ALU.add))
                after(2)
                start(dve.tensor_reduce(row[:], mine[:], AX_X, ALU.add))
                after(4)
                start(dve.scalar_tensor_tensor(kept_div[:], kept_sum[:], 0.0, kept_sum[:], ALU.is_equal,
                                               ALU.add))
                after(5)
                start(dve.tensor_tensor(row_f[:], row[:], no_row[:], ALU.add))
                after(6)
                start(dve.reciprocal(kept_inv[:], kept_div[:]))
                after(7)
                start(dve.tensor_copy(row_whole[:], row_f[:]))
                dve.tensor_tensor(placed[:, s], placed[:, 1 - s], onehot[:, s].rearrange("p k e -> p (k e)"),
                                  ALU.add).then_inc(placed_ready, 1)
                if isinstance(i, int) and i == 0:
                    dve.wait_ge(g_ready, 1)
                after(9)
                start(dve.tensor_scalar(tile_whole[:], row_whole[:], 7, None, ALU.arith_shift_right))
                dve.tensor_scalar(payload[:, s, :, 1], kept[:], kept_inv[:], g_tanh[:], ALU.mult,
                                  ALU.mult).then_inc(weight_ready, 1)
                after(10)
                start(dve.tensor_copy(tile_f[:], tile_whole[:]))
                dve.tensor_copy(payload[:, s, :, 0], iota_t[:, bass.ds(i, 1)].broadcast_to([P, TOP_K])).then_inc(
                    payload_ready, 1)
                after(11)
                start(dve.scalar_tensor_tensor(part_f[:], tile_f[:], -float(P), row_f[:], ALU.mult,
                                               ALU.add))
                after(12)
                dve.scalar_tensor_tensor(row_i[:, s], part_f[:], float(TABLE_TILES), tile_f[:], ALU.mult,
                                         ALU.add).then_inc(row_i_ready, 1)

            def step(i, s):
                if live(i - 2):
                    residual(i - 2, s)
                    y_moments_of(i - 2, s)
                if live(i + 2):
                    moments_of(i + 2, s)
                if live(i - 6):
                    take_ranks(i - 6, s)
                if live(i - 4):
                    take_logits(i - 4, s)
                if live(i - 2):
                    dve.wait_ge(x_stats_ready, i - 1)
                if live(i + 2):
                    dve.wait_ge(stats_ready, i + 3)
                if live(i - 4):
                    dve.wait_ge(norms_ready, i - 3)
                dve.nop(nofuse=True)
                if live(i - 2):
                    y_spread_of(i - 2, s)
                if live(i + 2):
                    spread_of(i + 2, s)
                if live(i):
                    less_top(i, s, 0)
                if live(i - 2):
                    y_normalize(i - 2, s)
                if live(i + 2):
                    normalize(i + 2, s)
                if live(i):
                    less_top(i, s, 1)
                    less_top(i, s, 2)
                if live(i - 6):
                    place_rows(i - 6, s)
                if live(i):
                    probabilities(i, s)
                if live(i - 4):
                    choose(i - 4, s)
                if live(i):
                    low_p(i, s)

            dve.memset(minus_half[:], -0.5).then_inc(const_ready, 1)
            for i in range(2):
                moments_of(i, i)
                dve.wait_ge(stats_ready, i + 1)
                spread_of(i, i)
                normalize(i, i)
            dve.wait_ge(gate_in, 16 * (DT + 1))
            dve.tensor_scalar(gate_scaled[:], gate_raw[:], G_SCALE, None, ALU.mult).then_inc(gate_scaled_ready, 1)
            dve.wait_ge(gate_scaled_ready, 1)
            dve.tensor_copy(gate_parts[:, :, 0, :], gate_scaled[:]).then_inc(gate_hi_ready, 1)
            dve.wait_ge(gate_hi_ready, 1)
            dve.tensor_tensor(gate_parts[:, :, 1, :], gate_scaled[:], gate_parts[:, :, 0, :],
                              ALU.subtract).then_inc(gate_lo_ready, 1)
            dve.memset(placed[:], 0.0).then_inc(placed_ready, 1)
            dve.wait_ge(placed_ready, 1)
            run(dve, step)

        @block.gpsimd
        def _(pool):
            def layernorm(i, s):
                pool.wait_ge(spread_ready, i + 1)
                pool.tensor_tensor(rstd[:, s], spread[:, s], minus_half[:], ALU.pow).then_inc(rstd_ready, 1)
                pool.wait_ge(z_ready, i + 1)
                pool.tensor_tensor(z[:, s, :], z[:, s, :], gamma[:], ALU.mult).then_inc(scaled_ready, 1)
                pool.wait_ge(scaled_ready, i + 1)
                pool.tensor_tensor(z[:, s, :], z[:, s, :], beta[:], ALU.add).then_inc(shifted_ready, 1)

            def z_low(i, s):
                pool.wait_ge(z_hi_ready, i + 1)
                pool.tensor_tensor(z_parts[:, s, 1, :], z[:, s, :], z_parts[:, s, 0, :], ALU.subtract).then_inc(z_lo_ready, 1)

            def y_rstd(i, s):
                pool.wait_ge(x_spread_ready, i + 1)
                pool.tensor_tensor(x_moments[:, s, 1:2], x_spread[:, s], minus_half[:], ALU.pow).then_inc(x_rstd_ready, 1)

            def y_low(i, s):
                pool.wait_ge(y_hi_ready, i + 1)
                pool.tensor_tensor(y_parts[:, s, 1, :], y[:, s, :], y_parts[:, s, 0, :], ALU.subtract).then_inc(y_lo_ready, 1)

            def scatter(i, s):
                pool.wait_ge(row_i_ready, i + 1)
                pool.wait_ge(weight_ready, i + 1)
                pool.wait_ge(payload_ready, 2 * i + 2)
                pool.nop(nofuse=True)
                for k in range(TOP_K):
                    pool.indirect_dma_start(table, bass.IndirectOffsetOnAxis(ap=row_i[:, s, k:k + 1], axis=0),
                                            payload[:, s, k, :], None, bounds_check=TABLE_ROWS - 1,
                                            oob_is_err=False).then_inc(scattered[s], 16)

            def split_w(i, s):
                pool.wait_ge(w_in[s], 8 * (i - s) + 16)
                pool.nop(nofuse=True)
                hi, lo = [w_parts.rearrange("p e t l n -> p (e t) l n")[:, bass.ds(i // 2, 1), part,
                          s * (D // 2):(s + 1) * (D // 2)].rearrange("p a n -> p (a n)") for part in range(2)]
                pool.tensor_scalar(w_raw[:, s, :], w_raw[:, s, :], W_SCALE, None, ALU.mult).then_inc(w_split, 1)
                pool.wait_ge(w_split, 3 * i + 1)
                pool.tensor_copy(hi, w_raw[:, s, :]).then_inc(w_split, 1)
                pool.wait_ge(w_split, 3 * i + 2)
                pool.tensor_tensor(lo, w_raw[:, s, :], hi, ALU.subtract).then_inc(w_split, 1)

            def step(i, s):
                if live(i - 2):
                    y_rstd(i - 2, s)
                if live(i + 2):
                    layernorm(i + 2, s)
                if live(i - 2):
                    y_low(i - 2, s)
                if live(i + 2):
                    z_low(i + 2, s)
                if live(i - 6):
                    scatter(i - 6, s)
                if live(i - 1):
                    split_w(i - 1, 1 - s)

            pool.wait_ge(const_ready, 1)
            pool.wait_ge(affine_in, 32)
            for i in range(2):
                layernorm(i, i)
                z_low(i, i)
            for k in range(TOP_K):
                pool.iota(iota_e[:, k], pattern=[[1, EXPERTS]], base=0, channel_multiplier=0,
                          allow_small_or_imprecise_dtypes=True)
                last = pool.iota(region[:, k], pattern=[[REGION_ROWS, EXPERTS]], base=k * REGIONS * REGION_ROWS,
                                 channel_multiplier=0, allow_small_or_imprecise_dtypes=True)
            last.then_inc(iota_ready, 1)
            pool.iota(iota_t[:], pattern=[[P, TILES]], base=0, channel_multiplier=1,
                      allow_small_or_imprecise_dtypes=True).then_inc(iota_ready, 1)
            pool.memset(below[:], 1.0).then_inc(iota_ready, 1)
            pool.wait_ge(iota_ready, 3)
            pool.affine_select(out=below[:], in_=below[:], compare_op=ALU.is_gt, fill=0.0, base=0,
                               pattern=[[1, P]], channel_multiplier=-1).then_inc(iota_ready, 1)
            run(pool, step)
            for s in range(2):
                pool.wait_ge(scattered[s], 16 * TOP_K * TILES // 2)


def list_tiles(nc, ones16, placed, table, expert_b, expert_bias, tile_expert, inner_passes, slots, got_rings):
    with ExitStack() as stack:
        def sb(name, shape, dt=F32):
            return stack.enter_context(nc.sbuf_tensor(name, shape, dt))

        def sem(name):
            return stack.enter_context(nc.semaphore(name))

        table_sb = sb("table_sb", [P, TABLE_TILES, 4])
        tokens = sb("tokens", [P, TOP_K, EXPERTS], I32)
        tiles_i = sb("tiles_i", [P, TOP_K, EXPERTS], I32)
        tiles_f = sb("tiles_f", [P, TOP_K, EXPERTS])
        ends = [sb(f"ends{n}", [P, TOP_K, EXPERTS]) for n in range(3)]
        starts = sb("starts", [P, TOP_K, EXPERTS + 4], I32)
        iota_j = sb("iota_j", [P, PASSES, LISTED, EXPERTS])
        iota_r = sb("iota_r", [P, TOP_K, PASSES])
        past = sb("past", [P, TOP_K, PASSES * LISTED, EXPERTS])
        owner = sb("owner", [P, TOP_K, PASSES * LISTED])
        begun = sb("begun", [P, TOP_K, PASSES])
        passes = sb("passes", [P, TOP_K])
        sums = stack.enter_context(nc.psum_tensor("sums", [P, TOP_K * EXPERTS], F32))
        bias_in = sem("bias_in")
        table_in = sem("table_in")
        summed = sem("summed")
        iotas = sem("iotas")
        done = sem("done")
        block = stack.enter_context(nc.Block())

        @block.sync
        def _(sp):
            sp.dma_start(table_sb[:], table.rearrange("(p t) w -> p t w", p=P)).then_inc(table_in, 16)
            sp.dma_start(expert_bias[:], expert_b.rearrange("(a e) d -> a e d", a=1).broadcast_to(
                [P, EXPERTS, D])).then_inc(bias_in, 16)
            sp.wait_ge(bias_in, 16)

        @block.tensor
        def _(pe):
            pe.matmul(sums[:], ones16[:], placed[:, (TILES - 1) % 2], start=True, stop=True).then_inc(summed, 1)

        @block.gpsimd
        def _(pool):
            pool.iota(iota_j[:], pattern=[[RING, PASSES], [1, LISTED], [0, EXPERTS]], base=0, channel_multiplier=0,
                      allow_small_or_imprecise_dtypes=True).then_inc(iotas, 1)
            pool.iota(iota_r[:], pattern=[[0, TOP_K], [RING, PASSES]], base=0, channel_multiplier=0,
                      allow_small_or_imprecise_dtypes=True).then_inc(iotas, 1)
            for ring in got_rings:
                pool.memset(ring[:], 0.0)

        @block.vector
        def _(dve):
            count = [0]

            def after(instruction):
                instruction.then_inc(done, 1)
                count[0] += 1
                dve.wait_ge(done, count[0])

            dve.wait_ge(summed, 1)
            after(dve.tensor_scalar(tokens[:].rearrange("p k e -> p (k e)"), sums[:], float(P - 1), None, ALU.add))
            after(dve.tensor_scalar(tiles_i[:], tokens[:], 7, None, ALU.arith_shift_right))
            after(dve.tensor_copy(tiles_f[:], tiles_i[:]))
            last, n = tiles_f, 1
            for to in ends:
                after(dve.tensor_copy(to[:, :, 0:n], last[:, :, 0:n]))
                after(dve.tensor_tensor(to[:, :, n:], last[:, :, n:], last[:, :, 0:EXPERTS - n], ALU.add))
                last, n = to, 2 * n
            after(dve.tensor_tensor(starts[:, :, 0:EXPERTS], last[:], tiles_f[:], ALU.subtract))
            after(dve.tensor_copy(starts[:, :, EXPERTS:REGIONS], last[:, :, EXPERTS - 1:EXPERTS]))
            dve.wait_ge(iotas, 2)
            for k in range(TOP_K):
                end = last[:, k].unsqueeze(1).broadcast_to([P, PASSES * LISTED, EXPERTS])
                after(dve.tensor_tensor(past[:, k], iota_j[:].rearrange("p r s e -> p (r s) e"), end, ALU.is_ge))
            after(dve.tensor_reduce(owner[:], past[:], AX_X, ALU.add))
            after(dve.tensor_scalar(tile_expert[:].rearrange("p k r s -> p k (r s)"), owner[:], float(EXPERTS - 1), None,
                                    ALU.min))
            total = last[:, :, EXPERTS - 1:EXPERTS].broadcast_to([P, TOP_K, PASSES])
            after(dve.tensor_tensor(begun[:], iota_r[:], total, ALU.is_lt))
            after(dve.tensor_reduce(passes[:], begun[:], AX_X, ALU.add))
            after(dve.tensor_scalar(inner_passes[:], passes[:], 2.0, -2.0, ALU.max, ALU.add))
            dve.wait_ge(table_in, 16)
            for k in range(TOP_K):
                first = nc.values_load_multi_w_load_instructions(
                    starts[0:1, k, 0:REGIONS], (dve.engine,), min_val=0, max_val=SLOT_TILES,
                    skip_runtime_bounds_check_because="a choice's tiles are no more than SLOT_TILES")[1]
                for e in range(REGIONS):
                    t0 = (k * REGIONS + e) * SLOT_TILES
                    after(dve.tensor_copy(slots[:, k, bass.ds(first[e], SLOT_TILES), :], table_sb[:, t0:t0 + SLOT_TILES, :]))


class Choice:

    def __init__(self, stack, nc, k, x_ring, sum_ring):
        def sem(name):
            return stack.enter_context(nc.semaphore(f"{name}_{k}"))

        def sb(name, shape, dt):
            return stack.enter_context(nc.sbuf_tensor(f"{name}_{k}", shape, dt))

        def psum(name, shape, dt):
            return stack.enter_context(nc.psum_tensor(f"{name}_{k}", shape, dt))

        self.k = k
        self.x_got, self.sum_got = x_ring, sum_ring
        self.gathers = 16 if sum_ring is x_ring else 32
        self.token = sb("token", [P, RING, 1], I32)
        self.token_out = sb("token_out", [P, RING, 1], I32)
        self.yT_bank = [psum(f"yT_bank{s}", [P, 2, DT, P], F16) for s in range(2)]
        self.out_bank = [psum(f"out_bank{s}", [P, D], F32) for s in range(2)]
        self.token_ready = sem("token_ready")
        self.got = [sem(f"got{s}") for s in range(RING)]
        self.y_ready = sem("y_ready")
        self.y_hi_ready = sem("y_hi_ready")
        self.y_lo_ready = sem("y_lo_ready")
        self.yT_summed = sem("yT_summed")
        self.yT_ready = sem("yT_ready")
        self.expert_summed = sem("expert_summed")
        self.biased_ready = sem("biased_ready")
        self.token_out_ready = sem("token_out_ready")
        self.result_ready = sem("result_ready")
        self.put = [sem(f"put{s}") for s in range(RING)]


def run_experts(nc, ident16, w_parts, tile_expert, inner_passes, slots, expert_bias, got_rings, x_mid, x_final):
    R = RING
    EARLY = 4
    with ExitStack() as stack:
        def sb(name, shape, dt=F32):
            return stack.enter_context(nc.sbuf_tensor(name, shape, dt))

        y = sb("y_rows", [P, 2, D])
        y_parts = sb("y_rows_parts", [P, 2, 2, D], F16)
        yT = sb("y_columns", [P, 2, 2, DT, P], F16)
        biased = sb("biased", [P, 2, D])
        result = sb("result", [P, R, D])
        choices = [Choice(stack, nc, 0, got_rings[0], got_rings[0]), Choice(stack, nc, 1, got_rings[1], got_rings[0])]

        def at(r, s, n):
            q, place = divmod(s + n, R)
            return r + q, place, R * r + s + n

        def later(j, n):
            return not isinstance(j, int) or j >= n

        def experts(engine, c, r):
            row = tile_expert[0:1, c.k, bass.ds(r, 1), 0:R].rearrange("p a s -> p (a s)")
            return nc.values_load_multi_w_load_instructions(row, (engine.engine,), min_val=0, max_val=EXPERTS - 1,
                                                            skip_runtime_bounds_check_because="list_tiles clamps it")[1]

        def run(engine, c, step, lead, uses_experts=False):
            last = engine.value_load(inner_passes[0:1, c.k:c.k + 1], min_val=0, max_val=PASSES - 2) + 1
            pass_experts = experts(engine, c, 0) if uses_experts else None
            for s in range(-lead, R):
                step(0, s, lambda n: s + n >= 0, pass_experts)
            with engine.Fori(1, PASSES - 1) as r:
                with engine.If(r < last):
                    pass_experts = experts(engine, c, r) if uses_experts else None
                    for s in range(R):
                        step(r, s, lambda n: True, pass_experts)
            pass_experts = experts(engine, c, last) if uses_experts else None
            for s in range(R + 1):
                step(last, s, lambda n: s + n < R, pass_experts)
            return R * last + R

        block = stack.enter_context(nc.Block())

        @block.gpsimd
        def _(pool):
            def gather(c, s, source, ring):
                rows = bass.IndirectOffsetOnAxis(ap=c.token[:, s, :], axis=0)
                pool.indirect_dma_start(ring[:, s, :], None, source, rows, bounds_check=TOKENS - 1,
                                        oob_is_err=False).then_inc(c.got[s], 16)

            def gathers(c, s, j):
                early = c.k == 1 and isinstance(j, int) and j < EARLY
                pool.wait_ge(c.token_ready, j + 1)
                if later(j, R):
                    pool.wait_ge(c.result_ready, j - R + 1)
                pool.nop(nofuse=True)
                if not early:
                    gather(c, s, x_mid, c.x_got)
                if c.k == 1:
                    gather(c, s, x_final, c.sum_got)

            def scatter(c, s, j):
                pool.wait_ge(c.token_out_ready, j + 1)
                pool.wait_ge(c.result_ready, j + 1)
                pool.nop(nofuse=True)
                pool.indirect_dma_start(x_final, bass.IndirectOffsetOnAxis(ap=c.token_out[:, s, :], axis=0),
                                        result[:, s, :], None, bounds_check=TOKENS - 1,
                                        oob_is_err=False).then_inc(c.put[s], 16)

            for j in range(EARLY):
                pool.wait_ge(choices[1].token_ready, j + 1)
                gather(choices[1], j, x_mid, choices[1].x_got)
            for c in choices:
                def step(r, s, live, _):
                    if live(4):
                        _, place, j = at(r, s, 4)
                        gathers(c, place, j)
                    if live(-1):
                        _, place, j = at(r, s, -1)
                        scatter(c, place, j)

                tiles = run(pool, c, step, 4)
                for s in range(R):
                    pool.wait_ge(c.put[s], 16 * (tiles // R))
                pool.nop(nofuse=True)

        @block.tensor
        def _(pe):
            def transpose_y(c, j, s):
                pe.wait_ge(c.y_hi_ready, j + 1)
                pe.wait_ge(c.y_lo_ready, j + 1)
                if later(j, 2):
                    pe.wait_ge(c.yT_ready, j - 1)
                for part in range(2):
                    for t in range(DT):
                        last = pe.transpose(c.yT_bank[s][:, part, t, :], y_parts[:, s, part, t * P:(t + 1) * P],
                                            ident16[:])
                last.then_inc(c.yT_summed, 1)

            def multiply(c, j, s, e):
                pe.wait_ge(c.yT_ready, j + 1)
                if later(j, 2):
                    pe.wait_ge(c.biased_ready, j - 1)
                for t in range(DT):
                    for yp, wp in PRODUCTS:
                        last = pe.matmul(c.out_bank[s][:], yT[:, s, yp, t, :],
                                         w_parts[:, bass.ds(e, 1), t, wp, :].rearrange("p a n -> p (a n)"),
                                         start=(t == 0 and (yp, wp) == PRODUCTS[0]),
                                         stop=(t == DT - 1 and (yp, wp) == PRODUCTS[-1]))
                last.then_inc(c.expert_summed, 1)

            for c in choices:
                def step(r, s, live, pass_experts):
                    if live(1):
                        transpose_y(c, R * r + s + 1, (s + 1) % 2)
                    if live(0):
                        multiply(c, R * r + s, s % 2, pass_experts[s])

                run(pe, c, step, 1, uses_experts=True)

        @block.scalar
        def _(act):
            def copy_yT(c, j, s):
                act.wait_ge(c.yT_summed, j + 1)
                if later(j, 2):
                    act.wait_ge(c.expert_summed, j - 1)
                act.copy(yT[:, s], c.yT_bank[s][:]).then_inc(c.yT_ready, 1)

            def high_y(c, j, s):
                act.wait_ge(c.y_ready, j + 1)
                if later(j, 2):
                    act.wait_ge(c.yT_summed, j - 1)
                act.copy(y_parts[:, s, 0, :], y[:, s, :]).then_inc(c.y_hi_ready, 1)

            for c in choices:
                def step(r, s, live, _):
                    if live(1):
                        copy_yT(c, R * r + s + 1, (s + 1) % 2)
                    if live(2):
                        high_y(c, R * r + s + 2, s % 2)

                if c.k == 1:
                    act.wait_ge(choices[0].yT_summed, tiles)
                    act.wait_ge(choices[0].expert_summed, tiles)
                    act.nop(nofuse=True)
                tiles = run(act, c, step, 2)

        @block.vector
        def _(dve):
            def name_token(c, r, s, j):
                if later(j, R):
                    dve.wait_ge(c.got[s], c.gathers * r)
                    dve.nop(nofuse=True)
                dve.tensor_copy(c.token[:, s, :], slots[:, c.k, bass.ds(j, 1), 0:1].rearrange("p a b -> p (a b)")).then_inc(
                    c.token_ready, 1)

            def normalize(c, r, s, j):
                dve.wait_ge(c.got[s], c.gathers * r + c.gathers)
                if later(j, 2):
                    dve.wait_ge(c.y_lo_ready, j - 1)
                own = slots[:, c.k, bass.ds(j, 1), 2:4].rearrange("p a b -> p (a b)")
                dve.tensor_scalar(y[:, s % 2, :], c.x_got[:, s, :], own[:, 0:1], own[:, 1:2], ALU.subtract,
                                  ALU.mult).then_inc(c.y_ready, 1)

            def low_y(c, r, s, j):
                dve.wait_ge(c.y_hi_ready, j + 1)
                dve.tensor_tensor(y_parts[:, s % 2, 1, :], y[:, s % 2, :], y_parts[:, s % 2, 0, :],
                                  ALU.subtract).then_inc(c.y_lo_ready, 1)

            def finish(c, r, s, j, e):
                dve.wait_ge(c.expert_summed, j + 1)
                dve.scalar_tensor_tensor(biased[:, s % 2, :], c.out_bank[s % 2][:], 1.0 / W_SCALE,
                                         expert_bias[:, bass.ds(e, 1), :].rearrange("p a n -> p (a n)"), ALU.mult,
                                         ALU.add).then_inc(c.biased_ready, 1)
                if later(j, R):
                    dve.wait_ge(c.put[s], 16 * r)
                    dve.nop(nofuse=True)
                own = slots[:, c.k, bass.ds(j, 1), 0:2].rearrange("p a b -> p (a b)")
                dve.tensor_copy(c.token_out[:, s, :], own[:, 0:1]).then_inc(c.token_out_ready, 1)
                dve.wait_ge(c.biased_ready, j + 1)
                dve.scalar_tensor_tensor(result[:, s, :], biased[:, s % 2, :], own[:, 1:2], c.sum_got[:, s, :], ALU.mult,
                                         ALU.add).then_inc(c.result_ready, 1)

            for j in range(EARLY):
                name_token(choices[1], 0, j, j)
            for c in choices:
                def step(r, s, live, pass_experts):
                    if live(3):
                        normalize(c, *at(r, s, 3))
                    if live(0):
                        finish(c, r, s, R * r + s, pass_experts[s])
                    if live(5) and not (c.k == 1 and isinstance(r, int) and s + 5 < EARLY):
                        name_token(c, *at(r, s, 5))
                    if live(3):
                        low_y(c, *at(r, s, 3))

                if c.k == 1:
                    dve.wait_ge(choices[0].y_lo_ready, tiles)
                    dve.wait_ge(choices[0].yT_summed, tiles)
                    dve.wait_ge(choices[0].result_ready, tiles)
                    for s in range(R):
                        dve.wait_ge(choices[0].put[s], 16 * (tiles // R))
                    dve.nop(nofuse=True)
                tiles = run(dve, c, step, 5, uses_experts=True)



def flamingo_block(nc, x, ctx_1024, g_xattn, g_ffn, L0_xattn_ln_gamma, L0_xattn_ln_beta, L0_xattn_w_q,
                   L0_xattn_w_kv, L0_xattn_w_out, L0_xattn_b_out, L0_xattn_gate, L0_ffn_gate_w, L0_ffn_gate_b,
                   L0_ffn_expert_w, L0_ffn_expert_b, identity, out):
    x_in = x.rearrange("b s d -> (b s) d")
    x_final = out.rearrange("b s d -> (b s) d")
    m_dram = nc.dram_tensor("m_dram", [BATCH, P, DT, 2, COLS], F16, kind="Internal").ap()
    u_dram = nc.dram_tensor("u_dram", [BATCH, COLS, 2, D], F16, kind="Internal").ap()
    x_mid = nc.dram_tensor("x_mid", [TOKENS, D], F32, kind="Internal").ap()
    table = nc.dram_tensor("table", [TABLE_ROWS, 4], F32, kind="Internal").ap()
    with ExitStack() as stack:
        ident = stack.enter_context(nc.sbuf_tensor("ident", [P, P], F32))
        ident16 = stack.enter_context(nc.sbuf_tensor("ident16", [P, P], F16))
        ones16 = stack.enter_context(nc.sbuf_tensor("ones16", [P, P], F16))
        placed = stack.enter_context(nc.sbuf_tensor("placed", [P, 2, TOP_K * EXPERTS], F16))
        ident_in = stack.enter_context(nc.semaphore("ident_in"))
        ident16_ready = stack.enter_context(nc.semaphore("ident16_ready"))
        with nc.Block() as block:
            @block.sync
            def _(sp):
                sp.dma_start(ident[:], identity).then_inc(ident_in, 16)

            @block.vector
            def _(dve):
                dve.wait_ge(ident_in, 16)
                dve.tensor_copy(ident16[:], ident[:]).then_inc(ident16_ready, 1)
                dve.memset(ones16[:], 1.0).then_inc(ident16_ready, 1)
                dve.wait_ge(ident16_ready, 2)

        m_sb = stack.enter_context(nc.sbuf_tensor("m_sb", [P, 2, DT, 2, COLS], F16))
        u_sb = stack.enter_context(nc.sbuf_tensor("u_sb", [P, KT, 2, D], F16))
        fold_context(nc, ident, L0_xattn_w_q, L0_xattn_w_kv, L0_xattn_w_out, L0_xattn_b_out, L0_xattn_gate,
                     g_xattn, ctx_1024, m_dram, u_dram, m_sb, u_sb, table)
        w_parts = stack.enter_context(nc.sbuf_tensor("w_parts", [P, EXPERTS, DT, 2, D], F16))
        attend(nc, ident16, x_in, L0_xattn_ln_gamma, L0_xattn_ln_beta, m_dram, u_dram, m_sb, u_sb, x_mid, x_final,
               L0_ffn_gate_w, L0_ffn_gate_b, g_ffn, table, placed, ones16, L0_ffn_expert_w, w_parts)
        tile_expert = stack.enter_context(nc.sbuf_tensor("tile_expert", [P, TOP_K, PASSES, LISTED], I32))
        inner_passes = stack.enter_context(nc.sbuf_tensor("inner_passes", [P, TOP_K], I32))
        slots = stack.enter_context(nc.sbuf_tensor("slots", [P, TOP_K, 2 * SLOT_TILES, 4], F32))
        expert_bias = stack.enter_context(nc.sbuf_tensor("expert_bias", [P, EXPERTS, D], F32))
        got_rings = [stack.enter_context(nc.sbuf_tensor(f"got_ring{n}", [P, RING, D], F32)) for n in range(2)]
        list_tiles(nc, ones16, placed, table, L0_ffn_expert_b, expert_bias, tile_expert, inner_passes, slots, got_rings)
        run_experts(nc, ident16, w_parts, tile_expert, inner_passes, slots, expert_bias, got_rings, x_mid, x_final)


_INS = ['x', 'ctx_1024', 'g_xattn', 'g_ffn', 'L0_xattn_ln_gamma', 'L0_xattn_ln_beta', 'L0_xattn_w_q',
        'L0_xattn_w_kv', 'L0_xattn_w_out', 'L0_xattn_b_out', 'L0_xattn_gate', 'L0_ffn_gate_w', 'L0_ffn_gate_b',
        'L0_ffn_expert_w', 'L0_ffn_expert_b']


def kernel(**inputs):
    import numpy as _np
    import concourse.bacc as _bacc
    from concourse import mybir as _mybir
    from concourse.bass_utils import run_bass_kernel_spmd as _run

    nc = _bacc.Bacc("TRN2", target_bir_lowering=False, num_devices=1)
    arrays, args = {}, []
    given = [(name, _np.ascontiguousarray(inputs[name])) for name in _INS]
    given.append(("identity", _np.eye(128, dtype=_np.float32)))
    for name, a in given:
        arrays[f"in_{name}_dram"] = a
        args.append(nc.dram_tensor(f"in_{name}_dram", a.shape, _mybir.dt.from_np(a.dtype), kind="ExternalInput").ap())
    args.append(nc.dram_tensor("out_0_dram", (4, 2048, 512), _mybir.dt.float32, kind="ExternalOutput").ap())
    flamingo_block(nc, *args)
    r = _run(nc, [arrays], core_ids=[0])
    return r.results[0]["out_0_dram"]
```
